# Optimizing a Trainium2 kernel written in Bass

```python
import numpy as np
import jax
import jax.numpy as jnp

def _softmax(x, axis=-1):
    return jax.nn.softmax(x, axis=axis)

def _gelu(x):
    return jax.nn.gelu(x, approximate=True)

def _silu(x):
    return jax.nn.silu(x)

def _sigmoid(x):
    return jax.nn.sigmoid(x)

def _layernorm(x, axis=-1, eps=1e-05):
    m = jnp.mean(x, axis=axis, keepdims=True)
    v = jnp.var(x, axis=axis, keepdims=True)
    return (x - m) / jnp.sqrt(v + eps)

def _scatter_add(tgt, idx, src, axis=0):
    return tgt.at[idx].add(src)

def _segment_sum(src, seg, n):
    return jax.ops.segment_sum(src, seg, n)
kernel_name = 'mk_flamingo_gated_d2_seqx_r8_3cb2fe'

def setup_inputs(seed: int=0):
    np.random.seed(seed)
    _w = jnp.asarray

    def _rec_inputs():
        import jax
        import jax.numpy as jnp
        _rk = jax.random.key(seed)
        x = 7.22e-05 + 1 * jax.random.normal(jax.random.fold_in(_rk, 1), (4, 256, 256), jnp.float32)
        _lenS = 256 - jax.random.randint(jax.random.fold_in(_rk, 7), (4,), 0, max(1, 256 // 4) + 1, jnp.int32)
        _lenS2 = 256 - jax.random.randint(jax.random.fold_in(_rk, 8), (4,), 0, max(1, 256 // 4) + 1, jnp.int32)
        _ctx_2048P = jax.random.normal(jax.random.fold_in(_rk, 11), (4, 16, 256), jnp.float32)
        _ctx_2048c = jax.random.dirichlet(jax.random.fold_in(_rk, 511), 0.3 * jnp.ones((16,), jnp.float32), (4, 256))
        _ctx_2048t = jnp.einsum('bsk,bkd->bsd', _ctx_2048c, _ctx_2048P)
        _ctx_2048t = _ctx_2048t * jax.lax.rsqrt(jnp.mean(jnp.square(_ctx_2048t)) + 1e-12) * 0.953939
        ctx_2048 = 4.13588e-05 + 0.999923 * (_ctx_2048t + 0.3 * jax.random.normal(jax.random.fold_in(_rk, 611), (4, 256, 256), jnp.float32))
        _validS = jnp.arange(256)[None, :] < _lenS[:, None]
        _validS2 = jnp.arange(256)[None, :] < _lenS2[:, None]
        _causal = jnp.tril(jnp.ones((256, 256), dtype=bool))
        mask_BxS2_if1 = jnp.where(jnp.ones((4, 256), dtype=bool), 1, 0).astype(jnp.int32)
        _g = jax.random.normal(jax.random.fold_in(_rk, 9001), (2, 2), jnp.float32)
        _g = jnp.sign(_g) * jnp.maximum(jnp.abs(_g), 1.0) + (_g == 0) * 1.0
        g_xattn = _g[0]
        g_ffn = _g[1]
        return (x, ctx_2048, mask_BxS2_if1, g_xattn, g_ffn)
    x, ctx_2048, mask_BxS2_if1, g_xattn, g_ffn = _rec_inputs()

    def _L0_xattn_setup():
        import jax, jax.numpy as jnp
        import numpy as np
        B, S, DIM, HD = (4, 128, 256, 128)
        H = DIM // HD
        GN_EPS = 0.001

        def _decay_masks(n_heads, seq_len):
            gam = 1.0 - 2.0 ** (-5.0 - jnp.arange(n_heads, dtype=jnp.float32))
            idx = jnp.arange(seq_len, dtype=jnp.float32)
            expo = idx[None, :] - idx[:, None]
            D = jnp.where(expo[None, :, :] <= 0, gam[:, None, None] ** expo[None, :, :], 0.0)
            return D / jnp.sqrt(D.sum(axis=-1))[:, None, :]
        key = jax.random.key(seed)
        ks = jax.random.split(key, 8)
        x = jax.random.normal(ks[0], (B, S, DIM), dtype=jnp.float32)
        k = jax.random.normal(ks[1], (B, S, DIM), dtype=jnp.float32)
        v = jax.random.normal(ks[2], (B, S, DIM), dtype=jnp.float32)
        Wh = jax.random.normal(ks[3], (H, HD, HD), dtype=jnp.float32) / np.sqrt(HD)
        wg_w = jax.random.normal(ks[4], (DIM, DIM), dtype=jnp.float32) / np.sqrt(DIM)
        wo_w = jax.random.normal(ks[5], (DIM, DIM), dtype=jnp.float32) / np.sqrt(DIM)
        gn_gamma = jnp.ones((DIM,), dtype=jnp.float32)
        gn_beta = jnp.zeros((DIM,), dtype=jnp.float32)
        return {'x': x, 'k': k, 'v': v, 'Wh': Wh, 'wg_w': wg_w, 'wo_w': wo_w, 'gn_gamma': gn_gamma, 'gn_beta': gn_beta}
    _L0_xattn_all = _L0_xattn_setup()
    _L0_xattn_in = {k: v for k, v in _L0_xattn_all.items() if k in ('Wh', 'wg_w', 'wo_w', 'gn_gamma', 'gn_beta')}
    del _L0_xattn_all

    def _L0_ffn_setup():
        import jax, jax.numpy as jnp
        import numpy as np
        B, S, H, I, E = (2, 256, 256, 176, 8)
        TOP_K = 2
        key = jax.random.key(seed)
        k0, k1, k2, k3, k4 = jax.random.split(key, 5)
        scale = float(np.sqrt(2.0 / (H + I)))
        return {'hidden_states': jax.random.normal(k0, (B, S, H), dtype=jnp.float32), 'router_w': jax.random.normal(k1, (E, H), dtype=jnp.float32) * H ** (-0.5), 'gate_w': jax.random.normal(k2, (E, I, H), dtype=jnp.float32) * scale, 'up_w': jax.random.normal(k3, (E, I, H), dtype=jnp.float32) * scale, 'down_w': jax.random.normal(k4, (E, H, I), dtype=jnp.float32) * scale}
    _L0_ffn_all = _L0_ffn_setup()
    _L0_ffn_in = {k: v for k, v in _L0_ffn_all.items() if k in ('router_w', 'gate_w', 'up_w', 'down_w')}
    del _L0_ffn_all

    def _L1_xattn_setup():
        import jax, jax.numpy as jnp
        import numpy as np
        D_MODEL = 256
        N_HEADS = 32
        N_GROUPS = 8
        HEAD_DIM = D_MODEL // N_HEADS
        BATCH, SEQ = (2, 128)
        NEG_INF = float('-inf')
        key = jax.random.key(seed)
        ks = jax.random.split(key, 9)
        s = 0.02
        return {'Q': jax.random.normal(ks[0], (BATCH, SEQ, D_MODEL), jnp.float32), 'K': jax.random.normal(ks[1], (BATCH, SEQ, D_MODEL), jnp.float32), 'V': jax.random.normal(ks[2], (BATCH, SEQ, D_MODEL), jnp.float32), 'attention_mask': jnp.ones((BATCH, SEQ), jnp.int32), 'w_q': jax.random.normal(ks[3], (D_MODEL, D_MODEL), jnp.float32) * s, 'w_k': jax.random.normal(ks[4], (HEAD_DIM * N_GROUPS, D_MODEL), jnp.float32) * s, 'w_v': jax.random.normal(ks[5], (HEAD_DIM * N_GROUPS, D_MODEL), jnp.float32) * s, 'w_o': jax.random.normal(ks[6], (D_MODEL, D_MODEL), jnp.float32) * s, 'b_o': jnp.zeros((D_MODEL,), jnp.float32)}
    _L1_xattn_all = _L1_xattn_setup()
    _L1_xattn_in = {k: v for k, v in _L1_xattn_all.items() if k in ('w_q', 'w_k', 'w_v', 'w_o', 'b_o')}
    del _L1_xattn_all

    def _L1_ffn_setup():
        import jax, jax.numpy as jnp
        import numpy as np

        def _sparsify_2to4(h):
            B, S, I = h.shape
            g = h.reshape(B, S, I // 4, 4)
            a = jnp.abs(g)
            _, idx = jax.lax.top_k(a, 2)
            pos = jnp.arange(4)
            mask = (pos == idx[..., 0:1]) | (pos == idx[..., 1:2])
            return (g * mask.astype(g.dtype)).reshape(B, S, I)
        key = jax.random.key(seed)
        k1, k2, k3, k4 = jax.random.split(key, 4)
        B, S, H, I = (4, 256, 256, 1024)
        x = jax.random.normal(k1, (B, S, H), dtype=jnp.float32)
        w_gate = jax.random.normal(k2, (H, I), dtype=jnp.float32) / np.sqrt(H)
        w_up = jax.random.normal(k3, (H, I), dtype=jnp.float32) / np.sqrt(H)
        w_down = jax.random.normal(k4, (I, H), dtype=jnp.float32) / np.sqrt(I)
        return {'x': x, 'w_gate': w_gate, 'w_up': w_up, 'w_down': w_down}
    _L1_ffn_all = _L1_ffn_setup()
    _L1_ffn_in = {k: v for k, v in _L1_ffn_all.items() if k in ('w_gate', 'w_up', 'w_down')}
    del _L1_ffn_all
    return {'x': x, 'ctx_2048': ctx_2048, 'mask_BxS2_if1': mask_BxS2_if1, 'g_xattn': g_xattn, 'g_ffn': g_ffn, 'L0_xattn_Wh': _L0_xattn_in['Wh'], 'L0_xattn_wg_w': _L0_xattn_in['wg_w'], 'L0_xattn_wo_w': _L0_xattn_in['wo_w'], 'L0_xattn_gn_gamma': _L0_xattn_in['gn_gamma'], 'L0_xattn_gn_beta': _L0_xattn_in['gn_beta'], 'L0_ffn_router_w': _L0_ffn_in['router_w'], 'L0_ffn_gate_w': _L0_ffn_in['gate_w'], 'L0_ffn_up_w': _L0_ffn_in['up_w'], 'L0_ffn_down_w': _L0_ffn_in['down_w'], 'L1_xattn_w_q': _L1_xattn_in['w_q'], 'L1_xattn_w_k': _L1_xattn_in['w_k'], 'L1_xattn_w_v': _L1_xattn_in['w_v'], 'L1_xattn_w_o': _L1_xattn_in['w_o'], 'L1_xattn_b_o': _L1_xattn_in['b_o'], 'L1_ffn_w_gate': _L1_ffn_in['w_gate'], 'L1_ffn_w_up': _L1_ffn_in['w_up'], 'L1_ffn_w_down': _L1_ffn_in['w_down']}

def reference(x, ctx_2048, mask_BxS2_if1, g_xattn, g_ffn, L0_xattn_Wh, L0_xattn_wg_w, L0_xattn_wo_w, L0_xattn_gn_gamma, L0_xattn_gn_beta, L0_ffn_router_w, L0_ffn_gate_w, L0_ffn_up_w, L0_ffn_down_w, L1_xattn_w_q, L1_xattn_w_k, L1_xattn_w_v, L1_xattn_w_o, L1_xattn_b_o, L1_ffn_w_gate, L1_ffn_w_up, L1_ffn_w_down):
    import jax
    import jax.numpy as jnp

    def _L0_xattn_ref(x, k, v, Wh, wg_w, wo_w, gn_gamma, gn_beta):
        import jax, jax.numpy as jnp
        import numpy as np
        B, S, DIM, HD = (4, 128, 256, 128)
        H = DIM // HD
        GN_EPS = 0.001

        def _decay_masks(n_heads, seq_len):
            gam = 1.0 - 2.0 ** (-5.0 - jnp.arange(n_heads, dtype=jnp.float32))
            idx = jnp.arange(seq_len, dtype=jnp.float32)
            expo = idx[None, :] - idx[:, None]
            D = jnp.where(expo[None, :, :] <= 0, gam[:, None, None] ** expo[None, :, :], 0.0)
            return D / jnp.sqrt(D.sum(axis=-1))[:, None, :]
        b, s, dim = x.shape
        h, hd, _ = Wh.shape
        xh = x.reshape(b, s, h, hd)
        kh = k.reshape(b, s, h, hd)
        vh = v.reshape(b, s, h, hd)
        Q = jnp.einsum('bshd,hde->bshe', xh, Wh)
        K = jnp.einsum('bshd,hde->bshe', kh, Wh)
        V = jnp.einsum('bshd,hde->bshe', vh, Wh)
        scores = jnp.einsum('bshe,bthe->bhst', Q, K) / jnp.sqrt(jnp.float32(hd))
        Dn = _decay_masks(h, s)
        masked = scores * Dn[None, :, :, :]
        A = jnp.maximum(jnp.abs(masked.sum(axis=0)), 1.0)
        O = jnp.einsum('hst,bthe->bshe', A, V).reshape(b, s, dim)
        mu = O.mean(axis=-1, keepdims=True)
        var = O.var(axis=-1, keepdims=True)
        Y = (O - mu) / jnp.sqrt(var + GN_EPS) * gn_gamma + gn_beta
        W = jax.nn.relu(x @ wg_w)
        return W * Y @ wo_w

    def _L0_ffn_ref(hidden_states, router_w, gate_w, up_w, down_w):
        import jax, jax.numpy as jnp
        import numpy as np
        B, S, H, I, E = (2, 256, 256, 176, 8)
        TOP_K = 2
        b, s, h = hidden_states.shape
        e = router_w.shape[0]
        x = hidden_states.reshape(-1, h)
        logits = jnp.einsum('th,eh->te', x, router_w)
        top_vals, top_idx = jax.lax.top_k(logits, TOP_K)
        top_w = jax.nn.softmax(top_vals, axis=-1)
        expert = top_idx[:, 0]
        weight = top_w[:, 0]
        gate = jnp.einsum('th,eih->eti', x, gate_w)
        up = jnp.einsum('th,eih->eti', x, up_w)
        act = jax.nn.silu(gate) * up
        out_e = jnp.einsum('eti,ehi->eth', act, down_w)
        combine = jax.nn.one_hot(expert, e, dtype=x.dtype) * weight[:, None]
        out = jnp.einsum('eth,te->th', out_e, combine)
        return out.reshape(b, s, h)

    def _L1_xattn_ref(Q, K, V, attention_mask, w_q, w_k, w_v, w_o, b_o):
        import jax, jax.numpy as jnp
        import numpy as np
        D_MODEL = 256
        N_HEADS = 32
        N_GROUPS = 8
        HEAD_DIM = D_MODEL // N_HEADS
        BATCH, SEQ = (2, 128)
        NEG_INF = float('-inf')
        B, S, D = Q.shape
        G, HG, HD = (N_GROUPS, N_HEADS // N_GROUPS, HEAD_DIM)
        q = (Q @ w_q.T).reshape(B, S, G, HG, HD)
        k = (K @ w_k.T).reshape(B, S, G, HD)
        v = (V @ w_v.T).reshape(B, S, G, HD)
        scale = jnp.sqrt(jnp.float32(HD))
        scores = jnp.einsum('bnghd,bmgd->bnghm', q, k) / scale
        pad = (attention_mask == 0)[:, None, None, None, :]
        scores = jnp.where(pad, NEG_INF, scores)
        causal = jnp.tril(jnp.ones((S, S), bool))[None, :, None, None, :]
        scores = jnp.where(causal, scores, NEG_INF)
        attn = jax.nn.softmax(scores, axis=-1)
        out = jnp.einsum('bnghm,bmgd->bnghd', attn, v).reshape(B, S, D)
        return out @ w_o.T + b_o

    def _L1_ffn_ref(x, w_gate, w_up, w_down):
        import jax, jax.numpy as jnp
        import numpy as np

        def _sparsify_2to4(h):
            B, S, I = h.shape
            g = h.reshape(B, S, I // 4, 4)
            a = jnp.abs(g)
            _, idx = jax.lax.top_k(a, 2)
            pos = jnp.arange(4)
            mask = (pos == idx[..., 0:1]) | (pos == idx[..., 1:2])
            return (g * mask.astype(g.dtype)).reshape(B, S, I)
        h = jax.nn.silu(jnp.einsum('bsh,hi->bsi', x, w_gate)) * jnp.einsum('bsh,hi->bsi', x, w_up)
        h_sparse = _sparsify_2to4(h)
        return jnp.einsum('bsi,ih->bsh', h_sparse, w_down)
    x = x + jnp.tanh(g_xattn[0]) * _L0_xattn_ref(_layernorm(x, axis=-1), ctx_2048, ctx_2048, L0_xattn_Wh, L0_xattn_wg_w, L0_xattn_wo_w, L0_xattn_gn_gamma, L0_xattn_gn_beta)
    x = x + jnp.tanh(g_ffn[0]) * _L0_ffn_ref(_layernorm(x, axis=-1), L0_ffn_router_w, L0_ffn_gate_w, L0_ffn_up_w, L0_ffn_down_w)
    x = x + jnp.tanh(g_xattn[1]) * _L1_xattn_ref(_layernorm(x, axis=-1), ctx_2048, ctx_2048, mask_BxS2_if1, L1_xattn_w_q, L1_xattn_w_k, L1_xattn_w_v, L1_xattn_w_o, L1_xattn_b_o)
    x = x + jnp.tanh(g_ffn[1]) * _L1_ffn_ref(_layernorm(x, axis=-1), L1_ffn_w_gate, L1_ffn_w_up, L1_ffn_w_down)
    return x

_drawn_inputs = setup_inputs


def setup_inputs(seed=0):
    import zlib

    import numpy as np

    out = dict(_drawn_inputs(seed))
    spreads = {'g_ffn': (-1.0, 0.538),
     'L0_xattn_gn_gamma': (1.0, 0.2),
     'L0_xattn_gn_beta': (0.0, 0.1),
     'L1_xattn_b_o': (0.0, 0.1)}
    factors = {'L1_xattn_w_q': 8.0, 'L1_xattn_w_k': 8.0}
    for name, (base, spread) in spreads.items():
        noise = np.random.default_rng([zlib.crc32(name.encode()), seed]).standard_normal(out[name].shape)
        drawn = base * np.exp(spread * noise) if base else spread * noise
        out[name] = jnp.asarray(drawn.astype(out[name].dtype))
    for name, factor in factors.items():
        out[name] = (out[name] * factor).astype(out[name].dtype)
    return out
```

```python
import numpy as np
import concourse.bass as bass
from concourse import mybir
from contextlib import ExitStack


P = 128
BATCH, SEQ, DIM = 4, 256, 256
TOKENS = BATCH * SEQ
TILES = TOKENS // P
KT = DIM // P
UNIT = 512
UNITS = TOKENS // UNIT
UNIT_TILES = UNIT // P
RET_HEADS, RET_HD = 2, 128
EXPERTS, EXPERT_I = 8, 176
MOE_MT = EXPERTS * EXPERT_I // P
HEADS, GROUPS, HD = 32, 8, 8
PER_GROUP = HEADS // GROUPS
QUADS = 4
HALVES = GROUPS // QUADS
FFN_I = 1024
FFN_MT = FFN_I // P
FFN_BLOCKS = FFN_I // 4 // P
LN_EPS, GN_EPS = 1e-5, 1e-3
MASKED = -float(2.0 ** 100)
DEAD = -3.0e38


def build_program(nc, a, out):
    F32, F32R, BF16, I32 = mybir.dt.float32, mybir.dt.float32r, mybir.dt.bfloat16, mybir.dt.int32
    ALU = mybir.AluOpType
    ACT = mybir.ActivationFunctionType
    AX = mybir.AxisListType.X

    ctx = ExitStack()
    with ctx:
        def sb(name, shape, dt=F32):
            return ctx.enter_context(nc.sbuf_tensor(name, shape, dt))

        sems = {}

        def sem(name):
            if name not in sems:
                sems[name] = ctx.enter_context(nc.semaphore(name))
            return sems[name]

        x_sb = sb("x_sb", [P, TILES, DIM])
        ctxT = sb("ctxT", [P, KT, TOKENS])
        wh = sb("wh", [P, RET_HEADS, RET_HD])
        wg = sb("wg", [P, KT, DIM])
        wo0 = sb("wo0", [P, KT, DIM])
        gamma = sb("gamma", [P, DIM])
        beta = sb("beta", [P, DIM])
        decay = sb("decay", [P, RET_HEADS, 3 * P])
        router = sb("router", [P, KT, EXPERTS])
        e_gate = sb("e_gate", [P, KT, MOE_MT * P])
        e_up = sb("e_up", [P, KT, MOE_MT * P])
        e_down = sb("e_down", [P, MOE_MT, DIM])
        wq = sb("wq", [P, KT, DIM])
        wk = sb("wk", [P, KT, P])
        wv = sb("wv", [P, KT, GROUPS * HD])
        wo1 = sb("wo1", [P, KT, DIM])
        bo = sb("bo", [P, DIM])
        f_gate = e_gate[:, :, 0:FFN_I]
        f_up = e_up[:, :, 0:FFN_I]
        f_down = e_down[:, 0:FFN_MT, :]
        gates = sb("gates", [P, 4])
        mask_col = sb("mask_col", [P, TILES], I32)
        ident = sb("ident", [P, P])
        small_c = sb("small_c", [P, 16])

        tg = sb("tg", [P, 4])
        bo_t = sb("bo_t", [P, DIM])
        selr = sb("selr", [P, 10 * P], F32R)
        identb = sb("identb", [P, P], BF16)
        causb = sb("causb", [P, 2, 4, P], BF16)
        padselr = sb("padselr", [1, P], F32R)
        padrow = sb("padrow", [1, TOKENS], F32R)
        padcol = sb("padcol", [P, TILES])
        eselr = sb("eselr", [2 * EXPERTS, MOE_MT * P], F32R)
        power = sb("power", [P, 1])
        stats = sb("stats", [P, 5, TILES, 6])
        mv = sb("mv", [P, 5, TILES, 2])
        veps = sb("veps", [P, 5, TILES])
        rstd = sb("rstd", [P, 5, TILES])
        xn = sb("xn", [P, 2, DIM])
        xT = sb("xT", [P, KT, TOKENS])
        logit = sb("logit", [P, TILES, EXPERTS])
        r_a = sb("r_a", [P, TILES, EXPERTS])
        r_b = sb("r_b", [P, TILES, EXPERTS])
        onehot = sb("onehot", [P, TILES, EXPERTS])
        r_s = sb("r_s", [P, 6, TILES])
        comb = sb("comb", [P, TILES, EXPERTS])
        combs = sb("combs", [P, TILES, 2 * EXPERTS], F32R)
        combT = sb("combT", [2 * EXPERTS, TOKENS], F32R)
        silu = sb("silu", [P, 2, UNIT])
        prod = sb("prod", [P, 2, UNIT])
        vaug = sb("vaug", [P, TILES, GROUPS, 32])
        mx = sb("mx", [P, 2, 2, QUADS, HALVES, PER_GROUP])
        nmx = sb("nmx", [P, 2, 2, 2 * HEADS], F32R)
        nmT = sb("nmT", [2 * HEADS, 2, SEQ], F32R)
        avT = prod
        rden = sb("rden", [P, 2, HALVES, QUADS])
        att = sb("att", [P, 2, DIM])
        actT = sb("actT", [P, 2, KT, P])
        region = sb("region", [P, 2, 6144])
        act_e = [region[:, u, 0:MOE_MT * UNIT].rearrange("p (m n) -> p m n", m=MOE_MT) for u in range(2)]
        pt0 = [region[:, u, 0:4096].rearrange("p (j h n) -> p j h n", j=QUADS, h=PER_GROUP) for u in range(2)]
        pt1 = [region[:, u, 4096:6144].rearrange("p (j h n) -> p j h n", j=QUADS, h=PER_GROUP) for u in range(2)]
        hs = [region[:, u, 0:4096].rearrange("p (m n) -> p m n", m=FFN_MT) for u in range(2)]
        absh = region[:, 0, 4096:6144].rearrange("p (j n) -> p j n", j=4)
        hbuf = region[:, 1, 4096:6144].rearrange("p (j n) -> p j n", j=4)
        ret = region[:, 0, :]
        kT0 = ret[:, 0:2048].rearrange("p (h n) -> p h n", h=2)
        qT0 = ret[:, 2048:4096].rearrange("p (h n) -> p h n", h=2)
        v0 = ret[:, 4096:6144].rearrange("p (t h n) -> p t h n", t=2, h=2)
        o_sb = region[:, 1, 0:2048].rearrange("p (k n) -> p k n", k=TILES)
        sel_in = region[:, 1, 2048:2048 + 11 * P]
        esel_in = region[0:2 * EXPERTS, 1, 3456:3456 + MOE_MT * P]
        mask_row = region[0:1, 1, 4864:4864 + TOKENS].bitcast(I32)
        amat = sb("amat", [P, RET_HEADS, 4 * P])
        aneg = silu[:, :, 0:3 * P]
        qhi = sb("qhi", [P, 2, HALVES, SEQ], F32R)
        qlo = sb("qlo", [P, 2, HALVES, SEQ], F32R)
        khl = sb("khl", [P, 2, SEQ], F32R)
        qst = sb("qst", [P, 2, HALVES, PER_GROUP, SEQ], F32R)
        kst = sb("kst", [P, 2, HALVES, SEQ], F32R)
        cmps = ctxT[:, :, :].rearrange("p t n -> p (t n)").bitcast(BF16).rearrange("p (c n) -> p c n", n=UNIT)
        cmp1, cmp2, cmp3 = cmps[:, 0:3, :], cmps[:, 3:5, :], cmps[:, 5, :]
        wins = amat[:, :, :].rearrange("p h n -> p (h n)").bitcast(BF16).rearrange("p (c n) -> p c n", n=UNIT)

        wide = [ctx.enter_context(nc.psum_tensor(f"wide{i}", [P, 2 * UNIT], F32)) for i in range(2)]
        turn = [ctx.enter_context(nc.psum_tensor(f"turn{i}", [P, UNIT], F32)) for i in range(2)]
        tokp = [ctx.enter_context(nc.psum_tensor(f"tokp{i}", [P, UNIT], F32)) for i in range(2)]

        fills, occupant, ring = {}, {}, {"one": 0, "two": 0, "turn": 0, "tok": 0}

        def plan(stage, i, kind):
            n = ring[kind]
            ring[kind] += 1
            if kind == "one":
                cells, ap = [("w", n % 4)], wide[n % 4 // 2][:, n % 2 * UNIT:n % 2 * UNIT + UNIT]
            elif kind == "two":
                cells, ap = [("w", n % 2 * 2), ("w", n % 2 * 2 + 1)], wide[n % 2][:, :]
            elif kind == "turn":
                cells, ap = [("t", n % 2)], turn[n % 2][:, 0:256]
            else:
                cells, ap = [("o", n % 2)], tokp[n % 2][:, :]
            before = {}
            for c in cells:
                if c in occupant:
                    s, m = occupant[c]
                    before[s] = max(before.get(s, 0), m + 1)
                occupant[c] = (stage, i)
            fills[stage, i] = (ap, before)

        for k in range(TILES):
            plan("ln0", k, "turn")
        for i in range(4):
            plan("rk", i, "one")
        for k in range(TILES):
            plan("rv", k, "one")
        for i in range(4):
            plan("rq", i, "one")
        for h in range(2):
            plan("rs", h, "one")
        for i in range(4):
            plan("ro", i, "one")
        for k in range(2):
            plan("rg", k, "one")
        for k in range(TILES):
            if k + 2 < TILES:
                plan("rg", k + 2, "one")
            plan("wyT", k, "turn")
            plan("res0", k, "tok")
        for u in range(UNITS):
            for k in range(UNIT_TILES * u, UNIT_TILES * (u + 1)):
                plan("ln1", k, "turn")
            plan("log", u, "one")
            for m in range(MOE_MT):
                plan("eg", u * MOE_MT + m, "one")
                plan("eu", u * MOE_MT + m, "one")
                if m == 0:
                    for k in range(UNIT_TILES * u, UNIT_TILES * (u + 1)):
                        plan("cT", k, "turn")
                plan("ec", u * MOE_MT + m, "tok")
            for k in range(UNIT_TILES * u, UNIT_TILES * (u + 1)):
                plan("res1", k, "tok")

        def plan_prep(b):
            for k in (2 * b, 2 * b + 1):
                plan("ln2", k, "turn")
            plan("kp", b, "one")
            plan("qp", b, "one")
            plan("vp", b, "one")
            for q in range(HALVES):
                plan("ks", 2 * b + q, "one")
                for h in range(2):
                    plan("qs", 4 * b + 2 * q + h, "one")
            for n in range(12):
                plan("sa", 12 * b + n, "two")

        def plan_attend(b):
            for n in range(12):
                plan("sb", 12 * b + n, "two")
            for n in range(4):
                plan("av", 4 * b + n, "one")
            for nt in range(2):
                for n in range(4):
                    plan("avT", 8 * b + 4 * nt + n, "turn")
                plan("atT", 2 * b + nt, "turn")
                plan("res2", 2 * b + nt, "tok")

        plan_prep(0)
        for nt in range(2):
            plan("nmT", nt, "turn")
        for b in range(BATCH):
            if b + 1 < BATCH:
                plan_prep(b + 1)
            plan_attend(b)
            if b + 1 < BATCH:
                for nt in range(2):
                    plan("nmT", 2 * b + 2 + nt, "turn")
        for u in range(UNITS):
            for k in range(UNIT_TILES * u, UNIT_TILES * (u + 1)):
                plan("ln3", k, "turn")
            for n in range(FFN_MT):
                plan("fg", u * FFN_MT + n, "one")
                plan("fu", u * FFN_MT + n, "one")
            for k in range(UNIT_TILES * u, UNIT_TILES * (u + 1)):
                plan("res3", k, "tok")

        def acquire(pe, stage, i):
            ap, before = fills[stage, i]
            for s, n in before.items():
                pe.wait_ge(sem(s + "_taken"), n)
            return ap

        def filled(eng, stage, i):
            eng.wait_ge(sem(stage + "_ready"), i + 1)
            return fills[stage, i][0]

        def ready(ins, stage):
            ins.then_inc(sem(stage + "_ready"), 1)

        def taken(ins, stage):
            ins.then_inc(sem(stage + "_taken"), 1)

        def has_taken(eng, stage, i):
            eng.wait_ge(sem(stage + "_taken"), i + 1)

        def made(eng, name, n):
            eng.wait_ge(sem(name), n)

        def tile_cols(k):
            return slice(k * P, (k + 1) * P)

        loads = {}

        def load(eng, name, dst, src):
            loads[name] = loads.get(name, 0)
            eng.dma_start(dst, src).then_inc(sem("in_" + name), 16)

        def loaded(eng, name, n=1):
            eng.wait_ge(sem("in_" + name), 16 * n)

        block = ctx.enter_context(nc.Block())

        @block.sync
        def _(sp):
            for k in range(TILES):
                load(sp, f"x{k}", x_sb[:, k, :], a["x"][k])
                if k == 0:
                    load(sp, "ident", ident[:, :], a["ident"])
                if k == 1:
                    load(sp, "gates", gates[:, 0:2], a["g_x"])
                    load(sp, "gates", gates[:, 2:4], a["g_f"])
                    load(sp, "wh", wh[:, :, :], a["wh"])
                    load(sp, "ctx", ctxT[:, :, :], a["ctxT"])
            load(sp, "decay", decay[:, :, :], a["decay"])
            load(sp, "wg", wg[:, :, :], a["wg"])
            load(sp, "gamma", gamma[:, :], a["gamma"])
            load(sp, "gamma", beta[:, :], a["beta"])
            load(sp, "wo0", wo0[:, :, :], a["wo0"])
            load(sp, "router", router[:, :, :], a["router"])
            load(sp, "small", small_c[:, :], a["small"])
            load(sp, "sel", esel_in, a["esel"])
            load(sp, "sel", sel_in, a["sel"])
            load(sp, "caus", causb[:, :, :, :].rearrange("p w h n -> p w (h n)"), a["caus"])
            load(sp, "caus", identb[:, :], a["identb"])
            load(sp, "sel", mask_row, a["mask_row"])
            load(sp, "sel", mask_col[:, :], a["mask_col"])
            for t in range(KT):
                load(sp, "e_gate", e_gate[:, t, :], a["e_gate"][:, t, :])
                load(sp, "e_up", e_up[:, t, :], a["e_up"][:, t, :])
            load(sp, "e_down", e_down[:, :, :], a["e_down"])
            load(sp, "w1", wq[:, :, :], a["wq"])
            load(sp, "w1", wk[:, :, :], a["wk"])
            load(sp, "w1", wv[:, :, :], a["wv"])
            load(sp, "w1", wo1[:, :, :], a["wo1"])
            load(sp, "w1", bo[:, :], a["bo"])
            sp.wait_ge(sem("res1_ready"), TILES)
            load(sp, "f", f_gate, a["f_gate"])
            load(sp, "f", f_up, a["f_up"])
            load(sp, "f", f_down, a["f_down"])
            for b in range(BATCH):
                has_taken(sp, "nmT", 2 * b + 1)
                for piece in range(2):
                    for j in range(QUADS):
                        rows = slice(piece * HEADS + j * 8, piece * HEADS + j * 8 + 8)
                        dst = qst[32 * j + 24 + piece:32 * j + 25 + piece, b % 2, :, :, :]
                        sp.dma_start(dst.rearrange("p q h n -> p (q h) n").bitcast(F32), nmT[rows, b % 2, :].bitcast(F32))\
                          .then_inc(sem("max_rows"), 16)
            for k in range(TILES):
                has_taken(sp, "res3", k)
                sp.dma_start(out[k], x_sb[:, k, :]).then_inc(sem("stored"), 16)
            sp.wait_ge(sem("stored"), 16 * TILES)

        @block.gpsimd
        def _(pool):
            pool.memset(power[:, :], -0.5).then_inc(sem("power_set"), 1)
            pool.memset(vaug[:, :, :, :], 1.0).then_inc(sem("ones_set"), 1)
            pool.memset(amat[:, :, :], 1.0).then_inc(sem("a_set"), 1)
            made(pool, "power_set", 1)

            def inverse_std(layer, k, eps):
                made(pool, f"mv{layer}", k + 1)
                pool.tensor_scalar(veps[:, layer, k:k + 1], mv[:, layer, k, 1:2], eps, None, ALU.add)\
                    .then_inc(sem(f"veps{layer}"), 1)
                made(pool, f"veps{layer}", k + 1)
                pool.tensor_tensor(out=rstd[:, layer, k:k + 1], in0=veps[:, layer, k:k + 1],
                                   in1=power[:, :], op=ALU.pow).then_inc(sem(f"rstd{layer}"), 1)

            for k in range(TILES):
                inverse_std(0, k, LN_EPS)
            for k in range(TILES):
                inverse_std(4, k, GN_EPS)
                if k == 0:
                    loaded(pool, "gamma", 2)
                made(pool, "gn_z", k + 1)
                pool.tensor_tensor(out=o_sb[:, k, :], in0=o_sb[:, k, :], in1=gamma[:, :], op=ALU.mult)\
                    .then_inc(sem("gn_scaled"), 1)
                made(pool, "gn_scaled", k + 1)
                pool.tensor_tensor(out=o_sb[:, k, :], in0=o_sb[:, k, :], in1=beta[:, :], op=ALU.add)\
                    .then_inc(sem("gn_y"), 1)
            for layer in (1, 2, 3):
                for k in range(TILES):
                    inverse_std(layer, k, LN_EPS)

        @block.scalar
        def _(act):
            loaded(act, "gates", 2)
            act.activation(tg[:, :], gates[:, :], ACT.Tanh).then_inc(sem("tanh"), 1)

            def ln_turn(layer, k):
                src = filled(act, f"ln{layer}", k)
                taken(act.activation(xT[:, :, tile_cols(k)], src.rearrange("p (t n) -> p t n", t=KT), ACT.Copy),
                      f"ln{layer}")

            for i in range(4):
                h, u = divmod(i, UNITS)
                taken(act.activation(kT0[:, h, u * UNIT:(u + 1) * UNIT], filled(act, "rk", i), ACT.Copy), "rk")
            for k in range(TILES):
                b, t = divmod(k, 2)
                src = filled(act, "rv", k)[:, 0:256].rearrange("p (h n) -> p h n", h=2)
                taken(act.activation(v0[:, t, :, b * P:(b + 1) * P], src, ACT.Copy), "rv")
            for k in range(TILES):
                ln_turn(0, k)
            for i in range(4):
                h, u = divmod(i, UNITS)
                taken(act.activation(qT0[:, h, u * UNIT:(u + 1) * UNIT], filled(act, "rq", i), ACT.Copy), "rq")
            for i in range(4):
                st, h = divmod(i, 2)
                dst = o_sb[:, st:TILES:2, h * P:(h + 1) * P]
                taken(act.activation(dst, filled(act, "ro", i).rearrange("p (b e) -> p b e", b=BATCH), ACT.Copy), "ro")
            for k in range(TILES):
                src = filled(act, "wyT", k)
                if k >= 2:
                    act.wait_ge(sem("res0_ready"), k - 1)
                taken(act.activation(actT[:, k % 2, :, :], src.rearrange("p (t n) -> p t n", t=KT), ACT.Copy), "wyT")

            loaded(act, "sel", 4)
            act.activation(eselr[:, :], esel_in, ACT.Copy).then_inc(sem("esel_made"), 1)
            act.activation(selr[:, :], sel_in[:, 0:10 * P], ACT.Copy).then_inc(sem("sel_made"), 1)
            act.activation(padselr[:, :], sel_in[0:1, 10 * P:11 * P], ACT.Copy).then_inc(sem("sel_made"), 1)
            for u in range(UNITS):
                for k in range(UNIT_TILES * u, UNIT_TILES * (u + 1)):
                    ln_turn(1, k)
                made(act, "vdiff", u + 1)
                act.activation(r_s[:, 3, UNIT_TILES * u:UNIT_TILES * (u + 1)],
                               r_s[:, 2, UNIT_TILES * u:UNIT_TILES * (u + 1)], ACT.Exp).then_inc(sem("vexp"), 1)
                for m in range(MOE_MT):
                    i = u * MOE_MT + m
                    src = filled(act, "eg", i)
                    if i >= 2:
                        has_taken(act, "eu", i - 2)
                    taken(act.activation(silu[:, i % 2, :], src, ACT.Silu), "eg")
                    if m == 0:
                        for k in range(UNIT_TILES * u, UNIT_TILES * (u + 1)):
                            src = filled(act, "cT", k)[0:2 * EXPERTS, 0:P]
                            taken(act.activation(combT[:, tile_cols(k)], src, ACT.Copy), "cT")

            def prep(b):
                for k in (2 * b, 2 * b + 1):
                    ln_turn(2, k)
                s = b % 2
                src = filled(act, "kp", b)
                if b >= 2:
                    act.wait_ge(sem("ks_ready"), 2 * b - 2)
                act.activation(khl[:, s, :], src[:, 0:SEQ], ACT.Copy).then_inc(sem("k_high"), 1)
                src = filled(act, "qp", b).rearrange("p (q n) -> p q n", q=HALVES)
                if b >= 2:
                    act.wait_ge(sem("qs_ready"), 4 * b - 4)
                act.activation(qhi[:, s, :, :], src, ACT.Copy).then_inc(sem("q_high"), 1)
                src = filled(act, "vp", b)[:, 0:2 * GROUPS * HD].rearrange("p (k g d) -> p k g d", k=2, g=GROUPS)
                if b == 0:
                    made(act, "ones_set", 1)
                for t in range(2):
                    ins = act.activation(vaug[:, 2 * b + t, :, 0:HD], src[:, t, :, :], ACT.Copy)
                taken(ins, "vp")
                for q in range(HALVES):
                    src = filled(act, "ks", 2 * b + q)[:, 0:SEQ]
                    if b >= 2:
                        act.wait_ge(sem("sb_ready"), 12 * (b - 1))
                    taken(act.activation(kst[:, s, q, :], src, ACT.Identity, bias=small_c[:, 1:2]), "ks")
                    for h in range(2):
                        src = filled(act, "qs", 4 * b + 2 * q + h).rearrange("p (h n) -> p h n", h=2)
                        taken(act.activation(qst[:, s, q, 2 * h:2 * h + 2, :], src, ACT.Identity,
                                             bias=small_c[:, 0:1]), "qs")

            def neg_turn(b):
                if b >= 2:
                    act.wait_ge(sem("max_rows"), 16 * 8 * (b - 1))
                for nt in range(2):
                    src = filled(act, "nmT", 2 * b + nt)[0:2 * HEADS, 0:P]
                    taken(act.activation(nmT[:, b % 2, tile_cols(nt)], src, ACT.Copy), "nmT")

            def attend(b):
                made(act, "padcol_made", 1)
                for q in range(HALVES):
                    r = (2 * b + q) % 2
                    if b == 0:
                        act.wait_ge(sem("res1_ready"), TILES)
                    else:
                        act.wait_ge(sem("av_ready"), 2 * (2 * (b - 1) + q) + 2)
                    for n in range(6):
                        src = filled(act, "sb", 12 * b + 6 * q + n)
                        if n < 4:
                            dst, key = pt0[r][:, n, :, :], 2 * b
                            src = src.rearrange("p (h n) -> p h n", h=PER_GROUP)
                        else:
                            j = 2 * (n - 4)
                            dst, key = pt1[r][:, j:j + 2, :, :], 2 * b + 1
                            src = src.rearrange("p (j h n) -> p j h n", j=2, h=PER_GROUP)
                        taken(act.activation(dst, src, ACT.Exp, bias=padcol[:, key:key + 1],
                                             scale=float(HD) ** -0.5), "sb")
                for n in range(4):
                    nt = n // 2
                    src = filled(act, "av", 4 * b + n)
                    i = 4 * b + n
                    if i >= 2:
                        act.wait_ge(sem("avT_ready"), av_slot_free(i))
                    taken(act.activation(avT[:, n % 2, :], src, ACT.Copy), "av")
                    if n % 2 == 1:
                        at_turn(b, nt)

            def av_slot_free(i):
                return 4 * ((i - 2) // 2) + 4

            def at_turn(b, nt):
                i = 2 * b + nt
                src = filled(act, "atT", i)
                if i >= 2:
                    act.wait_ge(sem("res2_ready"), i - 1)
                taken(act.activation(actT[:, i % 2, :, :], src.rearrange("p (t n) -> p t n", t=KT), ACT.Copy), "atT")

            prep(0)
            neg_turn(0)
            for b in range(BATCH):
                if b + 1 < BATCH:
                    prep(b + 1)
                attend(b)
                if b + 1 < BATCH:
                    neg_turn(b + 1)

            for u in range(UNITS):
                for k in range(UNIT_TILES * u, UNIT_TILES * (u + 1)):
                    ln_turn(3, k)
                for n in range(FFN_MT):
                    i = u * FFN_MT + n
                    src = filled(act, "fg", i)
                    if i >= 2:
                        has_taken(act, "fu", i - 2)
                    taken(act.activation(silu[:, i % 2, :], src, ACT.Silu), "fg")
                    if n % 4 == 3:
                        blk = i // 4
                        for j in range(4):
                            has_taken(act, "fu", 4 * blk + j)
                            if blk >= 1 and j == 0:
                                act.wait_ge(sem("compared"), 3 * blk)
                            act.activation(absh[:, j, :], hbuf[:, j, :], ACT.Abs).then_inc(sem("abs_made"), 1)

        @block.vector
        def _(dve):
            def stat(layer, k, src):
                dve.bn_stats(stats[:, layer, k, :], src).then_inc(sem(f"stats{layer}"), 1)
                made(dve, f"stats{layer}", k + 1)
                dve.bn_aggr(mv[:, layer, k, :], stats[:, layer, k, :]).then_inc(sem(f"mv{layer}"), 1)

            def norm(layer, k):
                made(dve, f"rstd{layer}", k + 1)
                if k >= 2:
                    dve.wait_ge(sem(f"ln{layer}_ready"), k - 1)
                elif layer:
                    dve.wait_ge(sem(f"ln{layer - 1}_ready"), TILES - 1 + k)
                dve.tensor_scalar(xn[:, k % 2, :], x_sb[:, k, :], mv[:, layer, k, 0:1], rstd[:, layer, k:k + 1],
                                  ALU.subtract, ALU.mult).then_inc(sem(f"xn{layer}"), 1)

            loaded(dve, "x0")
            stat(0, 0, x_sb[:, 0, :])
            for k in range(TILES):
                if k + 1 < TILES:
                    loaded(dve, f"x{k + 1}")
                    stat(0, k + 1, x_sb[:, k + 1, :])
                norm(0, k)

            loaded(dve, "decay")
            made(dve, "a_set", 1)
            for h in range(RET_HEADS):
                src = filled(dve, "rs", h)[:, 0:3 * P]
                taken(dve.tensor_tensor(out=aneg[:, h, :], in0=src, in1=decay[:, h, :], op=ALU.mult), "rs")
                has_taken(dve, "rs", h)
                for n, (o, w, d) in enumerate(((0, 2 * P, 0), (2 * P, P, 3 * P))):
                    dve.scalar_tensor_tensor(out=amat[:, h, d:d + w], in0=aneg[:, h, o:o + w], scalar=-1.0,
                                             in1=aneg[:, h, o:o + w], op0=ALU.mult, op1=ALU.max)\
                       .then_inc(sem("a_abs"), 1)
                    made(dve, "a_abs", 2 * h + n + 1)
                    dve.tensor_scalar(amat[:, h, d:d + w], amat[:, h, d:d + w], 1.0, None, ALU.max)\
                       .then_inc(sem("a_made"), 1)

            def residual(stage, k, g):
                dve.scalar_tensor_tensor(out=x_sb[:, k, :], in0=filled(dve, stage, k)[:, 0:DIM], scalar=tg[:, g:g + 1],
                                         in1=x_sb[:, k, :], op0=ALU.mult, op1=ALU.add)\
                   .then_inc(sem(stage + "_taken"), 1)

            made(dve, "tanh", 1)
            dve.wait_ge(sem("ro_taken"), 4)
            stat(4, 0, o_sb[:, 0, :])
            for k in range(TILES):
                if k + 1 < TILES:
                    stat(4, k + 1, o_sb[:, k + 1, :])
                made(dve, "rstd4", k + 1)
                dve.tensor_scalar(o_sb[:, k, :], o_sb[:, k, :], mv[:, 4, k, 0:1], rstd[:, 4, k:k + 1],
                                  ALU.subtract, ALU.mult).then_inc(sem("gn_z"), 1)
                made(dve, "gn_y", k + 1)
                src = filled(dve, "rg", k)[:, 0:DIM]
                if k >= 2:
                    dve.wait_ge(sem("wyT_ready"), k - 1)
                taken(dve.scalar_tensor_tensor(out=att[:, k % 2, :], in0=src, scalar=0.0, in1=o_sb[:, k, :],
                                               op0=ALU.max, op1=ALU.mult), "rg")
                if k >= 1:
                    residual("res0", k - 1, 0)
                    has_taken(dve, "res0", k - 1)
                    stat(1, k - 1, x_sb[:, k - 1, :])
            residual("res0", TILES - 1, 0)
            has_taken(dve, "res0", TILES - 1)
            stat(1, TILES - 1, x_sb[:, TILES - 1, :])

            loaded(dve, "sel", 4)
            loaded(dve, "small")
            dve.tensor_scalar(padrow[:, :], mask_row, 0.0, MASKED, ALU.is_equal, ALU.mult)\
               .then_inc(sem("padrow_made"), 1)
            dve.tensor_scalar(padcol[:, :], mask_col[:, :], 0.0, DEAD, ALU.is_equal, ALU.mult)\
               .then_inc(sem("padcol_made"), 1)

            def route(u):
                ks = slice(UNIT_TILES * u, UNIT_TILES * (u + 1))
                wide8 = [P, UNIT_TILES, EXPERTS]
                n = [0]

                def step(ins):
                    n[0] += 1
                    ins.then_inc(sem(f"route{u}"), 1)
                    dve.wait_ge(sem(f"route{u}"), n[0])

                def each(v):
                    return v.unsqueeze(2).to_broadcast(wide8)

                src = filled(dve, "log", u)[:, 0:UNIT_TILES * EXPERTS].rearrange("p (k e) -> p k e", e=EXPERTS)
                taken(dve.tensor_copy(logit[:, ks, :], src), "log")
                has_taken(dve, "log", u)
                step(dve.reduce_max(r_s[:, 0, ks], logit[:, ks, :], AX))
                step(dve.tensor_tensor(out=r_a[:, ks, :], in0=logit[:, ks, :], in1=each(r_s[:, 0, ks]), op=ALU.is_equal))
                rev = small_c[:, 8:16].unsqueeze(1).to_broadcast(wide8)
                step(dve.tensor_tensor(out=r_b[:, ks, :], in0=r_a[:, ks, :], in1=rev, op=ALU.mult))
                step(dve.reduce_max(r_s[:, 1, ks], r_b[:, ks, :], AX))
                step(dve.tensor_tensor(out=onehot[:, ks, :], in0=r_b[:, ks, :], in1=each(r_s[:, 1, ks]), op=ALU.is_equal))
                step(dve.scalar_tensor_tensor(out=r_a[:, ks, :], in0=onehot[:, ks, :], scalar=DEAD,
                                              in1=logit[:, ks, :], op0=ALU.mult, op1=ALU.add))
                step(dve.reduce_max(r_s[:, 1, ks], r_a[:, ks, :], AX))
                dve.tensor_tensor(out=r_s[:, 2, ks], in0=r_s[:, 1, ks], in1=r_s[:, 0, ks], op=ALU.subtract)\
                   .then_inc(sem("vdiff"), 1)
                made(dve, "vexp", u + 1)
                step(dve.tensor_scalar(r_s[:, 4, ks], r_s[:, 3, ks], 1.0, None, ALU.add))
                step(dve.reciprocal(r_s[:, 5, ks], r_s[:, 4, ks]))
                step(dve.tensor_tensor(out=comb[:, ks, :], in0=onehot[:, ks, :], in1=each(r_s[:, 5, ks]), op=ALU.mult))
                step(dve.tensor_copy(combs[:, ks, 0:EXPERTS], comb[:, ks, :]))
                dve.tensor_tensor(out=combs[:, ks, EXPERTS:2 * EXPERTS], in0=comb[:, ks, :],
                                  in1=combs[:, ks, 0:EXPERTS].bitcast(F32), op=ALU.subtract).then_inc(sem("combs_made"), 1)

            for u in range(UNITS):
                for k in range(UNIT_TILES * u, UNIT_TILES * (u + 1)):
                    norm(1, k)
                if u == 1:
                    made(dve, "esel_made", 1)
                    made(dve, "sel_made", 2)
                route(u)
                for m in range(MOE_MT):
                    i = u * MOE_MT + m
                    src = filled(dve, "eu", i)
                    has_taken(dve, "eg", i)
                    if i >= 2:
                        has_taken(dve, "ec", i - 2)
                    taken(dve.tensor_tensor(out=prod[:, i % 2, :], in0=src, in1=silu[:, i % 2, :], op=ALU.mult), "eu")
                    src = filled(dve, "ec", i)
                    has_taken(dve, "eu", i)
                    taken(dve.tensor_tensor(out=act_e[u][:, m, :], in0=src, in1=prod[:, i % 2, :], op=ALU.mult), "ec")
                for k in range(UNIT_TILES * u, UNIT_TILES * (u + 1)):
                    residual("res1", k, 2)
                    has_taken(dve, "res1", k)
                    stat(2, k, x_sb[:, k, :])

            def low_parts(b):
                s = b % 2
                made(dve, "k_high", b + 1)
                src = filled(dve, "kp", b)[64:128, 0:SEQ]
                taken(dve.tensor_tensor(out=khl[64:128, s, :], in0=src, in1=khl[64:128, s, :].bitcast(F32),
                                        op=ALU.subtract), "kp")
                made(dve, "q_high", b + 1)
                src = filled(dve, "qp", b).rearrange("p (q n) -> p q n", q=HALVES)
                if b >= 2:
                    dve.wait_ge(sem("qs_ready"), 4 * b - 4)
                taken(dve.tensor_tensor(out=qlo[:, s, :, :], in0=src, in1=qhi[:, s, :, :].bitcast(F32),
                                        op=ALU.subtract), "qp")

            def maxima(b):
                s = b % 2
                for q in range(HALVES):
                    for n in range(6):
                        src = filled(dve, "sa", 12 * b + 6 * q + n)
                        if n < 2:
                            src = src.rearrange("p (j h m) -> p j h m", j=2, h=PER_GROUP)
                            dst = mx[:, s, 0, 2 * n:2 * n + 2, q, :]
                        else:
                            src = src.rearrange("p (h m) -> p h m", h=PER_GROUP)
                            dst = mx[:, s, 1, n - 2, q, :]
                        taken(dve.reduce_max(dst, src, AX), "sa")
                has_taken(dve, "sa", 12 * b + 11)
                if b >= 2:
                    dve.wait_ge(sem("nmT_ready"), 2 * (b - 1))
                for nt in range(2):
                    m = mx[:, s, nt, :, :, :].rearrange("p j q h -> p (j q h)")
                    dve.tensor_scalar(nmx[:, s, nt, 0:HEADS], m, -1.0, None, ALU.mult).then_inc(sem("nm_high"), 1)
                    made(dve, "nm_high", 2 * b + nt + 1)
                    dve.scalar_tensor_tensor(out=nmx[:, s, nt, HEADS:2 * HEADS], in0=m, scalar=-1.0,
                                             in1=nmx[:, s, nt, 0:HEADS].bitcast(F32), op0=ALU.mult,
                                             op1=ALU.subtract).then_inc(sem("nm_made"), 1)

            def finish(b):
                for nt in range(2):
                    i = 2 * b + nt
                    if i >= 2:
                        dve.wait_ge(sem("atT_ready"), i - 1)
                    o = att[:, i % 2, :].rearrange("p (q j h d) -> p h q j d", q=HALVES, j=QUADS, h=PER_GROUP)
                    for n in range(PER_GROUP):
                        f = 8 * b + 4 * nt + n
                        src = filled(dve, "avT", f).rearrange("p (q j r) -> p q j r", q=HALVES, j=QUADS)
                        dve.reciprocal(rden[:, f % 2, :, :], src[:, :, :, HD]).then_inc(sem("rden_made"), 1)
                        made(dve, "rden_made", f + 1)
                        taken(dve.tensor_tensor(out=o[:, n, :, :, :], in0=src[:, :, :, 0:HD],
                                                in1=rden[:, f % 2, :, :].unsqueeze(3).to_broadcast([P, HALVES, QUADS, HD]),
                                                op=ALU.mult), "avT")
                    residual("res2", i, 1)
                    has_taken(dve, "res2", i)
                    dve.tensor_tensor(out=x_sb[:, i, :], in0=x_sb[:, i, :], in1=bo_t[:, :], op=ALU.add)\
                       .then_inc(sem("x3"), 1)
                    made(dve, "x3", i + 1)
                    stat(3, i, x_sb[:, i, :])

            loaded(dve, "w1", 5)
            dve.tensor_scalar(bo_t[:, :], bo[:, :], tg[:, 1:2], None, ALU.mult).then_inc(sem("bo_made"), 1)
            made(dve, "bo_made", 1)

            def prep(b):
                for k in (2 * b, 2 * b + 1):
                    norm(2, k)
                low_parts(b)

            prep(0)
            maxima(0)
            for b in range(BATCH):
                if b + 1 < BATCH:
                    prep(b + 1)
                    maxima(b + 1)
                finish(b)

            for u in range(UNITS):
                for k in range(UNIT_TILES * u, UNIT_TILES * (u + 1)):
                    norm(3, k)
                for blk in range(FFN_BLOCKS):
                    g = u * FFN_BLOCKS + blk
                    for j in range(4):
                        i = 4 * g + j
                        src = filled(dve, "fu", i)
                        has_taken(dve, "fg", i)
                        taken(dve.tensor_tensor(out=hbuf[:, j, :], in0=src, in1=silu[:, i % 2, :], op=ALU.mult), "fu")
                    made(dve, "abs_made", 4 * g + 4)
                    dve.tensor_tensor(out=cmp1[:, :, :], in0=absh[:, 0:3, :], in1=absh[:, 1:4, :], op=ALU.is_ge)\
                       .then_inc(sem("compared"), 1)
                    dve.tensor_tensor(out=cmp2[:, :, :], in0=absh[:, 0:2, :], in1=absh[:, 2:4, :], op=ALU.is_ge)\
                       .then_inc(sem("compared"), 1)
                    dve.tensor_tensor(out=cmp3[:, :], in0=absh[:, 0, :], in1=absh[:, 3, :], op=ALU.is_ge)\
                       .then_inc(sem("compared"), 1)
                    made(dve, "compared", 3 * g + 3)
                    dve.tensor_tensor(out=wins[:, 0:2, :], in0=cmp1[:, 0:2, :], in1=cmp2[:, :, :], op=ALU.add)\
                       .then_inc(sem("wins_a"), 1)
                    dve.tensor_tensor(out=wins[:, 2, :], in0=cmp1[:, 2, :], in1=cmp2[:, 0, :], op=ALU.subtract)\
                       .then_inc(sem("wins_a"), 1)
                    dve.tensor_tensor(out=wins[:, 3, :], in0=cmp1[:, 2, :], in1=cmp2[:, 1, :], op=ALU.add)\
                       .then_inc(sem("wins_a"), 1)
                    made(dve, "wins_a", 3 * g + 3)
                    dve.tensor_tensor(out=wins[:, 0, :], in0=wins[:, 0, :], in1=cmp3[:, :], op=ALU.add)\
                       .then_inc(sem("wins_b"), 1)
                    dve.tensor_tensor(out=wins[:, 1, :], in0=wins[:, 1, :], in1=cmp1[:, 0, :], op=ALU.subtract)\
                       .then_inc(sem("wins_b"), 1)
                    dve.tensor_tensor(out=wins[:, 2, :], in0=wins[:, 2, :], in1=cmp1[:, 1, :], op=ALU.subtract)\
                       .then_inc(sem("wins_b"), 1)
                    dve.tensor_tensor(out=wins[:, 3, :], in0=wins[:, 3, :], in1=cmp3[:, :], op=ALU.add)\
                       .then_inc(sem("wins_b"), 1)
                    made(dve, "wins_b", 4 * g + 4)
                    for j, (op, least) in enumerate(((ALU.is_ge, 2.0), (ALU.is_ge, 1.0), (ALU.is_ge, 0.0), (ALU.is_le, 1.0))):
                        dve.scalar_tensor_tensor(out=hs[u][:, 4 * blk + j, :], in0=wins[:, j, :], scalar=least,
                                                 in1=hbuf[:, j, :], op0=op, op1=ALU.mult).then_inc(sem("hs_made"), 1)
                    made(dve, "hs_made", 4 * g + 4)
                for k in range(UNIT_TILES * u, UNIT_TILES * (u + 1)):
                    dve.scalar_tensor_tensor(out=x_sb[:, k, :], in0=filled(dve, "res3", k)[:, 0:DIM], scalar=tg[:, 3:4],
                                             in1=x_sb[:, k, :], op0=ALU.mult, op1=ALU.add)\
                       .then_inc(sem("res3_taken"), 1)

        @block.tensor
        def _(pe):
            def mm(dst, lhsT, rhs, first, last):
                return pe.matmul(dst, lhsT, rhs, start=first, stop=last)

            def ln_turn(layer, k):
                dst = acquire(pe, f"ln{layer}", k)
                made(pe, f"xn{layer}", k + 1)
                for t in range(KT):
                    ins = pe.transpose(dst[:, tile_cols(t)], xn[:, k % 2, tile_cols(t)], ident[:, :])
                ready(ins, f"ln{layer}")

            def turn_pair(stage, i, src):
                dst = acquire(pe, stage, i)
                for t in range(KT):
                    ins = pe.transpose(dst[:, tile_cols(t)], src[:, tile_cols(t)], ident[:, :])
                ready(ins, stage)

            loaded(pe, "wh")
            loaded(pe, "ctx")
            for i in range(4):
                h, u = divmod(i, UNITS)
                dst = acquire(pe, "rk", i)
                ready(mm(dst, wh[:, h, :], ctxT[:, h, u * UNIT:(u + 1) * UNIT], True, True), "rk")
            for k in range(TILES):
                dst = acquire(pe, "rv", k)
                for h in range(RET_HEADS):
                    ins = mm(dst[:, h * P:(h + 1) * P], ctxT[:, h, tile_cols(k)], wh[:, h, :], True, True)
                ready(ins, "rv")
            loaded(pe, "ident")
            for k in range(TILES):
                ln_turn(0, k)
            for i in range(4):
                h, u = divmod(i, UNITS)
                dst = acquire(pe, "rq", i)
                has_taken(pe, "ln0", UNIT_TILES * (u + 1) - 1)
                ready(mm(dst, wh[:, h, :], xT[:, h, u * UNIT:(u + 1) * UNIT], True, True), "rq")
            has_taken(pe, "rk", 3)
            for h in range(RET_HEADS):
                dst = acquire(pe, "rs", h)
                has_taken(pe, "rq", 2 * h + 1)
                for t in range(2):
                    for b in range(BATCH):
                        at = b * SEQ + t * P
                        ins = mm(dst[:, 2 * P * t:2 * P * t + SEQ - t * P], kT0[:, h, at:at + P],
                                 qT0[:, h, at:(b + 1) * SEQ], b == 0, b == BATCH - 1)
                ready(ins, "rs")
            loaded(pe, "wg")
            has_taken(pe, "rv", TILES - 1)
            for i in range(4):
                st, h = divmod(i, 2)
                dst = acquire(pe, "ro", i)
                made(pe, "a_made", 2 * h + 2)
                for t in range(2):
                    ins = mm(dst, amat[:, h, t * SEQ + st * P:t * SEQ + st * P + P], v0[:, t, h, :], t == 0, t == 1)
                ready(ins, "ro")

            def gate(k):
                dst = acquire(pe, "rg", k)
                for t in range(KT):
                    ins = mm(dst[:, 0:DIM], xT[:, t, tile_cols(k)], wg[:, t, :], t == 0, t == KT - 1)
                ready(ins, "rg")

            gate(0)
            gate(1)
            loaded(pe, "wo0")
            for k in range(TILES):
                if k + 2 < TILES:
                    gate(k + 2)
                has_taken(pe, "rg", k)
                turn_pair("wyT", k, att[:, k % 2, :])
                dst = acquire(pe, "res0", k)[:, 0:DIM]
                has_taken(pe, "wyT", k)
                for t in range(KT):
                    ins = mm(dst, actT[:, k % 2, t, :], wo0[:, t, :], t == 0, t == KT - 1)
                ready(ins, "res0")

            for u in range(UNITS):
                us = slice(u * UNIT, (u + 1) * UNIT)
                ks = range(UNIT_TILES * u, UNIT_TILES * (u + 1))
                for k in ks:
                    ln_turn(1, k)
                loaded(pe, "router")
                dst = acquire(pe, "log", u)
                for k in ks:
                    has_taken(pe, "ln1", k)
                    for t in range(KT):
                        c = (k % UNIT_TILES) * EXPERTS
                        ins = mm(dst[:, c:c + EXPERTS], xT[:, t, tile_cols(k)], router[:, t, :], t == 0, t == KT - 1)
                ready(ins, "log")
                for m in range(MOE_MT):
                    i = u * MOE_MT + m
                    for stage, w in (("eg", e_gate), ("eu", e_up)):
                        dst = acquire(pe, stage, i)
                        if i == 0:
                            loaded(pe, "e_gate" if stage == "eg" else "e_up", 2)
                        for t in range(KT):
                            ins = mm(dst, w[:, t, tile_cols(m)], xT[:, t, us], t == 0, t == KT - 1)
                        ready(ins, stage)
                    if m == 0:
                        made(pe, "combs_made", u + 1)
                        made(pe, "esel_made", 1)
                        for k in ks:
                            dst = acquire(pe, "cT", k)
                            ready(pe.transpose(dst[0:2 * EXPERTS, 0:P], combs[:, k, :].bitcast(F32), ident[:, :]), "cT")
                        has_taken(pe, "cT", ks[-1])
                    dst = acquire(pe, "ec", i)
                    ready(mm(dst, eselr[:, tile_cols(m)], combT[:, us], True, True), "ec")
                if u == 0:
                    loaded(pe, "e_down")
                has_taken(pe, "ec", (u + 1) * MOE_MT - 1)
                for k in ks:
                    dst = acquire(pe, "res1", k)[:, 0:DIM]
                    for m in range(MOE_MT):
                        c = (k % UNIT_TILES) * P
                        ins = mm(dst, act_e[u][:, m, c:c + P], e_down[:, m, :], m == 0, m == MOE_MT - 1)
                    ready(ins, "res1")

            def bias_mask(dst, which, heads, width, at, stop):
                view = dst.rearrange("p (h m) -> p h m", h=heads)[:, :, at:at + P]
                return pe.matmul(view, identb[:, :], causb[:, which, 0:heads, :], start=False, stop=stop,
                                 skip_group_check=True)

            def prep(b):
                s = b % 2
                seq = slice(b * SEQ, (b + 1) * SEQ)
                for k in (2 * b, 2 * b + 1):
                    ln_turn(2, k)
                dst = acquire(pe, "kp", b)
                if b == 0:
                    loaded(pe, "w1", 5)
                for t in range(KT):
                    ins = mm(dst[:, 0:SEQ], wk[:, t, :], ctxT[:, t, seq], t == 0, t == KT - 1)
                ready(ins, "kp")
                dst = acquire(pe, "qp", b)
                has_taken(pe, "ln2", 2 * b + 1)
                for q in range(HALVES):
                    for t in range(KT):
                        ins = mm(dst[:, q * SEQ:(q + 1) * SEQ], wq[:, t, tile_cols(q)], xT[:, t, seq], t == 0, t == KT - 1)
                ready(ins, "qp")
                dst = acquire(pe, "vp", b)
                for r in range(2):
                    for t in range(KT):
                        w = GROUPS * HD
                        ins = mm(dst[:, r * w:(r + 1) * w], ctxT[:, t, tile_cols(2 * b + r)], wv[:, t, :], t == 0, t == KT - 1)
                ready(ins, "vp")
                if b == 0:
                    made(pe, "sel_made", 2)
                    made(pe, "padrow_made", 1)
                has_taken(pe, "kp", b)
                has_taken(pe, "qp", b)
                for q in range(HALVES):
                    dst = acquire(pe, "ks", 2 * b + q)
                    mm(dst[:, 0:SEQ], selr[:, (8 + q) * P:(9 + q) * P], khl[:, s, :], True, False)
                    ready(mm(dst[:, 0:SEQ], padselr[:, :], padrow[:, seq], False, True), "ks")
                    for h in range(2):
                        dst = acquire(pe, "qs", 4 * b + 2 * q + h)
                        for e in range(2):
                            hg = 2 * h + e
                            mm(dst[:, e * SEQ:(e + 1) * SEQ], selr[:, hg * P:(hg + 1) * P], qhi[:, s, q, :], True, False)
                            ins = mm(dst[:, e * SEQ:(e + 1) * SEQ], selr[:, (4 + hg) * P:(5 + hg) * P], qlo[:, s, q, :], False, True)
                        ready(ins, "qs")
                if b == 0:
                    loaded(pe, "caus", 2)
                for q in range(HALVES):
                    has_taken(pe, "ks", 2 * b + q)
                    has_taken(pe, "qs", 4 * b + 2 * q + 1)
                    for n in range(6):
                        dst = acquire(pe, "sa", 12 * b + 6 * q + n)
                        for half in range(2):
                            bank = dst[:, half * UNIT:(half + 1) * UNIT]
                            if n < 2:
                                j, nt, heads, w = 2 * n + half, 0, range(4), P
                            else:
                                j, nt, heads, w = n - 2, 1, range(2 * half, 2 * half + 2), SEQ
                            rows = slice(32 * j, 32 * j + 32)
                            for c, hg in enumerate(heads):
                                pe.matmul(bank[:, c * w:(c + 1) * w], qst[rows, s, q, hg, tile_cols(nt)],
                                          kst[rows, s, q, 0:w], start=(c == 0), stop=False, skip_group_check=True)
                            ins = bias_mask(bank, 0, len(heads), w, nt * P, True)
                        ready(ins, "sa")

            def neg_turn(b):
                s = b % 2
                for nt in range(2):
                    dst = acquire(pe, "nmT", 2 * b + nt)
                    made(pe, "nm_made", 2 * b + nt + 1)
                    ready(pe.transpose(dst[0:2 * HEADS, 0:P], nmx[:, s, nt, :].bitcast(F32), ident[:, :]), "nmT")

            def attend(b):
                s = b % 2
                made(pe, "max_rows", 16 * 8 * (b + 1))
                for q in range(HALVES):
                    for n in range(6):
                        dst = acquire(pe, "sb", 12 * b + 6 * q + n)
                        for half in range(2):
                            bank = dst[:, half * UNIT:(half + 1) * UNIT]
                            if n < 4:
                                j, mt, heads = n, 0, slice(2 * half, 2 * half + 2)
                            else:
                                j, mt, heads = 2 * (n - 4) + half, 1, slice(0, 4)
                            rows = slice(32 * j, 32 * j + 32)
                            w = SEQ - mt * P
                            pe.matmul(bank, kst[rows, s, q, tile_cols(mt)], qst[rows, s, q, heads, mt * P:SEQ],
                                      start=True, stop=False, skip_group_check=True)
                            ins = bias_mask(bank, 1, UNIT // w, w, 0, True)
                        ready(ins, "sb")
                for nt in range(2):
                    for q in range(HALVES):
                        r = q
                        dst = acquire(pe, "av", 4 * b + 2 * nt + q)
                        has_taken(pe, "sb", 12 * b + 6 * q + 5)
                        has_taken(pe, "vp", b)
                        for mt in range(nt + 1):
                            for j in range(QUADS):
                                rhs = pt0[r][:, j, :, tile_cols(nt)] if mt == 0 else pt1[r][:, j, :, :]
                                ins = pe.matmul(dst[32 * j:32 * j + 32, :], vaug[:, 2 * b + mt, 4 * q + j, :], rhs,
                                                start=(mt == 0), stop=(mt == nt), skip_group_check=True)
                        ready(ins, "av")
                for nt in range(2):
                    i = 2 * b + nt
                    has_taken(pe, "av", 4 * b + 2 * nt + 1)
                    for hg in range(PER_GROUP):
                        dst = acquire(pe, "avT", 8 * b + 4 * nt + hg)
                        for q in range(HALVES):
                            ins = pe.transpose(dst[:, tile_cols(q)], avT[:, q, hg * P:(hg + 1) * P], ident[:, :])
                        ready(ins, "avT")
                    has_taken(pe, "avT", 8 * b + 4 * nt + 3)
                    turn_pair("atT", i, att[:, i % 2, :])
                    dst = acquire(pe, "res2", i)[:, 0:DIM]
                    has_taken(pe, "atT", i)
                    for t in range(KT):
                        ins = mm(dst, actT[:, i % 2, t, :], wo1[:, t, :], t == 0, t == KT - 1)
                    ready(ins, "res2")

            prep(0)
            neg_turn(0)
            for b in range(BATCH):
                if b + 1 < BATCH:
                    prep(b + 1)
                attend(b)
                if b + 1 < BATCH:
                    neg_turn(b + 1)

            loaded(pe, "f", 3)
            for u in range(UNITS):
                us = slice(u * UNIT, (u + 1) * UNIT)
                ks = range(UNIT_TILES * u, UNIT_TILES * (u + 1))
                for k in ks:
                    ln_turn(3, k)
                has_taken(pe, "ln3", ks[-1])
                for n in range(FFN_MT):
                    blk, j = divmod(n, 4)
                    c = j * 2 * P + blk * P
                    for stage, w in (("fg", f_gate), ("fu", f_up)):
                        dst = acquire(pe, stage, u * FFN_MT + n)
                        for t in range(KT):
                            ins = mm(dst, w[:, t, c:c + P], xT[:, t, us], t == 0, t == KT - 1)
                        ready(ins, stage)
                made(pe, "hs_made", (u + 1) * FFN_MT)
                for k in ks:
                    dst = acquire(pe, "res3", k)[:, 0:DIM]
                    for m in range(FFN_MT):
                        c = (k % UNIT_TILES) * P
                        ins = mm(dst, hs[u][:, m, c:c + P], f_down[:, m, :], m == 0, m == FFN_MT - 1)
                    ready(ins, "res3")


def shape_constants():
    f = np.float32
    gam = (f(1.0) - f(2.0) ** (f(-5.0) - np.arange(RET_HEADS, dtype=f))).astype(f)
    idx = np.arange(SEQ, dtype=f)
    expo = idx[None, :] - idx[:, None]
    low = expo <= 0
    D = np.where(low[None], gam[:, None, None] ** np.where(low, expo, 0)[None], 0).astype(f)
    Dn = D / np.sqrt(D.sum(axis=-1, dtype=f))[:, None, :] / np.sqrt(f(RET_HD))
    G = Dn.transpose(0, 2, 1)
    decay = np.concatenate([G[:, :P, :], G[:, P:, P:]], axis=2).transpose(1, 0, 2)
    sel = np.zeros((P, 11, P), f)
    for j in range(QUADS):
        for d in range(HD):
            for hg in range(PER_GROUP):
                row = j * 32 + hg * HD + d
                sel[row, hg, [32 * j + d, 32 * j + 8 + d]] = 1
                sel[row, 4 + hg, 32 * j + 16 + d] = 1
            for q in range(HALVES):
                row = (QUADS * q + j) * HD + d
                sel[row, 8 + q, [32 * j + d, 32 * j + 16 + d]] = 1
                sel[64 + row, 8 + q, 32 * j + 8 + d] = 1
        sel[0, 10, 32 * j + 26] = 1
    expert = np.arange(MOE_MT * P) // EXPERT_I
    esel = (expert[None, :] == (np.arange(2 * EXPERTS) % EXPERTS)[:, None]).astype(f)
    small = np.zeros((P, 16), f)
    small[26::32, 0] = 1
    small[24::32, 1] = 1
    small[25::32, 1] = 1
    small[:, 8:16] = np.arange(EXPERTS, 0, -1)
    n = np.arange(P)
    later = np.where(n[None, :] > n[:, None], f(MASKED), f(0))
    caus = np.stack([np.tile(later, (1, 4)), np.tile(later.T, (1, 4))], 1).astype(f)
    return {"decay": decay, "sel": sel.reshape(P, 11 * P), "esel": esel, "small": small,
            "ident": np.eye(P, dtype=f), "caus": caus,
            "identb": np.eye(P, dtype=f)}


def kernel(**inputs):
    import numpy as _np
    import concourse.bacc as _bacc
    from concourse import mybir as _mybir
    from concourse.bass_utils import run_bass_kernel_spmd as _run

    i = {k: _np.asarray(v) for k, v in inputs.items()}

    def by_rows(w):
        return w.reshape(w.shape[0] // P, P, w.shape[1]).transpose(1, 0, 2)

    def everywhere(v):
        return _np.broadcast_to(v[None, :], (P, v.shape[0]))

    wk = i["L1_xattn_w_k"].T
    ffn_cols = (lambda w: by_rows(w.reshape(DIM, FFN_I // 4, 4).transpose(0, 2, 1).reshape(DIM, FFN_I)))
    arrays = {
        "x": i["x"].reshape(TILES, P, DIM),
        "ctxT": by_rows(i["ctx_2048"].reshape(TOKENS, DIM).T),
        "mask_row": i["mask_BxS2_if1"].reshape(1, TOKENS),
        "mask_col": i["mask_BxS2_if1"].reshape(TILES, P).T,
        "g_x": everywhere(i["g_xattn"]),
        "g_f": everywhere(i["g_ffn"]),
        "wh": i["L0_xattn_Wh"].transpose(1, 0, 2),
        "wg": by_rows(i["L0_xattn_wg_w"]),
        "wo0": by_rows(i["L0_xattn_wo_w"]),
        "gamma": everywhere(i["L0_xattn_gn_gamma"]),
        "beta": everywhere(i["L0_xattn_gn_beta"]),
        "router": by_rows(i["L0_ffn_router_w"].T),
        "e_gate": by_rows(i["L0_ffn_gate_w"].reshape(-1, DIM).T),
        "e_up": by_rows(i["L0_ffn_up_w"].reshape(-1, DIM).T),
        "e_down": by_rows(i["L0_ffn_down_w"].transpose(0, 2, 1).reshape(-1, DIM)),
        "wq": by_rows(i["L1_xattn_w_q"].T),
        "wk": by_rows(_np.concatenate([wk, wk], axis=1)),
        "wv": by_rows(i["L1_xattn_w_v"].T),
        "wo1": by_rows(i["L1_xattn_w_o"].T),
        "bo": everywhere(i["L1_xattn_b_o"]),
        "f_gate": ffn_cols(i["L1_ffn_w_gate"]),
        "f_up": ffn_cols(i["L1_ffn_w_up"]),
        "f_down": by_rows(i["L1_ffn_w_down"].reshape(FFN_BLOCKS, P, 4, DIM).transpose(0, 2, 1, 3).reshape(FFN_I, DIM)),
    }
    arrays.update(shape_constants())
    for n in ("caus", "identb"):
        arrays[n] = arrays[n].astype(_mybir.dt.np(_mybir.dt.bfloat16))
    arrays = {f"in_{n}_dram": _np.ascontiguousarray(v) for n, v in arrays.items()}

    nc = _bacc.Bacc("TRN2", target_bir_lowering=False, num_devices=1)
    args = {n[3:-5]: nc.dram_tensor(n, v.shape, _mybir.dt.from_np(v.dtype), kind="ExternalInput").ap()
            for n, v in arrays.items()}
    out = nc.dram_tensor("out_0_dram", (TILES, P, DIM), _mybir.dt.float32, kind="ExternalOutput").ap()
    build_program(nc, args, out)
    r = _run(nc, [arrays], core_ids=[0])
    return r.results[0]["out_0_dram"].reshape(BATCH, SEQ, DIM)
```

```python
import numpy as np
import concourse.bass as bass
from concourse import mybir
from contextlib import ExitStack


P = 128
BATCH, SEQ, DIM = 4, 256, 256
TOKENS = BATCH * SEQ
TILES = TOKENS // P
KT = DIM // P
UNIT = 512
UNITS = TOKENS // UNIT
UNIT_TILES = UNIT // P
RET_HEADS, RET_HD = 2, 128
EXPERTS, EXPERT_I = 8, 176
MOE_MT = EXPERTS * EXPERT_I // P
HEADS, GROUPS, HD = 32, 8, 8
PER_GROUP = HEADS // GROUPS
QUADS = 4
HALVES = GROUPS // QUADS
FFN_I = 1024
FFN_MT = FFN_I // P
FFN_BLOCKS = FFN_I // 4 // P
LN_EPS, GN_EPS = 1e-5, 1e-3
MASKED = -float(2.0 ** 100)
DEAD = -3.0e38


def build_program(nc, a, out):
    F32, F32R, BF16, I32 = mybir.dt.float32, mybir.dt.float32r, mybir.dt.bfloat16, mybir.dt.int32
    ALU = mybir.AluOpType
    ACT = mybir.ActivationFunctionType
    AX = mybir.AxisListType.X

    ctx = ExitStack()
    with ctx:
        def sb(name, shape, dt=F32):
            return ctx.enter_context(nc.sbuf_tensor(name, shape, dt))

        sems = {}

        def sem(name):
            if name not in sems:
                sems[name] = ctx.enter_context(nc.semaphore(name))
            return sems[name]

        x_sb = sb("x_sb", [P, TILES, DIM])
        ctxT = sb("ctxT", [P, KT, TOKENS])
        wh = sb("wh", [P, RET_HEADS, RET_HD])
        wg = sb("wg", [P, KT, DIM])
        wo0 = sb("wo0", [P, KT, DIM])
        gamma = sb("gamma", [P, DIM])
        beta = sb("beta", [P, DIM])
        decay = sb("decay", [P, RET_HEADS, 3 * P])
        router = sb("router", [P, KT, EXPERTS])
        e_gate = sb("e_gate", [P, KT, MOE_MT * P])
        e_up = sb("e_up", [P, KT, MOE_MT * P])
        e_down = sb("e_down", [P, MOE_MT, DIM])
        wq = sb("wq", [P, KT, DIM])
        wk = sb("wk", [P, KT, P])
        wv = sb("wv", [P, KT, GROUPS * HD])
        wo1 = sb("wo1", [P, KT, DIM])
        bo = sb("bo", [P, DIM])
        f_gate = e_gate[:, :, 0:FFN_I]
        f_up = e_up[:, :, 0:FFN_I]
        f_down = e_down[:, 0:FFN_MT, :]
        gates = sb("gates", [P, 4])
        mask_col = sb("mask_col", [P, TILES], I32)
        ident = sb("ident", [P, P])
        small_c = sb("small_c", [P, 16])

        tg = sb("tg", [P, 4])
        bo_t = sb("bo_t", [P, DIM])
        selr = sb("selr", [P, 10 * P], F32R)
        identb = sb("identb", [P, P], BF16)
        causb = sb("causb", [P, 4, P], BF16)
        padselr = sb("padselr", [1, P], F32R)
        padrow = sb("padrow", [1, TOKENS], F32R)
        padcol = sb("padcol", [P, TILES])
        eselr = sb("eselr", [2 * EXPERTS, MOE_MT * P], F32R)
        power = sb("power", [P, 1])
        stats = sb("stats", [P, 5, TILES, 6])
        mv = sb("mv", [P, 5, TILES, 2])
        veps = sb("veps", [P, 5, TILES])
        rstd = sb("rstd", [P, 5, TILES])
        xn = sb("xn", [P, 2, DIM])
        xT = sb("xT", [P, KT, TOKENS])
        logit = sb("logit", [P, TILES, EXPERTS])
        r_a = sb("r_a", [P, TILES, EXPERTS])
        r_b = sb("r_b", [P, TILES, EXPERTS])
        onehot = sb("onehot", [P, TILES, EXPERTS])
        r_s = sb("r_s", [P, 6, TILES])
        comb = sb("comb", [P, TILES, EXPERTS])
        combs = sb("combs", [P, TILES, 2 * EXPERTS], F32R)
        combT = sb("combT", [2 * EXPERTS, TOKENS], F32R)
        silu = sb("silu", [P, 2, UNIT])
        prod = sb("prod", [P, 2, UNIT])
        vaug = sb("vaug", [P, TILES, GROUPS, 32])
        mx = sb("mx", [P, 2, 2, QUADS, HALVES, PER_GROUP])
        nmx = sb("nmx", [P, 2, 2, 2 * HEADS], F32R)
        nmT = sb("nmT", [2 * HEADS, 2, SEQ], F32R)

        rden = sb("rden", [P, 2, HALVES, QUADS])
        att = sb("att", [P, 2, DIM])
        actT = sb("actT", [P, 2, KT, P])
        region = sb("region", [P, 2, 6144])
        act_e = [region[:, u, 0:MOE_MT * UNIT].rearrange("p (m n) -> p m n", m=MOE_MT) for u in range(2)]
        pt0 = [region[:, u, 0:4096].rearrange("p (j h n) -> p j h n", j=QUADS, h=PER_GROUP) for u in range(2)]
        pt1 = [region[:, u, 4096:6144].rearrange("p (j h n) -> p j h n", j=QUADS, h=PER_GROUP) for u in range(2)]
        hs = [region[:, u, 0:4096].rearrange("p (m n) -> p m n", m=FFN_MT) for u in range(2)]
        absh = [region[:, u, 4096:6144].rearrange("p (j n) -> p j n", j=4) for u in range(2)]
        ret = region[:, 0, :]
        kT0 = ret[:, 0:2048].rearrange("p (h n) -> p h n", h=2)
        qT0 = ret[:, 2048:4096].rearrange("p (h n) -> p h n", h=2)
        v0 = ret[:, 4096:6144].rearrange("p (t h n) -> p t h n", t=2, h=2)
        o_sb = region[:, 1, 0:2048].rearrange("p (k n) -> p k n", k=TILES)
        sel_in = region[:, 1, 2048:2048 + 11 * P]
        esel_in = region[0:2 * EXPERTS, 1, 3456:3456 + MOE_MT * P]
        mask_row = region[0:1, 1, 4864:4864 + TOKENS].bitcast(I32)
        amat = sb("amat", [P, RET_HEADS, 4 * P])
        aneg = silu[:, :, 0:3 * P]
        qhi = sb("qhi", [P, 2, HALVES, SEQ], F32R)
        qlo = sb("qlo", [P, 2, HALVES, SEQ], F32R)
        khl = sb("khl", [P, 2, SEQ], F32R)
        qst = sb("qst", [P, 2, HALVES, PER_GROUP, SEQ], F32R)
        kst = sb("kst", [P, 2, HALVES, SEQ], F32R)
        avT = (prod, amat[:, :, :])
        cmps = ctxT[:, :, :].rearrange("p t n -> p (t n)").bitcast(BF16).rearrange("p (c n) -> p c n", n=UNIT)
        cmp1, cmp2, cmp3 = cmps[:, 0:3, :], cmps[:, 3:5, :], cmps[:, 5, :]
        wins = amat[:, :, :].rearrange("p h n -> p (h n)").bitcast(BF16).rearrange("p (c n) -> p c n", n=UNIT)

        banks = [ctx.enter_context(nc.psum_tensor(f"bank{i}", [P, UNIT], F32)) for i in range(8)]
        KINDS = {"main": (0, 1, 2, 3), "turn": (4, 5), "tok": (6, 7),
                 "max": (0, 1, 2), "exp": (3, 4, 5), "wide": (0, 1, 2, 3, 4, 5),
                 "turn1": (6,), "tok1": (7,), "last": (6, 7)}
        fills, occupant, turns = {}, {}, {}

        def acquire(pe, stage, i, kind):
            n = turns.get(kind, 0)
            turns[kind] = n + 1
            bank = KINDS[kind][n % len(KINDS[kind])]
            if bank in occupant:
                before, m = occupant[bank]
                pe.wait_ge(sem(before + "_taken"), m + 1)
            occupant[bank] = (stage, i)
            fills[stage, i] = banks[bank][:, :]
            return fills[stage, i]

        def filled(eng, stage, i):
            eng.wait_ge(sem(stage + "_ready"), i + 1)
            return fills[stage, i]

        def ready(ins, stage):
            ins.then_inc(sem(stage + "_ready"), 1)

        def taken(ins, stage):
            ins.then_inc(sem(stage + "_taken"), 1)

        def has_taken(eng, stage, i):
            eng.wait_ge(sem(stage + "_taken"), i + 1)

        def made(eng, name, n):
            eng.wait_ge(sem(name), n)

        def score_fill(n):
            q, c = divmod(n, 12)
            return (q, c, 0, slice(0, 4)) if c < 4 else (q, (c - 4) // 2, 1, slice(c % 2 * 2, c % 2 * 2 + 2))

        def weight_fill(n):
            q, c = divmod(n, 12)
            return (q, c // 2, 0, slice(c % 2 * 2, c % 2 * 2 + 2)) if c < 8 else (q, c - 8, 1, slice(0, 4))

        def tile_cols(k):
            return slice(k * P, (k + 1) * P)

        loads = {}

        def load(eng, name, dst, src):
            loads[name] = loads.get(name, 0)
            eng.dma_start(dst, src).then_inc(sem("in_" + name), 16)

        def loaded(eng, name, n=1):
            eng.wait_ge(sem("in_" + name), 16 * n)

        block = ctx.enter_context(nc.Block())

        @block.tensor
        def _(pe):
            def mm(dst, lhsT, rhs, first, last):
                return pe.matmul(dst, lhsT, rhs, start=first, stop=last)

            def ln_turn(layer, k, kind="turn"):
                dst = acquire(pe, f"ln{layer}", k, kind)
                made(pe, f"xn{layer}", k + 1)
                for t in range(KT):
                    ins = pe.transpose(dst[:, tile_cols(t)], xn[:, k % 2, tile_cols(t)], ident[:, :])
                ready(ins, f"ln{layer}")

            def turn_pair(stage, i, src, kind):
                dst = acquire(pe, stage, i, kind)
                for t in range(KT):
                    ins = pe.transpose(dst[:, tile_cols(t)], src[:, tile_cols(t)], ident[:, :])
                ready(ins, stage)

            loaded(pe, "wh")
            loaded(pe, "ctx")
            for i in range(4):
                h, u = divmod(i, UNITS)
                dst = acquire(pe, "rk", i, "main")
                ready(mm(dst, wh[:, h, :], ctxT[:, h, u * UNIT:(u + 1) * UNIT], True, True), "rk")
            for k in range(TILES):
                dst = acquire(pe, "rv", k, "main")
                for h in range(RET_HEADS):
                    ins = mm(dst[:, h * P:(h + 1) * P], ctxT[:, h, tile_cols(k)], wh[:, h, :], True, True)
                ready(ins, "rv")
            loaded(pe, "ident")
            for k in range(TILES):
                ln_turn(0, k)
            for i in range(4):
                h, u = divmod(i, UNITS)
                dst = acquire(pe, "rq", i, "main")
                has_taken(pe, "ln0", UNIT_TILES * (u + 1) - 1)
                ready(mm(dst, wh[:, h, :], xT[:, h, u * UNIT:(u + 1) * UNIT], True, True), "rq")
            has_taken(pe, "rk", 3)
            for h in range(RET_HEADS):
                dst = acquire(pe, "rs", h, "main")
                has_taken(pe, "rq", 2 * h + 1)
                for t in range(2):
                    for b in range(BATCH):
                        at = b * SEQ + t * P
                        ins = mm(dst[:, 2 * P * t:2 * P * t + SEQ - t * P], kT0[:, h, at:at + P],
                                 qT0[:, h, at:(b + 1) * SEQ], b == 0, b == BATCH - 1)
                ready(ins, "rs")
            loaded(pe, "wg")
            has_taken(pe, "rv", TILES - 1)
            for i in range(4):
                st, h = divmod(i, 2)
                dst = acquire(pe, "ro", i, "main")
                made(pe, "a_made", 2 * h + 2)
                for t in range(2):
                    ins = mm(dst, amat[:, h, t * SEQ + st * P:t * SEQ + st * P + P], v0[:, t, h, :], t == 0, t == 1)
                ready(ins, "ro")

            def gate(k):
                dst = acquire(pe, "rg", k, "main")
                for t in range(KT):
                    ins = mm(dst[:, 0:DIM], xT[:, t, tile_cols(k)], wg[:, t, :], t == 0, t == KT - 1)
                ready(ins, "rg")

            def project(k):
                dst = acquire(pe, "res0", k, "tok")[:, 0:DIM]
                has_taken(pe, "wyT", k)
                for t in range(KT):
                    ins = mm(dst, actT[:, k % 2, t, :], wo0[:, t, :], t == 0, t == KT - 1)
                ready(ins, "res0")

            gate(0)
            gate(1)
            loaded(pe, "wo0")
            for k in range(TILES + 3):
                if k < TILES:
                    has_taken(pe, "rg", k)
                    turn_pair("wyT", k, att[:, k % 2, :], "turn")
                if 1 <= k <= TILES:
                    project(k - 1)
                if k + 2 < TILES:
                    gate(k + 2)
                if k >= 3:
                    ln_turn(1, k - 3)

            loaded(pe, "router")
            for u in range(UNITS):
                dst = acquire(pe, "log", u, "main")
                for k in range(UNIT_TILES * u, UNIT_TILES * (u + 1)):
                    has_taken(pe, "ln1", k)
                    for t in range(KT):
                        c = (k % UNIT_TILES) * EXPERTS
                        ins = mm(dst[:, c:c + EXPERTS], xT[:, t, tile_cols(k)], router[:, t, :], t == 0, t == KT - 1)
                ready(ins, "log")

            def experts(u):
                us = slice(u * UNIT, (u + 1) * UNIT)
                for m in range(MOE_MT):
                    i = u * MOE_MT + m
                    for stage, w in (("eg", e_gate), ("eu", e_up)):
                        dst = acquire(pe, stage, i, "main")
                        if i == 0:
                            loaded(pe, "e_gate" if stage == "eg" else "e_up", 2)
                        for t in range(KT):
                            ins = mm(dst, w[:, t, tile_cols(m)], xT[:, t, us], t == 0, t == KT - 1)
                        ready(ins, stage)
                    if i == 0:
                        made(pe, "combs_made", UNITS)
                        made(pe, "esel_made", 1)
                        for k in range(TILES):
                            dst = acquire(pe, "cT", k, "turn")
                            ready(pe.transpose(dst[0:2 * EXPERTS, 0:P], combs[:, k, :].bitcast(F32), ident[:, :]), "cT")
                        has_taken(pe, "cT", TILES - 1)
                    dst = acquire(pe, "ec", i, "tok")
                    ready(mm(dst, eselr[:, tile_cols(m)], combT[:, us], True, True), "ec")
                has_taken(pe, "ec", (u + 1) * MOE_MT - 1)

            def experts_down(k, m):
                c = (k % UNIT_TILES) * P
                dst = (acquire(pe, "res1", k, "tok") if m == 0 else fills["res1", k])[:, 0:DIM]
                ins = mm(dst, act_e[k // UNIT_TILES][:, m, c:c + P], e_down[:, m, :], m == 0, m == MOE_MT - 1)
                if m == MOE_MT - 1:
                    ready(ins, "res1")

            experts(0)
            loaded(pe, "e_down")
            for k in range(UNIT_TILES):
                for m in range(MOE_MT):
                    experts_down(k, m)
            experts(1)

            def prep(b, one, turn):
                s = b % 2
                seq = slice(b * SEQ, (b + 1) * SEQ)
                for k in (2 * b, 2 * b + 1):
                    ln_turn(2, k, turn)
                dst = acquire(pe, "kp", b, one)
                if b == 0:
                    loaded(pe, "w1", 5)
                for t in range(KT):
                    ins = mm(dst[:, 0:SEQ], wk[:, t, :], ctxT[:, t, seq], t == 0, t == KT - 1)
                ready(ins, "kp")
                dst = acquire(pe, "vp", b, one)
                for r in range(2):
                    for t in range(KT):
                        w = GROUPS * HD
                        ins = mm(dst[:, r * w:(r + 1) * w], ctxT[:, t, tile_cols(2 * b + r)], wv[:, t, :], t == 0, t == KT - 1)
                ready(ins, "vp")
                dst = acquire(pe, "qp", b, one)
                has_taken(pe, "ln2", 2 * b + 1)
                for q in range(HALVES):
                    for t in range(KT):
                        ins = mm(dst[:, q * SEQ:(q + 1) * SEQ], wq[:, t, tile_cols(q)], xT[:, t, seq], t == 0, t == KT - 1)
                ready(ins, "qp")
                if b == 0:
                    made(pe, "sel_made", 2)
                    made(pe, "padrow_made", 1)
                has_taken(pe, "kp", b)
                for q in range(HALVES):
                    dst = acquire(pe, "ks", 2 * b + q, one)
                    mm(dst[:, 0:SEQ], selr[:, (8 + q) * P:(9 + q) * P], khl[:, s, :], True, False)
                    ready(mm(dst[:, 0:SEQ], padselr[:, :], padrow[:, seq], False, True), "ks")
                has_taken(pe, "qp", b)
                for q in range(HALVES):
                    for h in range(2):
                        dst = acquire(pe, "qs", 4 * b + 2 * q + h, one)
                        for e in range(2):
                            hg = 2 * h + e
                            mm(dst[:, e * SEQ:(e + 1) * SEQ], selr[:, hg * P:(hg + 1) * P], qhi[:, s, q, :], True, False)
                            ins = mm(dst[:, e * SEQ:(e + 1) * SEQ], selr[:, (4 + hg) * P:(5 + hg) * P], qlo[:, s, q, :], False, True)
                        ready(ins, "qs")

            def scores(b, n):
                s = b % 2
                q, j, nt, heads = score_fill(n)
                if n == 0:
                    has_taken(pe, "ks", 2 * b + 1)
                    has_taken(pe, "qs", 4 * b + 3)
                    if b == 0:
                        loaded(pe, "caus", 2)
                dst = acquire(pe, "sa", 24 * b + n, "max")
                rows = slice(32 * j, 32 * j + 32)
                w = (nt + 1) * P
                for c, hg in enumerate(range(heads.start, heads.stop)):
                    pe.matmul(dst[:, c * w:(c + 1) * w], qst[rows, s, q, hg, tile_cols(nt)],
                              kst[rows, s, q, 0:w], start=(c == 0), stop=False, skip_group_check=True)
                diagonal = dst.rearrange("p (h m) -> p h m", m=w)[:, :, nt * P:(nt + 1) * P]
                ready(pe.matmul(diagonal, identb[:, :], causb[:, 0:UNIT // w, :], start=False, stop=True,
                                skip_group_check=True), "sa")

            def neg_turn(b, kind):
                s = b % 2
                for nt in range(2):
                    dst = acquire(pe, "nmT", 2 * b + nt, kind)
                    made(pe, "nm_made", 2 * b + nt + 1)
                    ready(pe.transpose(dst[0:2 * HEADS, 0:P], nmx[:, s, nt, :].bitcast(F32), ident[:, :]), "nmT")

            def weights(b, n):
                s = b % 2
                q, j, mt, heads = weight_fill(n)
                if n == 0:
                    made(pe, "max_rows", 16 * 8 * (b + 1))
                dst = acquire(pe, "sb", 24 * b + n, "exp")
                rows = slice(32 * j, 32 * j + 32)
                ready(mm(dst, kst[rows, s, q, tile_cols(mt)], qst[rows, s, q, heads, mt * P:SEQ], True, True), "sb")

            def values(b):
                for q in range(HALVES):
                    made(pe, "causal_done", 8 * b + 4 * q + 4)
                    for nt in range(2):
                        dst = acquire(pe, "av", 4 * b + 2 * q + nt, "wide")
                        has_taken(pe, "vp", b)
                        for mt in range(nt + 1):
                            for j in range(QUADS):
                                rhs = pt0[q][:, j, :, tile_cols(nt)] if mt == 0 else pt1[q][:, j, :, :]
                                ins = pe.matmul(dst[32 * j:32 * j + 32, :], vaug[:, 2 * b + mt, 4 * q + j, :], rhs,
                                                start=(mt == 0), stop=(mt == nt), skip_group_check=True)
                        ready(ins, "av")

            def finish(b, n):
                nt, c = divmod(n, 6)
                i = 2 * b + nt
                if c < PER_GROUP:
                    f = 4 * i + c
                    dst = acquire(pe, "avT", f, "turn1")
                    if c == 0:
                        has_taken(pe, "av", 4 * b + 2 + nt)
                    for q in range(HALVES):
                        ins = pe.transpose(dst[:, tile_cols(q)], avT[nt][:, q, c * P:(c + 1) * P], ident[:, :])
                    ready(ins, "avT")
                elif c == PER_GROUP:
                    has_taken(pe, "avT", 4 * i + 3)
                    turn_pair("atT", i, att[:, i % 2, :], "turn1")
                else:
                    dst = acquire(pe, "res2", i, "tok1")[:, 0:DIM]
                    has_taken(pe, "atT", i)
                    for t in range(KT):
                        ins = mm(dst, actT[:, i % 2, t, :], wo1[:, t, :], t == 0, t == KT - 1)
                    ready(ins, "res2")

            prep(0, "main", "turn")
            rest = [(k, m) for k in range(UNIT_TILES, TILES) for m in range(MOE_MT)]
            for n in range(24):
                scores(0, n)
                for k, m in rest[2 * n:2 * n + 2]:
                    experts_down(k, m)
            neg_turn(0, "turn")
            for b in range(BATCH):
                if b + 1 < BATCH:
                    prep(b + 1, "wide", "turn1")
                for n in range(24):
                    if b + 1 < BATCH:
                        scores(b + 1, n)
                    weights(b, n)
                    if b >= 1 and n % 2 == 1:
                        finish(b - 1, n // 2)
                if b + 1 < BATCH:
                    neg_turn(b + 1, "turn1")
                values(b)

            def gate_up(g, j):
                u, blk = divmod(g, FFN_BLOCKS)
                us = slice(u * UNIT, (u + 1) * UNIT)
                c = j * 2 * P + blk * P
                for stage, w in (("fg", f_gate), ("fu", f_up)):
                    dst = acquire(pe, stage, 4 * g + j, "wide")
                    for t in range(KT):
                        ins = mm(dst, w[:, t, c:c + P], xT[:, t, us], t == 0, t == KT - 1)
                    ready(ins, stage)

            def down(k, kind, tiles):
                u, c = k // UNIT_TILES, (k % UNIT_TILES) * P
                dst = (acquire(pe, "res3", k, kind) if tiles.start == 0 else fills["res3", k])[:, 0:DIM]
                for m in tiles:
                    ins = mm(dst, hs[u][:, m, c:c + P], f_down[:, m, :], m == 0, m == FFN_MT - 1)
                if tiles.stop == FFN_MT:
                    ready(ins, "res3")

            for k in range(UNIT_TILES):
                ln_turn(3, k, "turn1")
            has_taken(pe, "ln3", UNIT_TILES - 1)
            loaded(pe, "f", 3)
            for n in range(8):
                gate_up(n // 4, n % 4)
                for c in range(2 * n, min(2 * n + 2, 12)):
                    finish(BATCH - 1, c)
            for k in range(UNIT_TILES, TILES):
                ln_turn(3, k, "turn1")
            has_taken(pe, "ln3", TILES - 1)
            for j in range(4):
                gate_up(2, j)
            for j in range(4):
                gate_up(3, j)
                if j == 0:
                    made(pe, "hs_made", 8)
                down(j, "last", range(FFN_MT))
            made(pe, "hs_made", 12)
            for k in range(UNIT_TILES, TILES):
                down(k, "wide", range(4))
            made(pe, "hs_made", 16)
            for k in range(UNIT_TILES, TILES):
                down(k, "wide", range(4, FFN_MT))


        @block.sync
        def _(sp):
            for k in range(TILES):
                load(sp, f"x{k}", x_sb[:, k, :], a["x"][k])
                if k == 0:
                    load(sp, "ident", ident[:, :], a["ident"])
                if k == 1:
                    load(sp, "gates", gates[:, 0:2], a["g_x"])
                    load(sp, "gates", gates[:, 2:4], a["g_f"])
                    load(sp, "wh", wh[:, :, :], a["wh"])
                    load(sp, "ctx", ctxT[:, :, :], a["ctxT"])
            load(sp, "decay", decay[:, :, :], a["decay"])
            load(sp, "wg", wg[:, :, :], a["wg"])
            load(sp, "gamma", gamma[:, :], a["gamma"])
            load(sp, "gamma", beta[:, :], a["beta"])
            load(sp, "wo0", wo0[:, :, :], a["wo0"])
            load(sp, "router", router[:, :, :], a["router"])
            load(sp, "small", small_c[:, :], a["small"])
            load(sp, "sel", esel_in, a["esel"])
            load(sp, "sel", sel_in, a["sel"])
            load(sp, "caus", causb[:, :, :].rearrange("p h n -> p (h n)"), a["caus"])
            load(sp, "caus", identb[:, :], a["identb"])
            load(sp, "sel", mask_row, a["mask_row"])
            load(sp, "sel", mask_col[:, :], a["mask_col"])
            for t in range(KT):
                load(sp, "e_gate", e_gate[:, t, :], a["e_gate"][:, t, :])
                load(sp, "e_up", e_up[:, t, :], a["e_up"][:, t, :])
            load(sp, "e_down", e_down[:, :, :], a["e_down"])
            load(sp, "w1", wq[:, :, :], a["wq"])
            load(sp, "w1", wk[:, :, :], a["wk"])
            load(sp, "w1", wv[:, :, :], a["wv"])
            load(sp, "w1", wo1[:, :, :], a["wo1"])
            load(sp, "w1", bo[:, :], a["bo"])
            sp.wait_ge(sem("res1_ready"), TILES)
            load(sp, "f", f_gate, a["f_gate"])
            load(sp, "f", f_up, a["f_up"])
            load(sp, "f", f_down, a["f_down"])
            for b in range(BATCH):
                has_taken(sp, "nmT", 2 * b + 1)
                for piece in range(2):
                    for j in range(QUADS):
                        rows = slice(piece * HEADS + j * 8, piece * HEADS + j * 8 + 8)
                        dst = qst[32 * j + 24 + piece:32 * j + 25 + piece, b % 2, :, :, :]
                        sp.dma_start(dst.rearrange("p q h n -> p (q h) n").bitcast(F32), nmT[rows, b % 2, :].bitcast(F32))\
                          .then_inc(sem("max_rows"), 16)
            for k in range(TILES):
                has_taken(sp, "res3", k)
                sp.dma_start(out[k], x_sb[:, k, :]).then_inc(sem("stored"), 16)
            sp.wait_ge(sem("stored"), 16 * TILES)

        @block.gpsimd
        def _(pool):
            pool.memset(power[:, :], -0.5).then_inc(sem("power_set"), 1)
            pool.memset(vaug[:, :, :, :], 1.0).then_inc(sem("ones_set"), 1)
            pool.memset(amat[:, :, :], 1.0).then_inc(sem("a_set"), 1)
            made(pool, "power_set", 1)

            def inverse_std(layer, k, eps):
                made(pool, f"mv{layer}", k + 1)
                pool.tensor_scalar(veps[:, layer, k:k + 1], mv[:, layer, k, 1:2], eps, None, ALU.add)\
                    .then_inc(sem(f"veps{layer}"), 1)
                made(pool, f"veps{layer}", k + 1)
                pool.tensor_tensor(out=rstd[:, layer, k:k + 1], in0=veps[:, layer, k:k + 1],
                                   in1=power[:, :], op=ALU.pow).then_inc(sem(f"rstd{layer}"), 1)

            for k in range(TILES):
                inverse_std(0, k, LN_EPS)
            for k in range(TILES):
                inverse_std(4, k, GN_EPS)
                if k == 0:
                    loaded(pool, "gamma", 2)
                made(pool, "gn_z", k + 1)
                pool.tensor_tensor(out=o_sb[:, k, :], in0=o_sb[:, k, :], in1=gamma[:, :], op=ALU.mult)\
                    .then_inc(sem("gn_scaled"), 1)
                made(pool, "gn_scaled", k + 1)
                pool.tensor_tensor(out=o_sb[:, k, :], in0=o_sb[:, k, :], in1=beta[:, :], op=ALU.add)\
                    .then_inc(sem("gn_y"), 1)
                if k >= 3:
                    inverse_std(1, k - 3, LN_EPS)
            for k in range(TILES - 3, TILES):
                inverse_std(1, k, LN_EPS)
            for k in range(TILES):
                inverse_std(2, k, LN_EPS)
            for b in range(BATCH):
                for q in range(HALVES):
                    for n in range(4):
                        js = slice(n % 2 * 2, n % 2 * 2 + 2)
                        made(pool, "sb_taken", 24 * b + 12 * q + (4, 8, 10, 12)[n])
                        block = pt0[q][:, js, :, 0:P] if n < 2 else pt1[q][:, js, :, :]
                        pool.affine_select(out=block, in_=block, compare_op=ALU.is_ge, fill=0.0, base=0,
                                           pattern=[[0, 2], [0, PER_GROUP], [1, P]], channel_multiplier=-1)\
                            .then_inc(sem("causal_done"), 1)
                if b >= 1:
                    for k in (2 * b - 2, 2 * b - 1):
                        inverse_std(3, k, LN_EPS)
            for k in (TILES - 2, TILES - 1):
                inverse_std(3, k, LN_EPS)

        @block.scalar
        def _(act):
            loaded(act, "gates", 2)
            act.activation(tg[:, :], gates[:, :], ACT.Tanh).then_inc(sem("tanh"), 1)

            def ln_turn(layer, k):
                src = filled(act, f"ln{layer}", k)
                taken(act.activation(xT[:, :, tile_cols(k)], src[:, 0:DIM].rearrange("p (t n) -> p t n", t=KT), ACT.Copy),
                      f"ln{layer}")

            for i in range(4):
                h, u = divmod(i, UNITS)
                taken(act.activation(kT0[:, h, u * UNIT:(u + 1) * UNIT], filled(act, "rk", i), ACT.Copy), "rk")
            for k in range(TILES):
                b, t = divmod(k, 2)
                src = filled(act, "rv", k)[:, 0:256].rearrange("p (h n) -> p h n", h=2)
                taken(act.activation(v0[:, t, :, b * P:(b + 1) * P], src, ACT.Copy), "rv")
            for k in range(TILES):
                ln_turn(0, k)
            for i in range(4):
                h, u = divmod(i, UNITS)
                taken(act.activation(qT0[:, h, u * UNIT:(u + 1) * UNIT], filled(act, "rq", i), ACT.Copy), "rq")
            for i in range(4):
                st, h = divmod(i, 2)
                dst = o_sb[:, st:TILES:2, h * P:(h + 1) * P]
                taken(act.activation(dst, filled(act, "ro", i).rearrange("p (b e) -> p b e", b=BATCH), ACT.Copy), "ro")
            loaded(act, "sel", 4)
            act.activation(eselr[:, :], esel_in, ACT.Copy).then_inc(sem("esel_made"), 1)
            act.activation(selr[:, :], sel_in[:, 0:10 * P], ACT.Copy).then_inc(sem("sel_made"), 1)
            act.activation(padselr[:, :], sel_in[0:1, 10 * P:11 * P], ACT.Copy).then_inc(sem("sel_made"), 1)
            for k in range(TILES + 3):
                if k < TILES:
                    src = filled(act, "wyT", k)
                    if k >= 2:
                        act.wait_ge(sem("res0_ready"), k - 1)
                    taken(act.activation(actT[:, k % 2, :, :], src[:, 0:DIM].rearrange("p (t n) -> p t n", t=KT),
                                         ACT.Copy), "wyT")
                if k >= 3:
                    ln_turn(1, k - 3)

            for u in range(UNITS):
                made(act, "vdiff", u + 1)
                act.activation(r_s[:, 3, UNIT_TILES * u:UNIT_TILES * (u + 1)],
                               r_s[:, 2, UNIT_TILES * u:UNIT_TILES * (u + 1)], ACT.Exp).then_inc(sem("vexp"), 1)
            for i in range(UNITS * MOE_MT):
                src = filled(act, "eg", i)
                if i >= 2:
                    has_taken(act, "eu", i - 2)
                taken(act.activation(silu[:, i % 2, :], src, ACT.Silu), "eg")
                if i == 0:
                    for k in range(TILES):
                        src = filled(act, "cT", k)[0:2 * EXPERTS, 0:P]
                        taken(act.activation(combT[:, tile_cols(k)], src, ACT.Copy), "cT")

            def prep(b):
                for k in (2 * b, 2 * b + 1):
                    ln_turn(2, k)
                s = b % 2
                src = filled(act, "kp", b)
                if b >= 2:
                    act.wait_ge(sem("ks_ready"), 2 * b - 2)
                act.activation(khl[:, s, :], src[:, 0:SEQ], ACT.Copy).then_inc(sem("k_high"), 1)
                src = filled(act, "vp", b)[:, 0:2 * GROUPS * HD].rearrange("p (k g d) -> p k g d", k=2, g=GROUPS)
                if b == 0:
                    made(act, "ones_set", 1)
                for t in range(2):
                    ins = act.activation(vaug[:, 2 * b + t, :, 0:HD], src[:, t, :, :], ACT.Copy)
                taken(ins, "vp")
                src = filled(act, "qp", b).rearrange("p (q n) -> p q n", q=HALVES)
                if b >= 2:
                    act.wait_ge(sem("qs_ready"), 4 * b - 4)
                act.activation(qhi[:, s, :, :], src, ACT.Copy).then_inc(sem("q_high"), 1)
                for q in range(HALVES):
                    src = filled(act, "ks", 2 * b + q)[:, 0:SEQ]
                    if b >= 2:
                        act.wait_ge(sem("sb_ready"), 24 * (b - 1))
                    taken(act.activation(kst[:, s, q, :], src, ACT.Identity, bias=small_c[:, 1:2]), "ks")
                for q in range(HALVES):
                    for h in range(2):
                        src = filled(act, "qs", 4 * b + 2 * q + h).rearrange("p (h n) -> p h n", h=2)
                        taken(act.activation(qst[:, s, q, 2 * h:2 * h + 2, :], src, ACT.Identity,
                                             bias=small_c[:, 0:1]), "qs")

            def neg_turn(b):
                if b >= 2:
                    act.wait_ge(sem("max_rows"), 16 * 8 * (b - 1))
                for nt in range(2):
                    src = filled(act, "nmT", 2 * b + nt)[0:2 * HEADS, 0:P]
                    taken(act.activation(nmT[:, b % 2, tile_cols(nt)], src, ACT.Copy), "nmT")

            def exponentials(b, n):
                q, j, mt, heads = weight_fill(n)
                src = filled(act, "sb", 24 * b + n)
                if n == 0 and b == 0:
                    made(act, "padcol_made", 1)
                    act.wait_ge(sem("res1_ready"), TILES)
                if n == 0 and b >= 1:
                    act.wait_ge(sem("av_ready"), 4 * b)
                dst = pt0[q][:, j, heads, :] if mt == 0 else pt1[q][:, j, :, :]
                key = 2 * b + mt
                taken(act.activation(dst, src.rearrange("p (h n) -> p h n", n=SEQ - mt * P), ACT.Exp,
                                     bias=padcol[:, key:key + 1], scale=float(HD) ** -0.5), "sb")

            def value_turn(b):
                for q in range(HALVES):
                    for nt in range(2):
                        src = filled(act, "av", 4 * b + 2 * q + nt)
                        if b >= 1:
                            act.wait_ge(sem("avT_ready"), 8 * (b - 1) + 4 * nt + 4)
                        taken(act.activation(avT[nt][:, q, :], src, ACT.Copy), "av")

            def finish(b, n):
                nt, c = divmod(n, 6)
                i = 2 * b + nt
                if c == PER_GROUP:
                    src = filled(act, "atT", i)[:, 0:DIM]
                    if i >= 2:
                        act.wait_ge(sem("res2_ready"), i - 1)
                    taken(act.activation(actT[:, i % 2, :, :], src.rearrange("p (t n) -> p t n", t=KT), ACT.Copy), "atT")

            prep(0)
            neg_turn(0)
            for b in range(BATCH):
                if b + 1 < BATCH:
                    prep(b + 1)
                for n in range(24):
                    exponentials(b, n)
                    if b >= 1 and n % 2 == 1:
                        finish(b - 1, n // 2)
                if b + 1 < BATCH:
                    neg_turn(b + 1)
                value_turn(b)

            def magnitude(i):
                g, j = divmod(i, 4)
                has_taken(act, "fu", i)
                if g >= 2 and j == 0:
                    act.wait_ge(sem("compared"), 3 * (g - 1))
                u, blk = divmod(g, FFN_BLOCKS)
                act.activation(absh[g % 2][:, j, :], hs[u][:, 4 * blk + j, :], ACT.Abs).then_inc(sem("abs_made"), 1)

            for k in range(UNIT_TILES):
                ln_turn(3, k)
            for i in range(4 * FFN_BLOCKS * UNITS):
                if i == 8:
                    for k in range(UNIT_TILES, TILES):
                        ln_turn(3, k)
                src = filled(act, "fg", i)
                if i >= 2:
                    has_taken(act, "fu", i - 2)
                taken(act.activation(silu[:, i % 2, :], src, ACT.Silu), "fg")
                for c in range(2 * i, min(2 * i + 2, 12)):
                    finish(BATCH - 1, c)
                if i >= 1:
                    magnitude(i - 1)
            magnitude(4 * FFN_BLOCKS * UNITS - 1)

        @block.vector
        def _(dve):
            def stat(layer, k, src):
                dve.bn_stats(stats[:, layer, k, :], src).then_inc(sem(f"stats{layer}"), 1)
                made(dve, f"stats{layer}", k + 1)
                dve.bn_aggr(mv[:, layer, k, :], stats[:, layer, k, :]).then_inc(sem(f"mv{layer}"), 1)

            def norm(layer, k):
                made(dve, f"rstd{layer}", k + 1)
                if k >= 2:
                    dve.wait_ge(sem(f"ln{layer}_ready"), k - 1)
                elif layer:
                    dve.wait_ge(sem(f"ln{layer - 1}_ready"), TILES - 1 + k)
                dve.tensor_scalar(xn[:, k % 2, :], x_sb[:, k, :], mv[:, layer, k, 0:1], rstd[:, layer, k:k + 1],
                                  ALU.subtract, ALU.mult).then_inc(sem(f"xn{layer}"), 1)

            loaded(dve, "x0")
            stat(0, 0, x_sb[:, 0, :])
            for k in range(TILES):
                if k + 1 < TILES:
                    loaded(dve, f"x{k + 1}")
                    stat(0, k + 1, x_sb[:, k + 1, :])
                norm(0, k)

            loaded(dve, "decay")
            made(dve, "a_set", 1)
            for h in range(RET_HEADS):
                src = filled(dve, "rs", h)[:, 0:3 * P]
                taken(dve.tensor_tensor(out=aneg[:, h, :], in0=src, in1=decay[:, h, :], op=ALU.mult), "rs")
                has_taken(dve, "rs", h)
                for n, (o, w, d) in enumerate(((0, 2 * P, 0), (2 * P, P, 3 * P))):
                    dve.scalar_tensor_tensor(out=amat[:, h, d:d + w], in0=aneg[:, h, o:o + w], scalar=-1.0,
                                             in1=aneg[:, h, o:o + w], op0=ALU.mult, op1=ALU.max)\
                       .then_inc(sem("a_abs"), 1)
                    made(dve, "a_abs", 2 * h + n + 1)
                    dve.tensor_scalar(amat[:, h, d:d + w], amat[:, h, d:d + w], 1.0, None, ALU.max)\
                       .then_inc(sem("a_made"), 1)

            def residual(stage, k, g):
                dve.scalar_tensor_tensor(out=x_sb[:, k, :], in0=filled(dve, stage, k)[:, 0:DIM], scalar=tg[:, g:g + 1],
                                         in1=x_sb[:, k, :], op0=ALU.mult, op1=ALU.add)\
                   .then_inc(sem(stage + "_taken"), 1)

            loaded(dve, "sel", 4)
            loaded(dve, "small")
            dve.tensor_scalar(padrow[:, :], mask_row, 0.0, MASKED, ALU.is_equal, ALU.mult)\
               .then_inc(sem("padrow_made"), 1)
            dve.tensor_scalar(padcol[:, :], mask_col[:, :], 0.0, DEAD, ALU.is_equal, ALU.mult)\
               .then_inc(sem("padcol_made"), 1)

            def gn_scale(k):
                made(dve, "rstd4", k + 1)
                dve.tensor_scalar(o_sb[:, k, :], o_sb[:, k, :], mv[:, 4, k, 0:1], rstd[:, 4, k:k + 1],
                                  ALU.subtract, ALU.mult).then_inc(sem("gn_z"), 1)

            made(dve, "tanh", 1)
            dve.wait_ge(sem("ro_taken"), 4)
            for k in range(3):
                stat(4, k, o_sb[:, k, :])
            gn_scale(0)
            gn_scale(1)
            for k in range(TILES + 3):
                if k < TILES:
                    made(dve, "gn_y", k + 1)
                    src = filled(dve, "rg", k)[:, 0:DIM]
                    if k >= 2:
                        dve.wait_ge(sem("wyT_ready"), k - 1)
                    taken(dve.scalar_tensor_tensor(out=att[:, k % 2, :], in0=src, scalar=0.0, in1=o_sb[:, k, :],
                                                   op0=ALU.max, op1=ALU.mult), "rg")
                if k + 3 < TILES:
                    stat(4, k + 3, o_sb[:, k + 3, :])
                if k + 2 < TILES:
                    gn_scale(k + 2)
                if 1 <= k <= TILES:
                    residual("res0", k - 1, 0)
                    has_taken(dve, "res0", k - 1)
                    stat(1, k - 1, x_sb[:, k - 1, :])
                if k >= 3:
                    norm(1, k - 3)

            def route(u):
                ks = slice(UNIT_TILES * u, UNIT_TILES * (u + 1))
                wide8 = [P, UNIT_TILES, EXPERTS]
                n = [0]

                def step(ins):
                    n[0] += 1
                    ins.then_inc(sem(f"route{u}"), 1)
                    dve.wait_ge(sem(f"route{u}"), n[0])

                def each(v):
                    return v.unsqueeze(2).to_broadcast(wide8)

                src = filled(dve, "log", u)[:, 0:UNIT_TILES * EXPERTS].rearrange("p (k e) -> p k e", e=EXPERTS)
                taken(dve.tensor_copy(logit[:, ks, :], src), "log")
                has_taken(dve, "log", u)
                step(dve.reduce_max(r_s[:, 0, ks], logit[:, ks, :], AX))
                step(dve.tensor_tensor(out=r_a[:, ks, :], in0=logit[:, ks, :], in1=each(r_s[:, 0, ks]), op=ALU.is_equal))
                rev = small_c[:, 8:16].unsqueeze(1).to_broadcast(wide8)
                step(dve.tensor_tensor(out=r_b[:, ks, :], in0=r_a[:, ks, :], in1=rev, op=ALU.mult))
                step(dve.reduce_max(r_s[:, 1, ks], r_b[:, ks, :], AX))
                step(dve.tensor_tensor(out=onehot[:, ks, :], in0=r_b[:, ks, :], in1=each(r_s[:, 1, ks]), op=ALU.is_equal))
                step(dve.scalar_tensor_tensor(out=r_a[:, ks, :], in0=onehot[:, ks, :], scalar=DEAD,
                                              in1=logit[:, ks, :], op0=ALU.mult, op1=ALU.add))
                step(dve.reduce_max(r_s[:, 1, ks], r_a[:, ks, :], AX))
                dve.tensor_tensor(out=r_s[:, 2, ks], in0=r_s[:, 1, ks], in1=r_s[:, 0, ks], op=ALU.subtract)\
                   .then_inc(sem("vdiff"), 1)
                made(dve, "vexp", u + 1)
                step(dve.tensor_scalar(r_s[:, 4, ks], r_s[:, 3, ks], 1.0, None, ALU.add))
                step(dve.reciprocal(r_s[:, 5, ks], r_s[:, 4, ks]))
                step(dve.tensor_tensor(out=comb[:, ks, :], in0=onehot[:, ks, :], in1=each(r_s[:, 5, ks]), op=ALU.mult))
                step(dve.tensor_copy(combs[:, ks, 0:EXPERTS], comb[:, ks, :]))
                dve.tensor_tensor(out=combs[:, ks, EXPERTS:2 * EXPERTS], in0=comb[:, ks, :],
                                  in1=combs[:, ks, 0:EXPERTS].bitcast(F32), op=ALU.subtract).then_inc(sem("combs_made"), 1)

            for u in range(UNITS):
                route(u)

            def expert_residual(k):
                residual("res1", k, 2)
                has_taken(dve, "res1", k)
                stat(2, k, x_sb[:, k, :])

            for u in range(UNITS):
                if u == 1:
                    made(dve, "esel_made", 1)
                    made(dve, "sel_made", 2)
                for m in range(MOE_MT):
                    i = u * MOE_MT + m
                    src = filled(dve, "eu", i)
                    has_taken(dve, "eg", i)
                    if i >= 2:
                        has_taken(dve, "ec", i - 2)
                    taken(dve.tensor_tensor(out=prod[:, i % 2, :], in0=src, in1=silu[:, i % 2, :], op=ALU.mult), "eu")
                    src = filled(dve, "ec", i)
                    has_taken(dve, "eu", i)
                    taken(dve.tensor_tensor(out=act_e[u][:, m, :], in0=src, in1=prod[:, i % 2, :], op=ALU.mult), "ec")
                if u == 0:
                    for k in range(UNIT_TILES):
                        expert_residual(k)

            def low_parts(b):
                s = b % 2
                made(dve, "k_high", b + 1)
                src = filled(dve, "kp", b)[64:128, 0:SEQ]
                taken(dve.tensor_tensor(out=khl[64:128, s, :], in0=src, in1=khl[64:128, s, :].bitcast(F32),
                                        op=ALU.subtract), "kp")
                made(dve, "q_high", b + 1)
                src = filled(dve, "qp", b).rearrange("p (q n) -> p q n", q=HALVES)
                if b >= 2:
                    dve.wait_ge(sem("qs_ready"), 4 * b - 4)
                taken(dve.tensor_tensor(out=qlo[:, s, :, :], in0=src, in1=qhi[:, s, :, :].bitcast(F32),
                                        op=ALU.subtract), "qp")

            def row_maxima(b, n):
                q, j, nt, heads = score_fill(n)
                src = filled(dve, "sa", 24 * b + n).rearrange("p (h m) -> p h m", m=(nt + 1) * P)
                taken(dve.reduce_max(mx[:, b % 2, nt, j, q, heads], src, AX), "sa")

            def negate(b):
                s = b % 2
                has_taken(dve, "sa", 24 * b + 23)
                if b >= 2:
                    dve.wait_ge(sem("nmT_ready"), 2 * (b - 1))
                for nt in range(2):
                    m = mx[:, s, nt, :, :, :].rearrange("p j q h -> p (j q h)")
                    dve.tensor_scalar(nmx[:, s, nt, 0:HEADS], m, -1.0, None, ALU.mult).then_inc(sem("nm_high"), 1)
                    made(dve, "nm_high", 2 * b + nt + 1)
                    dve.scalar_tensor_tensor(out=nmx[:, s, nt, HEADS:2 * HEADS], in0=m, scalar=-1.0,
                                             in1=nmx[:, s, nt, 0:HEADS].bitcast(F32), op0=ALU.mult,
                                             op1=ALU.subtract).then_inc(sem("nm_made"), 1)

            def finish(b, n):
                nt, c = divmod(n, 6)
                i = 2 * b + nt
                if c == 0 and i >= 2:
                    dve.wait_ge(sem("atT_ready"), i - 1)
                if c < PER_GROUP:
                    o = att[:, i % 2, :].rearrange("p (q j h d) -> p h q j d", q=HALVES, j=QUADS, h=PER_GROUP)
                    f = 4 * i + c
                    src = filled(dve, "avT", f)[:, 0:2 * P].rearrange("p (q j r) -> p q j r", q=HALVES, j=QUADS)
                    dve.reciprocal(rden[:, f % 2, :, :], src[:, :, :, HD]).then_inc(sem("rden_made"), 1)
                    made(dve, "rden_made", f + 1)
                    taken(dve.tensor_tensor(out=o[:, c, :, :, :], in0=src[:, :, :, 0:HD],
                                            in1=rden[:, f % 2, :, :].unsqueeze(3).to_broadcast([P, HALVES, QUADS, HD]),
                                            op=ALU.mult), "avT")
                elif c > PER_GROUP:
                    residual("res2", i, 1)
                    has_taken(dve, "res2", i)
                    dve.tensor_tensor(out=x_sb[:, i, :], in0=x_sb[:, i, :], in1=bo_t[:, :], op=ALU.add)\
                       .then_inc(sem("x3"), 1)
                    made(dve, "x3", i + 1)
                    stat(3, i, x_sb[:, i, :])

            loaded(dve, "w1", 5)
            dve.tensor_scalar(bo_t[:, :], bo[:, :], tg[:, 1:2], None, ALU.mult).then_inc(sem("bo_made"), 1)
            made(dve, "bo_made", 1)

            def prep(b):
                for k in (2 * b, 2 * b + 1):
                    norm(2, k)
                low_parts(b)

            prep(0)
            for n in range(24):
                row_maxima(0, n)
                for k in range(UNIT_TILES, TILES):
                    if n == min((MOE_MT * (k - UNIT_TILES + 1) - 1) // 2 + 1, 23):
                        expert_residual(k)
            negate(0)
            for b in range(BATCH):
                if b + 1 < BATCH:
                    prep(b + 1)
                for n in range(24):
                    if b + 1 < BATCH:
                        row_maxima(b + 1, n)
                    if b >= 1 and n % 2 == 1:
                        finish(b - 1, n // 2)
                if b + 1 < BATCH:
                    negate(b + 1)

            def sparsify(g, step):
                u, blk = divmod(g, FFN_BLOCKS)
                m = absh[g % 2]
                if step == 0:
                    made(dve, "abs_made", 4 * g + 4)
                    if g >= 1:
                        made(dve, "hs_made", 4 * g)
                    dve.tensor_tensor(out=cmp1[:, :, :], in0=m[:, 0:3, :], in1=m[:, 1:4, :], op=ALU.is_ge)\
                       .then_inc(sem("compared"), 1)
                    dve.tensor_tensor(out=cmp2[:, :, :], in0=m[:, 0:2, :], in1=m[:, 2:4, :], op=ALU.is_ge)\
                       .then_inc(sem("compared"), 1)
                    dve.tensor_tensor(out=cmp3[:, :], in0=m[:, 0, :], in1=m[:, 3, :], op=ALU.is_ge)\
                       .then_inc(sem("compared"), 1)
                elif step == 1:
                    made(dve, "compared", 3 * g + 3)
                    dve.tensor_tensor(out=wins[:, 0:2, :], in0=cmp1[:, 0:2, :], in1=cmp2[:, :, :], op=ALU.add)\
                       .then_inc(sem("wins_a"), 1)
                    dve.tensor_tensor(out=wins[:, 2, :], in0=cmp1[:, 2, :], in1=cmp2[:, 0, :], op=ALU.subtract)\
                       .then_inc(sem("wins_a"), 1)
                    dve.tensor_tensor(out=wins[:, 3, :], in0=cmp1[:, 2, :], in1=cmp2[:, 1, :], op=ALU.add)\
                       .then_inc(sem("wins_a"), 1)
                    made(dve, "wins_a", 3 * g + 3)
                    dve.tensor_tensor(out=wins[:, 0, :], in0=wins[:, 0, :], in1=cmp3[:, :], op=ALU.add)\
                       .then_inc(sem("wins_b"), 1)
                    dve.tensor_tensor(out=wins[:, 1, :], in0=wins[:, 1, :], in1=cmp1[:, 0, :], op=ALU.subtract)\
                       .then_inc(sem("wins_b"), 1)
                    dve.tensor_tensor(out=wins[:, 2, :], in0=wins[:, 2, :], in1=cmp1[:, 1, :], op=ALU.subtract)\
                       .then_inc(sem("wins_b"), 1)
                    dve.tensor_tensor(out=wins[:, 3, :], in0=wins[:, 3, :], in1=cmp3[:, :], op=ALU.add)\
                       .then_inc(sem("wins_b"), 1)
                else:
                    if step == 2:
                        made(dve, "wins_b", 4 * g + 4)
                    for j in (2 * step - 4, 2 * step - 3):
                        op, least = ((ALU.is_ge, 2.0), (ALU.is_ge, 1.0), (ALU.is_ge, 0.0), (ALU.is_le, 1.0))[j]
                        h = hs[u][:, 4 * blk + j, :]
                        dve.scalar_tensor_tensor(out=h, in0=wins[:, j, :], scalar=least, in1=h,
                                                 op0=op, op1=ALU.mult).then_inc(sem("hs_made"), 1)

            for k in range(UNIT_TILES):
                norm(3, k)
            for g in range(FFN_BLOCKS * UNITS):
                if g == FFN_BLOCKS:
                    for k in range(UNIT_TILES, TILES):
                        norm(3, k)
                for j in range(4):
                    i = 4 * g + j
                    u, blk = divmod(g, FFN_BLOCKS)
                    src = filled(dve, "fu", i)
                    has_taken(dve, "fg", i)
                    taken(dve.tensor_tensor(out=hs[u][:, 4 * blk + j, :], in0=src, in1=silu[:, i % 2, :], op=ALU.mult), "fu")
                    for c in range(2 * i, min(2 * i + 2, 12)):
                        finish(BATCH - 1, c)
                    if g >= 1:
                        sparsify(g - 1, j)
                    if g == FFN_BLOCKS * UNITS - 1:
                        residual("res3", j, 3)
            for step in range(4):
                sparsify(FFN_BLOCKS * UNITS - 1, step)
            for k in range(UNIT_TILES, TILES):
                residual("res3", k, 3)


def shape_constants():
    f = np.float32
    gam = (f(1.0) - f(2.0) ** (f(-5.0) - np.arange(RET_HEADS, dtype=f))).astype(f)
    idx = np.arange(SEQ, dtype=f)
    expo = idx[None, :] - idx[:, None]
    low = expo <= 0
    D = np.where(low[None], gam[:, None, None] ** np.where(low, expo, 0)[None], 0).astype(f)
    Dn = D / np.sqrt(D.sum(axis=-1, dtype=f))[:, None, :] / np.sqrt(f(RET_HD))
    G = Dn.transpose(0, 2, 1)
    decay = np.concatenate([G[:, :P, :], G[:, P:, P:]], axis=2).transpose(1, 0, 2)
    sel = np.zeros((P, 11, P), f)
    for j in range(QUADS):
        for d in range(HD):
            for hg in range(PER_GROUP):
                row = j * 32 + hg * HD + d
                sel[row, hg, [32 * j + d, 32 * j + 8 + d]] = 1
                sel[row, 4 + hg, 32 * j + 16 + d] = 1
            for q in range(HALVES):
                row = (QUADS * q + j) * HD + d
                sel[row, 8 + q, [32 * j + d, 32 * j + 16 + d]] = 1
                sel[64 + row, 8 + q, 32 * j + 8 + d] = 1
        sel[0, 10, 32 * j + 26] = 1
    expert = np.arange(MOE_MT * P) // EXPERT_I
    esel = (expert[None, :] == (np.arange(2 * EXPERTS) % EXPERTS)[:, None]).astype(f)
    small = np.zeros((P, 16), f)
    small[26::32, 0] = 1
    small[24::32, 1] = 1
    small[25::32, 1] = 1
    small[:, 8:16] = np.arange(EXPERTS, 0, -1)
    n = np.arange(P)
    later = np.where(n[None, :] > n[:, None], f(MASKED), f(0))
    caus = np.tile(later, (1, 4)).astype(f)
    return {"decay": decay, "sel": sel.reshape(P, 11 * P), "esel": esel, "small": small,
            "ident": np.eye(P, dtype=f), "caus": caus,
            "identb": np.eye(P, dtype=f)}


def kernel(**inputs):
    import numpy as _np
    import concourse.bacc as _bacc
    from concourse import mybir as _mybir
    from concourse.bass_utils import run_bass_kernel_spmd as _run

    i = {k: _np.asarray(v) for k, v in inputs.items()}

    def by_rows(w):
        return w.reshape(w.shape[0] // P, P, w.shape[1]).transpose(1, 0, 2)

    def everywhere(v):
        return _np.broadcast_to(v[None, :], (P, v.shape[0]))

    wk = i["L1_xattn_w_k"].T
    ffn_cols = (lambda w: by_rows(w.reshape(DIM, FFN_I // 4, 4).transpose(0, 2, 1).reshape(DIM, FFN_I)))
    arrays = {
        "x": i["x"].reshape(TILES, P, DIM),
        "ctxT": by_rows(i["ctx_2048"].reshape(TOKENS, DIM).T),
        "mask_row": i["mask_BxS2_if1"].reshape(1, TOKENS),
        "mask_col": i["mask_BxS2_if1"].reshape(TILES, P).T,
        "g_x": everywhere(i["g_xattn"]),
        "g_f": everywhere(i["g_ffn"]),
        "wh": i["L0_xattn_Wh"].transpose(1, 0, 2),
        "wg": by_rows(i["L0_xattn_wg_w"]),
        "wo0": by_rows(i["L0_xattn_wo_w"]),
        "gamma": everywhere(i["L0_xattn_gn_gamma"]),
        "beta": everywhere(i["L0_xattn_gn_beta"]),
        "router": by_rows(i["L0_ffn_router_w"].T),
        "e_gate": by_rows(i["L0_ffn_gate_w"].reshape(-1, DIM).T),
        "e_up": by_rows(i["L0_ffn_up_w"].reshape(-1, DIM).T),
        "e_down": by_rows(i["L0_ffn_down_w"].transpose(0, 2, 1).reshape(-1, DIM)),
        "wq": by_rows(i["L1_xattn_w_q"].T),
        "wk": by_rows(_np.concatenate([wk, wk], axis=1)),
        "wv": by_rows(i["L1_xattn_w_v"].T),
        "wo1": by_rows(i["L1_xattn_w_o"].T),
        "bo": everywhere(i["L1_xattn_b_o"]),
        "f_gate": ffn_cols(i["L1_ffn_w_gate"]),
        "f_up": ffn_cols(i["L1_ffn_w_up"]),
        "f_down": by_rows(i["L1_ffn_w_down"].reshape(FFN_BLOCKS, P, 4, DIM).transpose(0, 2, 1, 3).reshape(FFN_I, DIM)),
    }
    arrays.update(shape_constants())
    for n in ("caus", "identb"):
        arrays[n] = arrays[n].astype(_mybir.dt.np(_mybir.dt.bfloat16))
    arrays = {f"in_{n}_dram": _np.ascontiguousarray(v) for n, v in arrays.items()}

    nc = _bacc.Bacc("TRN2", target_bir_lowering=False, num_devices=1)
    args = {n[3:-5]: nc.dram_tensor(n, v.shape, _mybir.dt.from_np(v.dtype), kind="ExternalInput").ap()
            for n, v in arrays.items()}
    out = nc.dram_tensor("out_0_dram", (TILES, P, DIM), _mybir.dt.float32, kind="ExternalOutput").ap()
    build_program(nc, args, out)
    r = _run(nc, [arrays], core_ids=[0])
    return r.results[0]["out_0_dram"].reshape(BATCH, SEQ, DIM)
```

```python
import numpy as np
import concourse.bass as bass
from concourse import mybir
from contextlib import ExitStack


P = 128
BATCH, SEQ, DIM = 4, 256, 256
TOKENS = BATCH * SEQ
TILES = TOKENS // P
KT = DIM // P
HALF_ORDER = tuple(range(0, TILES, 2)) + tuple(range(1, TILES, 2))
UNIT = 512
UNITS = TOKENS // UNIT
UNIT_TILES = UNIT // P
RET_HEADS, RET_HD = 2, 128
EXPERTS, EXPERT_I = 8, 176
SLOTS = TILES + EXPERTS - 1
SORTED_LOADS = (0, 2, 7)
EXPERT_R = EXPERT_I - P
HEADS, GROUPS, HD = 32, 8, 8
PER_GROUP = HEADS // GROUPS
QUADS = 4
HALVES = GROUPS // QUADS
FFN_I = 1024
FFN_MT = FFN_I // P
FFN_BLOCKS = FFN_I // 4 // P
LEAD = 12
QUERIES_AT = 10
NORM_STEPS, LATE_NORM_STEPS = (13, 15, 17, 19), (3, 4, 6, 7)
NEGATE_AT = 15
LN_EPS, GN_EPS = 1e-5, 1e-3
MASKED = -float(2.0 ** 100)
DEAD = -3.0e38


def build_program(nc, a, out):
    F32, F32R, BF16, I32 = mybir.dt.float32, mybir.dt.float32r, mybir.dt.bfloat16, mybir.dt.int32
    ALU = mybir.AluOpType
    ACT = mybir.ActivationFunctionType
    AX = mybir.AxisListType.X

    ctx = ExitStack()
    with ctx:
        def sb(name, shape, dt=F32):
            return ctx.enter_context(nc.sbuf_tensor(name, shape, dt))

        sems = {}

        def sem(name):
            if name not in sems:
                sems[name] = ctx.enter_context(nc.semaphore(name))
            return sems[name]

        x_sb = sb("x_sb", [P, TILES, DIM])
        ctxT = sb("ctxT", [P, KT, TOKENS])
        gamma = sb("gamma", [P, DIM])
        beta = sb("beta", [P, DIM])
        router = sb("router", [P, KT, EXPERTS])
        e_gu = sb("e_gu", [P, KT, EXPERTS, 2 * EXPERT_I])
        e_down = sb("e_down", [P, EXPERTS, DIM])
        wq = sb("wq", [P, KT, DIM])
        wk = sb("wk", [P, KT, P])
        wv = sb("wv", [P, KT, GROUPS * HD])
        wo1 = sb("wo1", [P, KT, DIM])
        bo = gamma
        f_flat = e_gu[:, :, :, :].rearrange("p t e n -> p (t e n)")
        f_gate = f_flat[:, 0:KT * FFN_I].rearrange("p (t n) -> p t n", t=KT)
        f_up = f_flat[:, KT * FFN_I:2 * KT * FFN_I].rearrange("p (t n) -> p t n", t=KT)
        f_down = e_down[:, :, :]
        gates = sb("gates", [P, 4])
        mask_col = sb("mask_col", [P, TILES], I32)
        ident = sb("ident", [P, P])
        small_c = sb("small_c", [P, 103])
        tri = sb("tri", [P, 2, P], BF16)

        tg = sb("tg", [P, 4])
        bo_t = beta
        selr = sb("selr", [P, 10 * P], F32R)
        identb = sb("identb", [P, P], BF16)
        causb = sb("causb", [P, 4, P], BF16)
        padselr = sb("padselr", [1, P], F32R)
        padrow = sb("padrow", [1, TOKENS], F32R)
        padcol = sb("padcol", [P, TILES])
        power = sb("power", [P, 1])
        stats = sb("stats", [P, 5, TILES, 6])
        mv = sb("mv", [P, 5, TILES, 2])
        veps = sb("veps", [P, 5, TILES])
        rstd = sb("rstd", [P, 5, TILES])
        xn = sb("xn", [P, 2, DIM])
        xT = sb("xT", [P, KT, TOKENS])
        logit = sb("logit", [P, TILES, EXPERTS])
        r_a = sb("r_a", [P, TILES, EXPERTS])
        r_b = sb("r_b", [P, TILES, EXPERTS])
        onehot = sb("onehot", [P, TILES, EXPERTS])
        r_s = sb("r_s", [P, 12, TILES])
        onehot16 = sb("onehot16", [P, TILES, EXPERTS], BF16)
        r_slot = sb("r_slot", [P, SLOTS, EXPERTS])
        slot_f = sb("slot_f", [P, SLOTS])
        slot_expert = sb("slot_expert", [P, SLOTS], I32)
        place = sb("place", [P, TILES], I32)
        zero = sb("zero", [P, DIM])
        sT = sb("sT", [P, 4, KT, P])
        sact = sb("sact", [P, 2, EXPERT_I])
        silu = sb("silu", [P, 2, UNIT])
        prod = sb("prod", [P, 2, UNIT])
        vaug = sb("vaug", [P, TILES, GROUPS, 32])
        mx = sb("mx", [P, 2, 2, QUADS, HALVES, PER_GROUP])
        nmx = sb("nmx", [P, 2, 2, 2 * HEADS], F32R)
        nmT = sb("nmT", [2 * HEADS, 2, SEQ], F32R)

        rden = sb("rden", [P, 2, HALVES, QUADS])
        att = sb("att", [P, 2, DIM])
        actT = sb("actT", [P, 2, KT, P])
        region = sb("region", [P, 2, 6144])
        sorted_x = region[:, 0, 0:SLOTS * DIM].rearrange("p (s n) -> p s n", s=SLOTS)
        sorted_y = region[:, 1, 0:SLOTS * DIM].rearrange("p (s n) -> p s n", s=SLOTS)
        own_y = region[:, 0, 3840:5888].rearrange("p (k n) -> p k n", k=TILES)
        xn1 = region[:, 1, 4096:6144].rearrange("p (k n) -> p k n", k=TILES)
        pt0 = [region[:, u, 0:4096].rearrange("p (j h n) -> p j h n", j=QUADS, h=PER_GROUP) for u in range(2)]
        pt1 = [region[:, u, 4096:6144].rearrange("p (j h n) -> p j h n", j=QUADS, h=PER_GROUP) for u in range(2)]
        hs = [region[:, u, 0:4096].rearrange("p (m n) -> p m n", m=FFN_MT) for u in range(2)]
        absh = [region[:, u, 4096:6144].rearrange("p (j n) -> p j n", j=4) for u in range(2)]
        ret = region[:, 0, :]
        kT0 = ret[:, 0:2048].rearrange("p (h n) -> p h n", h=2)
        qT0 = ret[:, 2048:4096].rearrange("p (h n) -> p h n", h=2)
        v0 = ret[:, 4096:6144].rearrange("p (t h n) -> p t h n", t=2, h=2)
        o_sb = region[:, 1, 0:2048].rearrange("p (k n) -> p k n", k=TILES)
        sel_in = region[:, 1, 2048:2048 + 11 * P]
        mask_row = sT[0:1, :, :, :].rearrange("p s t n -> p (s t n)").bitcast(I32)
        amat = sb("amat", [P, RET_HEADS, 4 * P])
        aneg = silu[:, :, 0:3 * P]
        qhi = sb("qhi", [P, 2, HALVES, SEQ], F32R)
        qlo = sb("qlo", [P, 2, HALVES, SEQ], F32R)
        khl = sb("khl", [P, 2, SEQ], F32R)
        qst = sb("qst", [P, 2, HALVES, PER_GROUP, SEQ], F32R)
        with ExitStack() as early:
            def brief(name, shape):
                return early.enter_context(nc.sbuf_tensor(name, shape, F32))
            wh = brief("wh", [P, RET_HEADS, RET_HD])
            decay = brief("decay", [P, RET_HEADS, 3 * P])
            wg = brief("wg", [P, KT, DIM])
            wo0 = brief("wo0", [P, KT, DIM])
            e_down2 = brief("e_down2", [EXPERT_R, EXPERTS, DIM])
        kblk_all = sb("kblk", [P, 2, HALVES, QUADS, SEQ], F32R)
        kblk = [[kblk_all[:, s, q, :, :] for q in range(HALVES)] for s in range(2)]
        avT = (prod, amat[:, :, :])
        cmps = ctxT[:, :, :].rearrange("p t n -> p (t n)").bitcast(BF16).rearrange("p (c n) -> p c n", n=UNIT)
        cmp1, cmp2, cmp3 = cmps[:, 0:3, :], cmps[:, 3:5, :], cmps[:, 5, :]
        wins = amat[:, :, :].rearrange("p h n -> p (h n)").bitcast(BF16).rearrange("p (c n) -> p c n", n=UNIT)

        x_sorted = nc.dram_tensor("x_sorted", (SLOTS * P, DIM), F32, kind="Internal").ap()
        y_sorted = nc.dram_tensor("y_sorted", (SLOTS * P, DIM), F32, kind="Internal").ap()

        banks = [ctx.enter_context(nc.psum_tensor(f"bank{i}", [P, UNIT], F32)) for i in range(8)]
        KINDS = {"main": (0, 1, 2, 3), "turn": (4, 5), "tok": (6, 7),
                 "max": (0, 1, 2), "exp": (3, 4, 5), "wide": (0, 1, 2, 3, 4, 5),
                 "turn1": (6,), "tok1": (7,), "last": (6, 7)}
        fills, occupant, turns = {}, {}, {}

        def acquire(pe, stage, i, kind):
            n = turns.get(kind, 0)
            turns[kind] = n + 1
            bank = KINDS[kind][n % len(KINDS[kind])]
            if bank in occupant:
                before, m = occupant[bank]
                pe.wait_ge(sem(before + "_taken"), m + 1)
            occupant[bank] = (stage, i)
            fills[stage, i] = banks[bank][:, :]
            return fills[stage, i]

        def filled(eng, stage, i):
            eng.wait_ge(sem(stage + "_ready"), i + 1)
            return fills[stage, i]

        def ready(ins, stage):
            ins.then_inc(sem(stage + "_ready"), 1)

        def taken(ins, stage):
            ins.then_inc(sem(stage + "_taken"), 1)

        def score_fill(n):
            q, c = divmod(n, 12)
            return (q, c, 0, slice(0, 4)) if c < 4 else (q, (c - 4) // 2, 1, slice(c % 2 * 2, c % 2 * 2 + 2))

        def weight_fill(n):
            q, c = divmod(n, 12)
            return (q, c // 2, 0, slice(c % 2 * 2, c % 2 * 2 + 2)) if c < 8 else (q, c - 8, 1, slice(0, 4))

        def tile_cols(k):
            return slice(k * P, (k + 1) * P)

        def load(eng, name, dst, src):
            eng.dma_start(dst, src).then_inc(sem("in_" + name), 16)

        def loaded(eng, name, n=1):
            eng.wait_ge(sem("in_" + name), 16 * n)

        block = ctx.enter_context(nc.Block())

        @block.tensor
        def _(pe):
            def mm(dst, lhsT, rhs, first, last):
                return pe.matmul(dst, lhsT, rhs, start=first, stop=last)

            def ln_turn(layer, k, kind="turn"):
                dst = acquire(pe, f"ln{layer}", k, kind)
                pe.wait_ge(sem(f"xn{layer}"), k + 1)
                src = xn1[:, HALF_ORDER[k], :] if layer == 1 else xn[:, k % 2, :]
                for t in range(KT):
                    ins = pe.transpose(dst[:, tile_cols(t)], src[:, tile_cols(t)], ident[:, :])
                ready(ins, f"ln{layer}")

            def turn_pair(stage, i, src, kind):
                dst = acquire(pe, stage, i, kind)
                for t in range(KT):
                    ins = pe.transpose(dst[:, tile_cols(t)], src[:, tile_cols(t)], ident[:, :])
                ready(ins, stage)

            loaded(pe, "wh")
            for i in range(4):
                u, h = divmod(i, RET_HEADS)
                if h == 0:
                    loaded(pe, f"ctx{u}")
                dst = acquire(pe, "rk", i, "main")
                ready(mm(dst, wh[:, h, :], ctxT[:, h, u * UNIT:(u + 1) * UNIT], True, True), "rk")
            loaded(pe, "ident")
            for k in range(TILES):
                ln_turn(0, k)
            for i in range(4):
                h, u = divmod(i, UNITS)
                dst = acquire(pe, "rq", i, "main")
                pe.wait_ge(sem("ln0_taken"), UNIT_TILES * (u + 1))
                ready(mm(dst, wh[:, h, :], xT[:, h, u * UNIT:(u + 1) * UNIT], True, True), "rq")
            pe.wait_ge(sem("rk_taken"), 4)
            for h in range(RET_HEADS):
                dst = acquire(pe, "rs", h, "main")
                pe.wait_ge(sem("rq_taken"), 2 * h + 2)
                for t in range(2):
                    for b in range(BATCH):
                        at = b * SEQ + t * P
                        ins = mm(dst[:, 2 * P * t:2 * P * t + SEQ - t * P], kT0[:, h, at:at + P],
                                 qT0[:, h, at:(b + 1) * SEQ], b == 0, b == BATCH - 1)
                ready(ins, "rs")
            for k in range(TILES):
                dst = acquire(pe, "rv", k, "main")
                for h in range(RET_HEADS):
                    ins = mm(dst[:, h * P:(h + 1) * P], ctxT[:, h, tile_cols(k)], wh[:, h, :], True, True)
                ready(ins, "rv")
            loaded(pe, "wg")
            pe.wait_ge(sem("rv_taken"), TILES)

            def gate(k):
                dst = acquire(pe, "rg", k, "main")
                for t in range(KT):
                    ins = mm(dst[:, 0:DIM], xT[:, t, tile_cols(HALF_ORDER[k])], wg[:, t, :], t == 0, t == KT - 1)
                ready(ins, "rg")

            for i in range(4):
                st, h = divmod(i, 2)
                if i == 2:
                    gate(0)
                dst = acquire(pe, "ro", i, "main")
                pe.wait_ge(sem("a_made"), 2 * h + 2)
                for t in range(2):
                    ins = mm(dst, amat[:, h, t * SEQ + st * P:t * SEQ + st * P + P], v0[:, t, h, :], t == 0, t == 1)
                ready(ins, "ro")

            def project(k):
                dst = acquire(pe, "res0", k, "tok")[:, 0:DIM]
                pe.wait_ge(sem("wyT_taken"), k + 1)
                for t in range(KT):
                    ins = mm(dst, actT[:, k % 2, t, :], wo0[:, t, :], t == 0, t == KT - 1)
                ready(ins, "res0")

            def logits(k):
                dst = acquire(pe, "log", 0, "main") if k == 0 else fills["log", 0]
                cols = slice(HALF_ORDER[k] * EXPERTS, (HALF_ORDER[k] + 1) * EXPERTS)
                pe.wait_ge(sem("ln1_taken"), k + 1)
                for t in range(KT):
                    ins = mm(dst[:, cols], xT[:, t, tile_cols(HALF_ORDER[k])], router[:, t, :], t == 0, t == KT - 1)
                if k == TILES - 1:
                    ready(ins, "log")

            gate(1)
            loaded(pe, "wo0")
            loaded(pe, "router")
            for k in range(TILES + 4):
                if k < TILES:
                    pe.wait_ge(sem("rg_taken"), k + 1)
                    turn_pair("wyT", k, att[:, k % 2, :], "turn")
                if 1 <= k <= TILES:
                    project(k - 1)
                if k + 2 < TILES:
                    gate(k + 2)
                if 3 <= k < TILES + 3:
                    ln_turn(1, k - 3)
                if k >= 4:
                    logits(k - 4)

            pe.wait_ge(sem("onehot_made"), 1)
            loaded(pe, "tri")
            dst = acquire(pe, "rank", 0, "main")[:, 0:(TILES + 1) * EXPERTS].rearrange("p (k e) -> p k e", e=EXPERTS)
            pe.matmul(dst[:, 0:TILES, :], tri[:, 0, :], onehot16[:, :, :], start=True, stop=False, skip_group_check=True)
            for k in range(TILES):
                later = TILES - k
                ins = pe.matmul(dst[:, k + 1:TILES + 1, :], tri[:, 1, :],
                                onehot16[:, k, :].unsqueeze(1).to_broadcast([P, later, EXPERTS]),
                                start=False, stop=(k == TILES - 1), skip_group_check=True)
            ready(ins, "rank")

            def queries(b, n):
                if n in (QUERIES_AT, QUERIES_AT + 2):
                    ln_turn(2, 2 * b + (n - QUERIES_AT) // 2, "turn1")
                if n != QUERIES_AT + 4:
                    return
                seq = slice(b * SEQ, (b + 1) * SEQ)
                dst = acquire(pe, "qp", b, "tok1")
                pe.wait_ge(sem("ln2_taken"), 2 * b + 2)
                for q in range(HALVES):
                    for t in range(KT):
                        ins = mm(dst[:, q * SEQ:(q + 1) * SEQ], wq[:, t, tile_cols(q)], xT[:, t, seq], t == 0, t == KT - 1)
                ready(ins, "qp")

            def query_stack(b, one):
                s = b % 2
                pe.wait_ge(sem("qp_taken"), b + 1)
                for q in range(HALVES):
                    for h in range(2):
                        dst = acquire(pe, "qs", 4 * b + 2 * q + h, one)
                        for e in range(2):
                            hg = 2 * h + e
                            mm(dst[:, e * SEQ:(e + 1) * SEQ], selr[:, hg * P:(hg + 1) * P], qhi[:, s, q, :], True, False)
                            ins = mm(dst[:, e * SEQ:(e + 1) * SEQ], selr[:, (4 + hg) * P:(5 + hg) * P], qlo[:, s, q, :], False, True)
                        ready(ins, "qs")

            def keys(b, one):
                s = b % 2
                seq = slice(b * SEQ, (b + 1) * SEQ)
                dst = acquire(pe, "kp", b, one)
                if b == 0:
                    loaded(pe, "w1", 4)
                for t in range(KT):
                    ins = mm(dst[:, 0:SEQ], wk[:, t, :], ctxT[:, t, seq], t == 0, t == KT - 1)
                ready(ins, "kp")
                dst = acquire(pe, "vp", b, one)
                for r in range(2):
                    for t in range(KT):
                        w = GROUPS * HD
                        ins = mm(dst[:, r * w:(r + 1) * w], ctxT[:, t, tile_cols(2 * b + r)], wv[:, t, :], t == 0, t == KT - 1)
                ready(ins, "vp")
                if b == 0:
                    pe.wait_ge(sem("sel_made"), 2)
                    pe.wait_ge(sem("padrow_made"), 1)
                pe.wait_ge(sem("kp_taken"), b + 1)
                for q in range(HALVES):
                    dst = acquire(pe, f"ks{q}", b, one)
                    mm(dst[:, 0:SEQ], selr[:, (8 + q) * P:(9 + q) * P], khl[:, s, :], True, False)
                    ready(mm(dst[:, 0:SEQ], padselr[:, :], padrow[:, seq], False, True), f"ks{q}")

            def scores(b, n):
                s = b % 2
                q, hg, nt, quads = score_fill(n)
                if n % 12 == 0:
                    pe.wait_ge(sem(f"ks{q}_taken"), b + 1)
                    pe.wait_ge(sem("qs_taken"), 4 * b + 2 + 2 * q)
                if n == 0:
                    if b == 0:
                        loaded(pe, "caus", 2)
                dst = acquire(pe, "sa", 24 * b + n, "max").rearrange("p (j m) -> p j m", m=(nt + 1) * P)
                pe.matmul(dst, qst[:, s, q, hg, tile_cols(nt)], kblk[s][q][:, quads, 0:(nt + 1) * P],
                          start=True, stop=False, skip_group_check=True)
                diagonal = dst[:, :, nt * P:(nt + 1) * P]
                ready(pe.matmul(diagonal, identb[:, :], causb[:, 0:diagonal.shape[1], :], start=False, stop=True,
                                skip_group_check=True), "sa")

            def neg_turn(b, kind):
                s = b % 2
                for nt in range(2):
                    dst = acquire(pe, "nmT", 2 * b + nt, kind)
                    pe.wait_ge(sem("nm_made"), 2 * b + nt + 1)
                    ready(pe.transpose(dst[0:2 * HEADS, 0:P], nmx[:, s, nt, :].bitcast(F32), ident[:, :]), "nmT")

            def weights(b, n):
                s = b % 2
                q, j, mt, heads = weight_fill(n)
                if n == 0:
                    pe.wait_ge(sem("max_rows"), 16 * 2 * (b + 1))
                dst = acquire(pe, "sb", 24 * b + n, "exp")
                ready(mm(dst, kblk[s][q][:, j, tile_cols(mt)], qst[:, s, q, heads, mt * P:SEQ], True, True), "sb")

            def values(b, i):
                q, nt = divmod(i, 2)
                if nt == 0:
                    pe.wait_ge(sem("causal_done"), 8 * b + 4 * q + 4)
                dst = acquire(pe, "av", 4 * b + i, "wide")
                pe.wait_ge(sem("vp_taken"), b + 1)
                for mt in range(nt + 1):
                    for j in range(QUADS):
                        rhs = pt0[q][:, j, :, tile_cols(nt)] if mt == 0 else pt1[q][:, j, :, :]
                        ins = pe.matmul(dst[32 * j:32 * j + 32, :], vaug[:, 2 * b + mt, 4 * q + j, :], rhs,
                                        start=(mt == 0), stop=(mt == nt), skip_group_check=True)
                ready(ins, "av")

            def finish(b, n):
                nt, c = divmod(n, 6)
                i = 2 * b + nt
                if c < PER_GROUP:
                    f = 4 * i + c
                    dst = acquire(pe, "avT", f, "turn1")
                    if c == 0:
                        pe.wait_ge(sem("av_taken"), 4 * b + 2 + nt + 1)
                    for q in range(HALVES):
                        ins = pe.transpose(dst[:, tile_cols(q)], avT[nt][:, q, c * P:(c + 1) * P], ident[:, :])
                    ready(ins, "avT")
                elif c == PER_GROUP:
                    pe.wait_ge(sem("avT_taken"), 4 * i + 4)
                    turn_pair("atT", i, att[:, i % 2, :], "turn1")
                else:
                    dst = acquire(pe, "res2", i, "tok1")[:, 0:DIM]
                    pe.wait_ge(sem("atT_taken"), i + 1)
                    for t in range(KT):
                        ins = mm(dst, actT[:, i % 2, t, :], wo1[:, t, :], t == 0, t == KT - 1)
                    ready(ins, "res2")

            keys(0, "main")

            def slot_turn(i):
                if i in SORTED_LOADS:
                    pe.wait_ge(sem(f"sorted_loaded{SORTED_LOADS.index(i)}"), 16)
                turn_pair("sx", i, sorted_x[:, i, :], "turn")

            def slot_gate_up(i):
                expert = pe.value_load(slot_expert[0:1, i:i + 1], min_val=0, max_val=EXPERTS - 1)
                dst = acquire(pe, "sg", i, "main")[:, 0:2 * EXPERT_I]
                pe.wait_ge(sem("sx_taken"), i + 1)
                for t in range(KT):
                    ins = mm(dst, sT[:, i % 2, t, :], e_gu[:, t, bass.ds(expert, 1), :].rearrange("p e n -> p (e n)"),
                             t == 0, t == KT - 1)
                ready(ins, "sg")
                return expert

            def slot_act_turn(i):
                dst = acquire(pe, "sa_t", i, "turn")
                pe.wait_ge(sem("sg_taken"), i + 1)
                pe.transpose(dst[:, 0:P], sact[:, i % 2, 0:P], ident[:, :])
                ready(pe.transpose(dst[0:EXPERT_R, P:2 * P], sact[:, i % 2, P:EXPERT_I], ident[:, :]), "sa_t")

            def slot_down(i, expert):
                dst = acquire(pe, "sy", i, "tok")[:, 0:DIM]
                pe.wait_ge(sem("sa_t_taken"), i + 1)
                one = bass.ds(expert, 1)
                mm(dst, sT[:, 2 + i % 2, 0, :], e_down[:, one, :].rearrange("p e n -> p (e n)"), True, False)
                ready(mm(dst, sT[0:EXPERT_R, 2 + i % 2, 1, :], e_down2[:, one, :].rearrange("p e n -> p (e n)"), False, True), "sy")

            pe.wait_ge(sem("slots_made"), 1)
            loaded(pe, "e", 4)
            slot_turn(0)
            slot_turn(1)
            expert = [slot_gate_up(0)]
            for i in range(SLOTS + 1):
                if i + 2 < SLOTS:
                    slot_turn(i + 2)
                if i + 1 < SLOTS:
                    expert.append(slot_gate_up(i + 1))
                if i >= 1:
                    slot_down(i - 1, expert[i - 1])
                if i < SLOTS:
                    slot_act_turn(i)

            keys(1, "main")
            for n in range(QUERIES_AT, QUERIES_AT + 6, 2):
                queries(0, n)
            query_stack(0, "main")
            for n in range(24):
                scores(0, n)
                queries(1, n)
            query_stack(1, "exp")
            neg_turn(0, "turn1")
            for n in range(LEAD):
                scores(1, n)
            for b in range(BATCH):
                for n in range(24):
                    if b + 1 < BATCH and n + LEAD < 24:
                        scores(b + 1, n + LEAD)
                    weights(b, n)
                    if b >= 1 and n % 2 == 1:
                        finish(b - 1, n // 2)
                    if b + 2 < BATCH:
                        queries(b + 2, n)
                    if b == BATCH - 1 and n in NORM_STEPS:
                        ln_turn(3, NORM_STEPS.index(n), "tok1")
                    if n == NEGATE_AT and b + 1 < BATCH:
                        neg_turn(b + 1, "turn1")
                if b + 2 < BATCH:
                    keys(b + 2, "wide")
                    query_stack(b + 2, "wide")
                for i in range(4):
                    values(b, i)
                    for n in range(i * LEAD // 4, (i + 1) * LEAD // 4):
                        if b + 2 < BATCH:
                            scores(b + 2, n)

            def gate_up(g, j):
                u, blk = divmod(g, FFN_BLOCKS)
                us = slice(u * UNIT, (u + 1) * UNIT)
                c = j * 2 * P + blk * P
                for stage, w in (("fg", f_gate), ("fu", f_up)):
                    dst = acquire(pe, stage, 4 * g + j, "wide")
                    for t in range(KT):
                        ins = mm(dst, w[:, t, c:c + P], xT[:, t, us], t == 0, t == KT - 1)
                    ready(ins, stage)

            def down(k, kind):
                u, c = k // UNIT_TILES, (k % UNIT_TILES) * P
                dst = acquire(pe, "res3", k, kind)[:, 0:DIM]
                for m in range(FFN_MT):
                    ins = mm(dst, hs[u][:, m, c:c + P], f_down[:, m, :], m == 0, m == FFN_MT - 1)
                ready(ins, "res3")

            pe.wait_ge(sem("ln3_taken"), UNIT_TILES)
            loaded(pe, "f", 3)
            for n in range(8):
                gate_up(n // 4, n % 4)
                for c in range(2 * n, min(2 * n + 2, 12)):
                    finish(BATCH - 1, c)
                if n in LATE_NORM_STEPS:
                    ln_turn(3, UNIT_TILES + LATE_NORM_STEPS.index(n), "turn1")
            pe.wait_ge(sem("ln3_taken"), TILES)
            for j in range(4):
                gate_up(2, j)
            for j in range(4):
                gate_up(3, j)
            pe.wait_ge(sem("hs_made"), 8)
            for k in range(UNIT_TILES):
                down(k, "last")
            pe.wait_ge(sem("hs_made"), 16)
            for k in range(UNIT_TILES, TILES):
                down(k, "wide")


        @block.sync
        def _(sp):
            for k in range(0, TILES, 2):
                load(sp, f"x{k}", x_sb[:, k:k + 2, :], a["x"][k:k + 2].rearrange("k p n -> p k n"))
                if k == 0:
                    load(sp, "wh", wh[:, :, :], a["wh"])
                    for u in range(UNITS):
                        us = slice(u * UNIT, (u + 1) * UNIT)
                        load(sp, f"ctx{u}", ctxT[:, :, us], a["ctxT"][:, :, us])
                    load(sp, "ident", ident[:, :], a["ident"])
            load(sp, "gates", gates[:, 0:2], a["g_x"])
            load(sp, "gates", gates[:, 2:4], a["g_f"])
            load(sp, "decay", decay[:, :, :], a["decay"])
            load(sp, "wg", wg[:, :, :], a["wg"])
            load(sp, "gamma", gamma[:, :], a["gamma"])
            load(sp, "gamma", beta[:, :], a["beta"])
            load(sp, "wo0", wo0[:, :, :], a["wo0"])
            load(sp, "router", router[:, :, :], a["router"])
            load(sp, "small", small_c[:, :], a["small"])
            load(sp, "sel", sel_in, a["sel"])
            load(sp, "caus", causb[:, :, :].rearrange("p h n -> p (h n)"), a["caus"])
            load(sp, "caus", identb[:, :], a["identb"])
            load(sp, "sel", mask_row, a["mask_row"])
            load(sp, "sel", mask_col[:, :], a["mask_col"])
            load(sp, "tri", tri[:, :, :], a["tri"])
            sp.wait_ge(sem("zero_set"), 1)
            sp.dma_start(x_sorted.rearrange("(s p) n -> p s n", p=P),
                         zero[:, :].unsqueeze(1).to_broadcast([P, SLOTS, DIM])).then_inc(sem("sorted_zeroed"), 16)
            for t in range(KT):
                load(sp, "e", e_gu[:, t, :, :], a["e_gu"][:, t, :, :])
            load(sp, "e", e_down[:, :, :], a["e_down"])
            load(sp, "e", e_down2[:, :, :], a["e_down2"])
            load(sp, "w1", wq[:, :, :], a["wq"])
            load(sp, "w1", wk[:, :, :], a["wk"])
            load(sp, "w1", wv[:, :, :], a["wv"])
            load(sp, "w1", wo1[:, :, :], a["wo1"])
            sp.wait_ge(sem("gn_y"), TILES)
            load(sp, "bo", bo[:, :], a["bo"])
            sp.wait_ge(sem("tokens_sorted"), 16 * TILES)
            for n, first in enumerate(SORTED_LOADS):
                end = (SORTED_LOADS + (SLOTS,))[n + 1]
                sp.dma_start(sorted_x[:, first:end, :],
                             x_sorted[first * P:end * P, :].rearrange("(s p) n -> p s n", p=P))\
                  .then_inc(sem(f"sorted_loaded{n}"), 16)
            for i in range(SLOTS):
                sp.wait_ge(sem("sy_taken"), i + 1)
                sp.dma_start(y_sorted[i * P:(i + 1) * P, :], sorted_y[:, i, :]).then_inc(sem("y_stored"), 16)
            sp.wait_ge(sem("y_back3"), 32)
            load(sp, "f", f_gate, a["f_gate"])
            load(sp, "f", f_up, a["f_up"])
            load(sp, "f", f_down, a["f_down"])
            for b in range(BATCH):
                sp.wait_ge(sem("nmT_taken"), 2 * b + 2)
                for piece in range(2):
                    rows = slice(piece * HEADS, (piece + 1) * HEADS)
                    dst = qst[24 + piece:P:32, b % 2, :, :, :]
                    sp.dma_start(dst.rearrange("p q h n -> p (q h) n").bitcast(F32),
                                 nmT[rows, b % 2, :].bitcast(F32))\
                      .then_inc(sem("max_rows"), 16)
            for k in range(TILES):
                sp.wait_ge(sem("res3_taken"), k + 1)
                sp.dma_start(out[k], x_sb[:, k, :]).then_inc(sem("stored"), 16)
            sp.wait_ge(sem("stored"), 16 * TILES)

        @block.gpsimd
        def _(pool):
            pool.memset(zero[:, :], 0.0).then_inc(sem("zero_set"), 1)
            pool.memset(power[:, :], -0.5).then_inc(sem("power_set"), 1)
            pool.memset(vaug[:, :, :, :], 1.0).then_inc(sem("ones_set"), 1)
            pool.memset(amat[:, :, :], 1.0).then_inc(sem("a_set"), 1)
            pool.wait_ge(sem("power_set"), 1)

            chain = [0]

            def inverse_std(layer, k, eps):
                pool.wait_ge(sem(f"mv{layer}"), k + 1)
                pool.tensor_scalar(veps[:, layer, k:k + 1], mv[:, layer, k, 1:2], eps, None, ALU.add)\
                    .then_inc(sem("veps"), 1)
                chain[0] += 1
                pool.wait_ge(sem("veps"), chain[0])
                pool.tensor_tensor(out=rstd[:, layer, k:k + 1], in0=veps[:, layer, k:k + 1],
                                   in1=power[:, :], op=ALU.pow).then_inc(sem(f"rstd{layer}"), 1)

            for k in range(TILES):
                inverse_std(0, k, LN_EPS)
            for k in range(TILES + 3):
                if k < TILES:
                    inverse_std(4, k, GN_EPS)
                if k >= 3:
                    inverse_std(1, k - 3, LN_EPS)

            def clear_blocks(s):
                for q in range(HALVES):
                    pool.memset(kblk[s][q].bitcast(F32), 0.0).then_inc(sem("blocks_clear"), 1)

            pool.wait_ge(sem("res0_ready"), TILES)
            pool.wait_ge(sem("rs_taken"), RET_HEADS)
            clear_blocks(0)
            pool.wait_ge(sem("blocks_clear"), HALVES)
            pool.wait_ge(sem("placed"), 1)
            pool.wait_ge(sem("sorted_zeroed"), 16)
            for k in range(TILES):
                pool.indirect_dma_start(x_sorted, bass.IndirectOffsetOnAxis(ap=place[:, k:k + 1], axis=0),
                                        xn1[:, k, :], None).then_inc(sem("tokens_sorted"), 16)
            pool.wait_ge(sem("tokens_sorted"), 16 * TILES)

            pool.wait_ge(sem("sy_ready"), SLOTS)
            clear_blocks(1)
            pool.wait_ge(sem("y_stored"), 16 * SLOTS)
            for k in range(TILES):
                pool.indirect_dma_start(own_y[:, k, :], None, y_sorted,
                                        bass.IndirectOffsetOnAxis(ap=place[:, k:k + 1], axis=0))\
                    .then_inc(sem(f"y_back{k // 2}"), 16)
                if k == 1:
                    pool.wait_ge(sem("y_back0"), 32)
                    for t in range(2):
                        inverse_std(2, t, LN_EPS)
            for n in range(1, TILES // 2):
                pool.wait_ge(sem(f"y_back{n}"), 32)

            def add_bias(k):
                pool.wait_ge(sem("bo_made"), 1)
                pool.wait_ge(sem("xn2"), k + 1)
                pool.tensor_tensor(out=x_sb[:, k, :], in0=x_sb[:, k, :], in1=bo_t[:, :], op=ALU.add)\
                    .then_inc(sem("bias_added"), 1)

            for k in range(2, TILES):
                inverse_std(2, k, LN_EPS)
            for k in range(4):
                add_bias(k)
            for b in range(BATCH):
                for q in range(HALVES):
                    for n in range(4):
                        js = slice(n % 2 * 2, n % 2 * 2 + 2)
                        pool.wait_ge(sem("sb_taken"), 24 * b + 12 * q + (4, 8, 10, 12)[n])
                        block = pt0[q][:, js, :, 0:P] if n < 2 else pt1[q][:, js, :, :]
                        pool.affine_select(out=block, in_=block, compare_op=ALU.is_ge, fill=0.0, base=0,
                                           pattern=[[0, 2], [0, PER_GROUP], [1, P]], channel_multiplier=-1)\
                            .then_inc(sem("causal_done"), 1)
                if b + 2 < BATCH:
                    for k in (2 * b + 4, 2 * b + 5):
                        add_bias(k)
                if b >= 1:
                    for k in (2 * b - 2, 2 * b - 1):
                        inverse_std(3, k, LN_EPS)
            for k in (TILES - 2, TILES - 1):
                inverse_std(3, k, LN_EPS)

        @block.scalar
        def _(act):
            def ln_turn(layer, k):
                src = filled(act, f"ln{layer}", k)
                tile = HALF_ORDER[k] if layer == 1 else k
                taken(act.activation(xT[:, :, tile_cols(tile)], src[:, 0:DIM].rearrange("p (t n) -> p t n", t=KT), ACT.Copy),
                      f"ln{layer}")

            for i in range(4):
                u, h = divmod(i, RET_HEADS)
                taken(act.activation(kT0[:, h, u * UNIT:(u + 1) * UNIT], filled(act, "rk", i), ACT.Copy), "rk")
            for k in range(TILES):
                ln_turn(0, k)
            for i in range(4):
                h, u = divmod(i, UNITS)
                taken(act.activation(qT0[:, h, u * UNIT:(u + 1) * UNIT], filled(act, "rq", i), ACT.Copy), "rq")
            loaded(act, "gates", 2)
            act.activation(tg[:, :], gates[:, :], ACT.Tanh).then_inc(sem("tanh"), 1)
            for k in range(TILES):
                b, t = divmod(k, 2)
                src = filled(act, "rv", k)[:, 0:256].rearrange("p (h n) -> p h n", h=2)
                taken(act.activation(v0[:, t, :, b * P:(b + 1) * P], src, ACT.Copy), "rv")
            for i in range(4):
                st, h = divmod(i, 2)
                dst = o_sb[:, st:TILES:2, h * P:(h + 1) * P]
                taken(act.activation(dst, filled(act, "ro", i).rearrange("p (b e) -> p b e", b=BATCH), ACT.Copy), "ro")
            loaded(act, "sel", 3)
            act.activation(selr[:, :], sel_in[:, 0:10 * P], ACT.Copy).then_inc(sem("sel_made"), 1)
            act.activation(padselr[:, :], sel_in[0:1, 10 * P:11 * P], ACT.Copy).then_inc(sem("sel_made"), 1)
            for k in range(TILES + 3):
                if k < TILES:
                    src = filled(act, "wyT", k)
                    if k >= 2:
                        act.wait_ge(sem("res0_ready"), k - 1)
                    taken(act.activation(actT[:, k % 2, :, :], src[:, 0:DIM].rearrange("p (t n) -> p t n", t=KT),
                                         ACT.Copy), "wyT")
                if k >= 3:
                    ln_turn(1, k - 3)

            act.wait_ge(sem("vdiff"), 1)
            act.activation(r_s[:, 3, :], r_s[:, 2, :], ACT.Exp).then_inc(sem("vexp"), 1)

            def keys(b):
                s = b % 2
                src = filled(act, "kp", b)
                if b >= 2:
                    act.wait_ge(sem("ks1_ready"), b - 1)
                act.activation(khl[:, s, :], src[:, 0:SEQ], ACT.Copy).then_inc(sem("k_high"), 1)
                src = filled(act, "vp", b)[:, 0:2 * GROUPS * HD].rearrange("p (k g d) -> p k g d", k=2, g=GROUPS)
                if b == 0:
                    act.wait_ge(sem("ones_set"), 1)
                for t in range(2):
                    ins = act.activation(vaug[:, 2 * b + t, :, 0:HD], src[:, t, :, :], ACT.Copy)
                taken(ins, "vp")
                if b < 2:
                    act.wait_ge(sem("blocks_clear"), HALVES * (b + 1))
                src = filled(act, "ks0", b)
                for j in range(QUADS):
                    rows = slice(32 * j, 32 * j + 32)
                    ins = act.activation(kblk[s][0][rows, j, :], src[rows, 0:SEQ], ACT.Identity, bias=small_c[rows, 1:2])
                taken(ins, "ks0")

            def queries(b, n):
                if n in (QUERIES_AT, QUERIES_AT + 2):
                    ln_turn(2, 2 * b + (n - QUERIES_AT) // 2)
                if n != QUERIES_AT + 4:
                    return
                s = b % 2
                src = filled(act, "qp", b).rearrange("p (q n) -> p q n", q=HALVES)
                if b >= 2:
                    act.wait_ge(sem("qs_ready"), 4 * b - 4)
                act.activation(qhi[:, s, :, :], src, ACT.Copy).then_inc(sem("q_high"), 1)

            def query_stack(b):
                s = b % 2
                for q in range(HALVES):
                    for h in range(2):
                        src = filled(act, "qs", 4 * b + 2 * q + h).rearrange("p (h n) -> p h n", h=2)
                        if b >= 2:
                            act.wait_ge(sem("sb_ready"), 24 * (b - 1))
                        taken(act.activation(qst[:, s, q, 2 * h:2 * h + 2, :], src, ACT.Identity,
                                             bias=small_c[:, 0:1]), "qs")

            keys(0)
            def slot_turn(i):
                src = filled(act, "sx", i)[:, 0:DIM].rearrange("p (t n) -> p t n", t=KT)
                if i >= 2:
                    act.wait_ge(sem("sg_ready"), i - 1)
                taken(act.activation(sT[:, i % 2, :, :], src, ACT.Copy), "sx")

            def slot_silu(i):
                src = filled(act, "sg", i)[:, 0:EXPERT_I]
                if i >= 2:
                    act.wait_ge(sem("sg_taken"), i - 1)
                act.activation(silu[:, i % 2, 0:EXPERT_I], src, ACT.Silu).then_inc(sem("silu_made"), 1)

            act.wait_ge(sem("padrow_made"), 1)
            slot_turn(0)
            slot_turn(1)
            slot_silu(0)
            for i in range(SLOTS):
                if i + 2 < SLOTS:
                    slot_turn(i + 2)
                if i + 1 < SLOTS:
                    slot_silu(i + 1)
                src = filled(act, "sa_t", i)
                if i >= 2:
                    act.wait_ge(sem("sy_ready"), i - 1)
                act.activation(sT[:, 2 + i % 2, 0, :], src[:, 0:P], ACT.Copy)
                taken(act.activation(sT[0:EXPERT_R, 2 + i % 2, 1, :], src[0:EXPERT_R, P:2 * P], ACT.Copy), "sa_t")

            def neg_turn(b):
                if b >= 2:
                    act.wait_ge(sem("max_rows"), 16 * 2 * (b - 1))
                for nt in range(2):
                    src = filled(act, "nmT", 2 * b + nt)[0:2 * HEADS, 0:P]
                    taken(act.activation(nmT[:, b % 2, tile_cols(nt)], src, ACT.Copy), "nmT")

            def exponentials(b, n):
                q, j, mt, heads = weight_fill(n)
                src = filled(act, "sb", 24 * b + n)
                if n == 0 and b == 0:
                    act.wait_ge(sem("padcol_made"), 1)
                    act.wait_ge(sem("x2"), TILES)
                if n % 12 == 0 and b >= 1:
                    act.wait_ge(sem("av_ready"), 4 * b - 2 + n // 6)
                dst = pt0[q][:, j, heads, :] if mt == 0 else pt1[q][:, j, :, :]
                key = 2 * b + mt
                taken(act.activation(dst, src.rearrange("p (h n) -> p h n", n=SEQ - mt * P), ACT.Exp,
                                     bias=padcol[:, key:key + 1], scale=float(HD) ** -0.5), "sb")

            def value_turn(b):
                for q in range(HALVES):
                    for nt in range(2):
                        src = filled(act, "av", 4 * b + 2 * q + nt)
                        if b >= 1:
                            act.wait_ge(sem("avT_ready"), 8 * (b - 1) + 4 * nt + 4)
                        taken(act.activation(avT[nt][:, q, :], src, ACT.Copy), "av")

            def finish(b, n):
                nt, c = divmod(n, 6)
                i = 2 * b + nt
                if c == PER_GROUP:
                    src = filled(act, "atT", i)[:, 0:DIM]
                    if i >= 2:
                        act.wait_ge(sem("res2_ready"), i - 1)
                    taken(act.activation(actT[:, i % 2, :, :], src.rearrange("p (t n) -> p t n", t=KT), ACT.Copy), "atT")

            keys(1)
            for n in range(QUERIES_AT, QUERIES_AT + 6, 2):
                queries(0, n)
            query_stack(0)
            for n in range(24):
                queries(1, n)
            query_stack(1)
            neg_turn(0)
            for b in range(BATCH):
                for n in range(24):
                    exponentials(b, n)
                    if b >= 1 and n % 2 == 1:
                        finish(b - 1, n // 2)
                    if b + 2 < BATCH:
                        queries(b + 2, n)
                    if b == BATCH - 1 and n in NORM_STEPS:
                        ln_turn(3, NORM_STEPS.index(n))
                    if n == NEGATE_AT and b + 1 < BATCH:
                        neg_turn(b + 1)
                if b + 2 < BATCH:
                    keys(b + 2)
                    query_stack(b + 2)
                value_turn(b)

            def magnitude(i):
                g, j = divmod(i, 4)
                act.wait_ge(sem("fu_taken"), i + 1)
                if g >= 2 and j == 0:
                    act.wait_ge(sem("compared"), 3 * (g - 1))
                u, blk = divmod(g, FFN_BLOCKS)
                act.activation(absh[g % 2][:, j, :], hs[u][:, 4 * blk + j, :], ACT.Abs).then_inc(sem("abs_made"), 1)

            for i in range(4 * FFN_BLOCKS * UNITS):
                src = filled(act, "fg", i)
                if i >= 2:
                    act.wait_ge(sem("fu_taken"), i - 1)
                taken(act.activation(silu[:, i % 2, :], src, ACT.Silu), "fg")
                for c in range(2 * i, min(2 * i + 2, 12)):
                    finish(BATCH - 1, c)
                if i in LATE_NORM_STEPS:
                    ln_turn(3, UNIT_TILES + LATE_NORM_STEPS.index(i))
                if i >= 1:
                    magnitude(i - 1)
            magnitude(4 * FFN_BLOCKS * UNITS - 1)

        @block.vector
        def _(dve):
            stats_done = [0]

            def stat(layer, k, src):
                stats_done[0] += 1
                dve.bn_stats(stats[:, layer, k, :], src).then_inc(sem("stats"), 1)
                dve.wait_ge(sem("stats"), stats_done[0])
                dve.bn_aggr(mv[:, layer, k, :], stats[:, layer, k, :]).then_inc(sem(f"mv{layer}"), 1)

            def norm(layer, k):
                dve.wait_ge(sem(f"rstd{layer}"), k + 1)
                if k >= 2:
                    dve.wait_ge(sem(f"ln{layer}_ready"), k - 1)
                elif layer:
                    dve.wait_ge(sem(f"ln{layer - 1}_ready"), TILES - 1 + k)
                tile = HALF_ORDER[k] if layer == 1 else k
                dst = xn1[:, tile, :] if layer == 1 else xn[:, k % 2, :]
                dve.tensor_scalar(dst, x_sb[:, tile, :], mv[:, layer, k, 0:1], rstd[:, layer, k:k + 1],
                                  ALU.subtract, ALU.mult).then_inc(sem(f"xn{layer}"), 1)

            for k in range(TILES + 2):
                if k < TILES:
                    if k % 2 == 0:
                        loaded(dve, f"x{k}")
                    stat(0, k, x_sb[:, k, :])
                if k >= 2:
                    norm(0, k - 2)

            loaded(dve, "decay")
            dve.wait_ge(sem("a_set"), 1)
            for h in range(RET_HEADS):
                src = filled(dve, "rs", h)[:, 0:3 * P]
                taken(dve.tensor_tensor(out=aneg[:, h, :], in0=src, in1=decay[:, h, :], op=ALU.mult), "rs")
                dve.wait_ge(sem("rs_taken"), h + 1)
                for n, (o, w, d) in enumerate(((0, 2 * P, 0), (2 * P, P, 3 * P))):
                    dve.scalar_tensor_tensor(out=amat[:, h, d:d + w], in0=aneg[:, h, o:o + w], scalar=-1.0,
                                             in1=aneg[:, h, o:o + w], op0=ALU.mult, op1=ALU.max)\
                       .then_inc(sem("a_abs"), 1)
                    dve.wait_ge(sem("a_abs"), 2 * h + n + 1)
                    dve.tensor_scalar(amat[:, h, d:d + w], amat[:, h, d:d + w], 1.0, None, ALU.max)\
                       .then_inc(sem("a_made"), 1)

            def residual(stage, k, g):
                tile = HALF_ORDER[k] if stage == "res0" else k
                dve.scalar_tensor_tensor(out=x_sb[:, tile, :], in0=filled(dve, stage, k)[:, 0:DIM], scalar=tg[:, g:g + 1],
                                         in1=x_sb[:, tile, :], op0=ALU.mult, op1=ALU.add)\
                   .then_inc(sem(stage + "_taken"), 1)

            loaded(dve, "sel", 3)
            loaded(dve, "small")
            dve.tensor_scalar(padrow[:, :], mask_row, 0.0, MASKED, ALU.is_equal, ALU.mult)\
               .then_inc(sem("padrow_made"), 1)
            dve.tensor_scalar(padcol[:, :], mask_col[:, :], 0.0, DEAD, ALU.is_equal, ALU.mult)\
               .then_inc(sem("padcol_made"), 1)

            def gn_center(k):
                dve.wait_ge(sem("mv4"), k + 1)
                dve.scalar_tensor_tensor(out=o_sb[:, HALF_ORDER[k], :], in0=o_sb[:, HALF_ORDER[k], :], scalar=mv[:, 4, k, 0:1], in1=gamma[:, :],
                                         op0=ALU.subtract, op1=ALU.mult).then_inc(sem("gn_z"), 1)

            def gn_scale(k):
                dve.wait_ge(sem("rstd4"), k + 1)
                dve.wait_ge(sem("gn_z"), k + 1)
                dve.scalar_tensor_tensor(out=o_sb[:, HALF_ORDER[k], :], in0=o_sb[:, HALF_ORDER[k], :], scalar=rstd[:, 4, k:k + 1], in1=beta[:, :],
                                         op0=ALU.mult, op1=ALU.add).then_inc(sem("gn_y"), 1)

            loaded(dve, "gamma", 2)
            dve.wait_ge(sem("tanh"), 1)
            dve.wait_ge(sem("ro_taken"), 2)
            for k in range(2):
                stat(4, k, o_sb[:, HALF_ORDER[k], :])
            for k in range(2):
                gn_center(k)
            gn_scale(0)
            for k in range(TILES + 2):
                if k < TILES:
                    dve.wait_ge(sem("gn_y"), k + 1)
                    src = filled(dve, "rg", k)[:, 0:DIM]
                    if k >= 2:
                        dve.wait_ge(sem("wyT_ready"), k - 1)
                    taken(dve.scalar_tensor_tensor(out=att[:, k % 2, :], in0=src, scalar=0.0, in1=o_sb[:, HALF_ORDER[k], :],
                                                   op0=ALU.max, op1=ALU.mult), "rg")
                if k + 2 == TILES // 2:
                    dve.wait_ge(sem("ro_taken"), 4)
                if k + 2 < TILES:
                    stat(4, k + 2, o_sb[:, HALF_ORDER[k + 2], :])
                    gn_center(k + 2)
                if k + 1 < TILES:
                    gn_scale(k + 1)
                if k >= 2:
                    norm(1, k - 2)
                if 1 <= k <= TILES:
                    residual("res0", k - 1, 0)
                    dve.wait_ge(sem("res0_taken"), k)
                    stat(1, k - 1, x_sb[:, HALF_ORDER[k - 1], :])

            steps = [0]

            def step(ins):
                steps[0] += 1
                ins.then_inc(sem("routing"), 1)
                dve.wait_ge(sem("routing"), steps[0])

            def each(v, n, axis=2):
                shape = [P, v.shape[1], n] if axis == 2 else [P, n, v.shape[1]]
                return v.unsqueeze(axis).to_broadcast(shape)

            src = filled(dve, "log", 0)[:, 0:TILES * EXPERTS].rearrange("p (k e) -> p k e", e=EXPERTS)
            taken(dve.tensor_copy(logit[:, :, :], src), "log")
            dve.wait_ge(sem("log_taken"), 1)
            step(dve.reduce_max(r_s[:, 0, :], logit[:, :, :], AX))
            step(dve.tensor_tensor(out=r_a[:, :, :], in0=logit[:, :, :], in1=each(r_s[:, 0, :], EXPERTS), op=ALU.is_equal))
            step(dve.tensor_tensor(out=r_b[:, :, :], in0=r_a[:, :, :], in1=each(small_c[:, 8:16], TILES, 1), op=ALU.mult))
            step(dve.reduce_max(r_s[:, 1, :], r_b[:, :, :], AX))
            dve.tensor_tensor(out=onehot16[:, :, :], in0=r_b[:, :, :], in1=each(r_s[:, 1, :], EXPERTS), op=ALU.is_equal)\
               .then_inc(sem("onehot_made"), 1)
            step(dve.tensor_tensor(out=onehot[:, :, :], in0=r_b[:, :, :], in1=each(r_s[:, 1, :], EXPERTS), op=ALU.is_equal))
            step(dve.scalar_tensor_tensor(out=r_a[:, :, :], in0=onehot[:, :, :], scalar=DEAD,
                                          in1=logit[:, :, :], op0=ALU.mult, op1=ALU.add))
            step(dve.reduce_max(r_s[:, 1, :], r_a[:, :, :], AX))
            dve.tensor_tensor(out=r_s[:, 2, :], in0=r_s[:, 1, :], in1=r_s[:, 0, :], op=ALU.subtract)\
               .then_inc(sem("vdiff"), 1)
            rank = filled(dve, "rank", 0)[:, 0:(TILES + 1) * EXPERTS].rearrange("p (k e) -> p k e", e=EXPERTS)
            step(dve.tensor_copy(r_s[:, 6, :], rank[:, TILES, :]))
            step(dve.tensor_tensor(out=r_b[:, :, :], in0=each(r_s[:, 6, :], TILES), in1=each(small_c[:, 16:24], EXPERTS, 1),
                                   op=ALU.is_gt))
            step(dve.reduce_sum(r_s[:, 7, :], r_b[:, :, :], AX))
            step(dve.tensor_tensor(out=r_a[:, :, :], in0=each(r_s[:, 7, :], EXPERTS, 1),
                                   in1=small_c[:, 24:88].rearrange("p (e f) -> p e f", e=EXPERTS), op=ALU.mult))
            step(dve.reduce_sum(r_s[:, 8, :], r_a[:, :, :], AX))
            taken(dve.tensor_tensor(out=r_b[:, :, :], in0=rank[:, 0:TILES, :], in1=each(r_s[:, 8, :], TILES, 1),
                                    op=ALU.add), "rank")
            dve.wait_ge(sem("rank_taken"), 1)
            step(dve.tensor_tensor(out=r_a[:, :, :], in0=r_b[:, :, :], in1=onehot[:, :, :], op=ALU.mult))
            step(dve.reduce_sum(r_s[:, 9, :], r_a[:, :, :], AX))
            dve.tensor_copy(place[:, :], r_s[:, 9, :]).then_inc(sem("placed"), 1)
            step(dve.scalar_tensor_tensor(out=r_s[:, 10, :], in0=r_s[:, 7, :], scalar=float(P), in1=r_s[:, 8, :],
                                          op0=ALU.mult, op1=ALU.add))
            step(dve.tensor_tensor(out=r_slot[:, :, :], in0=each(r_s[:, 10, :], SLOTS, 1),
                                   in1=each(small_c[:, 88:88 + SLOTS], EXPERTS), op=ALU.is_le))
            step(dve.reduce_sum(slot_f[:, :], r_slot[:, :, :], AX))
            dve.tensor_scalar(slot_expert[:, :], slot_f[:, :], float(EXPERTS - 1), None, ALU.min)\
               .then_inc(sem("slots_made"), 1)
            dve.wait_ge(sem("vexp"), 1)
            step(dve.tensor_scalar(r_s[:, 4, :], r_s[:, 3, :], 1.0, None, ALU.add))
            step(dve.reciprocal(r_s[:, 5, :], r_s[:, 4, :]))
            step(dve.tensor_scalar(r_s[:, 11, :], r_s[:, 5, :], tg[:, 2:3], None, ALU.mult))

            def key_low(b):
                s = b % 2
                dve.wait_ge(sem("k_high"), b + 1)
                src = filled(dve, "kp", b)[64:128, 0:SEQ]
                taken(dve.tensor_tensor(out=khl[64:128, s, :], in0=src, in1=khl[64:128, s, :].bitcast(F32),
                                        op=ALU.subtract), "kp")

            def spread_keys(b):
                s = b % 2
                if b < 2:
                    dve.wait_ge(sem("blocks_clear"), HALVES * (b + 1))
                src = filled(dve, "ks1", b)
                for j in range(QUADS):
                    rows = slice(32 * j, 32 * j + 32)
                    ins = dve.tensor_scalar(kblk[s][1][rows, j, :], src[rows, 0:SEQ], small_c[rows, 1:2], None, ALU.add)
                taken(ins, "ks1")

            key_low(0)
            spread_keys(0)

            def slot_product(i):
                src = filled(dve, "sg", i)[:, EXPERT_I:2 * EXPERT_I]
                dve.wait_ge(sem("silu_made"), i + 1)
                if i >= 2:
                    dve.wait_ge(sem("sa_t_ready"), i - 1)
                taken(dve.tensor_tensor(out=sact[:, i % 2, :], in0=src, in1=silu[:, i % 2, 0:EXPERT_I], op=ALU.mult), "sg")

            slot_product(0)
            for i in range(SLOTS + 1):
                if i + 1 < SLOTS:
                    slot_product(i + 1)
                if i >= 1:
                    taken(dve.tensor_copy(sorted_y[:, i - 1, :], filled(dve, "sy", i - 1)[:, 0:DIM]), "sy")

            def expert_residual(k):
                dve.wait_ge(sem(f"y_back{k // 2}"), 32)
                dve.scalar_tensor_tensor(out=x_sb[:, k, :], in0=own_y[:, k, :], scalar=r_s[:, 11, k:k + 1],
                                         in1=x_sb[:, k, :], op0=ALU.mult, op1=ALU.add).then_inc(sem("x2"), 1)
                dve.wait_ge(sem("x2"), k + 1)
                stat(2, k, x_sb[:, k, :])

            def low_parts(b):
                s = b % 2
                dve.wait_ge(sem("q_high"), b + 1)
                src = filled(dve, "qp", b).rearrange("p (q n) -> p q n", q=HALVES)
                if b >= 2:
                    dve.wait_ge(sem("qs_ready"), 4 * b - 4)
                taken(dve.tensor_tensor(out=qlo[:, s, :, :], in0=src, in1=qhi[:, s, :, :].bitcast(F32),
                                        op=ALU.subtract), "qp")

            def row_maxima(b, n):
                q, hg, nt, quads = score_fill(n)
                src = filled(dve, "sa", 24 * b + n).rearrange("p (j m) -> p j m", m=(nt + 1) * P)
                taken(dve.reduce_max(mx[:, b % 2, nt, quads, q, hg], src, AX), "sa")

            def negate(b):
                s = b % 2
                dve.wait_ge(sem("sa_taken"), 24 * b + 24)
                if b >= 2:
                    dve.wait_ge(sem("nmT_ready"), 2 * (b - 1))
                for nt in range(2):
                    m = mx[:, s, nt, :, :, :].rearrange("p j q h -> p (j q h)")
                    dve.tensor_scalar(nmx[:, s, nt, 0:HEADS], m, -1.0, None, ALU.mult).then_inc(sem("nm_high"), 1)
                    dve.wait_ge(sem("nm_high"), 2 * b + nt + 1)
                    dve.scalar_tensor_tensor(out=nmx[:, s, nt, HEADS:2 * HEADS], in0=m, scalar=-1.0,
                                             in1=nmx[:, s, nt, 0:HEADS].bitcast(F32), op0=ALU.mult,
                                             op1=ALU.subtract).then_inc(sem("nm_made"), 1)

            def finish(b, n):
                nt, c = divmod(n, 6)
                i = 2 * b + nt
                if c == 0 and i >= 2:
                    dve.wait_ge(sem("atT_ready"), i - 1)
                if c < PER_GROUP:
                    o = att[:, i % 2, :].rearrange("p (q j h d) -> p h q j d", q=HALVES, j=QUADS, h=PER_GROUP)
                    f = 4 * i + c
                    src = filled(dve, "avT", f)[:, 0:2 * P].rearrange("p (q j r) -> p q j r", q=HALVES, j=QUADS)
                    dve.reciprocal(rden[:, f % 2, :, :], src[:, :, :, HD]).then_inc(sem("rden_made"), 1)
                    dve.wait_ge(sem("rden_made"), f + 1)
                    taken(dve.tensor_tensor(out=o[:, c, :, :, :], in0=src[:, :, :, 0:HD],
                                            in1=rden[:, f % 2, :, :].unsqueeze(3).to_broadcast([P, HALVES, QUADS, HD]),
                                            op=ALU.mult), "avT")
                elif c > PER_GROUP:
                    dve.wait_ge(sem("bias_added"), i + 1)
                    residual("res2", i, 1)
                    dve.wait_ge(sem("res2_taken"), i + 1)
                    stat(3, i, x_sb[:, i, :])

            loaded(dve, "bo")
            dve.tensor_scalar(bo_t[:, :], bo[:, :], tg[:, 1:2], None, ALU.mult).then_inc(sem("bo_made"), 1)

            def queries(b, n):
                if n in (QUERIES_AT - 2, QUERIES_AT):
                    norm(2, 2 * b + (n - QUERIES_AT + 2) // 2)
                elif n == QUERIES_AT + 6:
                    low_parts(b)

            key_low(1)
            spread_keys(1)
            expert_residual(0)
            expert_residual(1)
            queries(0, QUERIES_AT - 2)
            queries(0, QUERIES_AT)
            expert_residual(2)
            expert_residual(3)
            queries(0, QUERIES_AT + 6)
            for k in range(4, TILES):
                expert_residual(k)
            for n in range(24):
                row_maxima(0, n)
                queries(1, n)
            negate(0)
            for b in range(BATCH):
                if b + 1 < BATCH:
                    for n in range(LEAD):
                        row_maxima(b + 1, n)
                for n in range(24):
                    if b + 1 < BATCH and n + LEAD < 24:
                        row_maxima(b + 1, n + LEAD)
                        if n + LEAD == 23:
                            negate(b + 1)
                    if b >= 1 and n % 2 == 1:
                        finish(b - 1, n // 2)
                    if b + 2 < BATCH:
                        queries(b + 2, n)
                    if b == BATCH - 1 and n + 2 in NORM_STEPS:
                        norm(3, NORM_STEPS.index(n + 2))
                if b + 2 < BATCH:
                    key_low(b + 2)
                    spread_keys(b + 2)

            def sparsify(g, step):
                u, blk = divmod(g, FFN_BLOCKS)
                m = absh[g % 2]
                if step == 0:
                    dve.wait_ge(sem("abs_made"), 4 * g + 4)
                    if g >= 1:
                        dve.wait_ge(sem("hs_made"), 4 * g)
                    dve.tensor_tensor(out=cmp1[:, :, :], in0=m[:, 0:3, :], in1=m[:, 1:4, :], op=ALU.is_ge)\
                       .then_inc(sem("compared"), 1)
                    dve.tensor_tensor(out=cmp2[:, :, :], in0=m[:, 0:2, :], in1=m[:, 2:4, :], op=ALU.is_ge)\
                       .then_inc(sem("compared"), 1)
                    dve.tensor_tensor(out=cmp3[:, :], in0=m[:, 0, :], in1=m[:, 3, :], op=ALU.is_ge)\
                       .then_inc(sem("compared"), 1)
                elif step == 1:
                    dve.wait_ge(sem("compared"), 3 * g + 3)
                    dve.tensor_tensor(out=wins[:, 0:2, :], in0=cmp1[:, 0:2, :], in1=cmp2[:, :, :], op=ALU.add)\
                       .then_inc(sem("wins"), 1)
                    dve.tensor_tensor(out=wins[:, 2, :], in0=cmp1[:, 2, :], in1=cmp2[:, 0, :], op=ALU.subtract)\
                       .then_inc(sem("wins"), 1)
                    dve.tensor_tensor(out=wins[:, 3, :], in0=cmp1[:, 2, :], in1=cmp2[:, 1, :], op=ALU.add)\
                       .then_inc(sem("wins"), 1)
                    dve.wait_ge(sem("wins"), 7 * g + 3)
                    dve.tensor_tensor(out=wins[:, 0, :], in0=wins[:, 0, :], in1=cmp3[:, :], op=ALU.add)\
                       .then_inc(sem("wins"), 1)
                    dve.tensor_tensor(out=wins[:, 1, :], in0=wins[:, 1, :], in1=cmp1[:, 0, :], op=ALU.subtract)\
                       .then_inc(sem("wins"), 1)
                    dve.tensor_tensor(out=wins[:, 2, :], in0=wins[:, 2, :], in1=cmp1[:, 1, :], op=ALU.subtract)\
                       .then_inc(sem("wins"), 1)
                    dve.tensor_tensor(out=wins[:, 3, :], in0=wins[:, 3, :], in1=cmp3[:, :], op=ALU.add)\
                       .then_inc(sem("wins"), 1)
                else:
                    if step == 2:
                        dve.wait_ge(sem("wins"), 7 * g + 7)
                    for j in (2 * step - 4, 2 * step - 3):
                        op, least = ((ALU.is_ge, 2.0), (ALU.is_ge, 1.0), (ALU.is_ge, 0.0), (ALU.is_le, 1.0))[j]
                        h = hs[u][:, 4 * blk + j, :]
                        dve.scalar_tensor_tensor(out=h, in0=wins[:, j, :], scalar=least, in1=h,
                                                 op0=op, op1=ALU.mult).then_inc(sem("hs_made"), 1)

            for g in range(FFN_BLOCKS * UNITS):
                for j in range(4):
                    i = 4 * g + j
                    u, blk = divmod(g, FFN_BLOCKS)
                    src = filled(dve, "fu", i)
                    dve.wait_ge(sem("fg_taken"), i + 1)
                    taken(dve.tensor_tensor(out=hs[u][:, 4 * blk + j, :], in0=src, in1=silu[:, i % 2, :], op=ALU.mult), "fu")
                    for c in range(2 * i, min(2 * i + 2, 12)):
                        finish(BATCH - 1, c)
                    if i + 1 in LATE_NORM_STEPS:
                        norm(3, UNIT_TILES + LATE_NORM_STEPS.index(i + 1))
                    if g >= 1:
                        sparsify(g - 1, j)
            for step in range(4):
                sparsify(FFN_BLOCKS * UNITS - 1, step)
                residual("res3", step, 3)
            for k in range(UNIT_TILES, TILES):
                residual("res3", k, 3)


def shape_constants():
    f = np.float32
    gam = (f(1.0) - f(2.0) ** (f(-5.0) - np.arange(RET_HEADS, dtype=f))).astype(f)
    idx = np.arange(SEQ, dtype=f)
    expo = idx[None, :] - idx[:, None]
    low = expo <= 0
    D = np.where(low[None], gam[:, None, None] ** np.where(low, expo, 0)[None], 0).astype(f)
    Dn = D / np.sqrt(D.sum(axis=-1, dtype=f))[:, None, :] / np.sqrt(f(RET_HD))
    G = Dn.transpose(0, 2, 1)
    decay = np.concatenate([G[:, :P, :], G[:, P:, P:]], axis=2).transpose(1, 0, 2)
    sel = np.zeros((P, 11, P), f)
    for j in range(QUADS):
        for d in range(HD):
            for hg in range(PER_GROUP):
                row = j * 32 + hg * HD + d
                sel[row, hg, [32 * j + d, 32 * j + 8 + d]] = 1
                sel[row, 4 + hg, 32 * j + 16 + d] = 1
            for q in range(HALVES):
                row = (QUADS * q + j) * HD + d
                sel[row, 8 + q, [32 * j + d, 32 * j + 16 + d]] = 1
                sel[64 + row, 8 + q, 32 * j + 8 + d] = 1
        sel[0, 10, 32 * j + 26] = 1
    small = np.zeros((P, 103), f)
    small[26::32, 0] = 1
    small[24::32, 1] = 1
    small[25::32, 1] = 1
    small[:, 8:16] = np.arange(EXPERTS, 0, -1)
    small[:, 16:24] = P * np.arange(TILES)
    small[:, 24:88] = (P * np.tri(EXPERTS, k=-1)).reshape(-1)
    small[:, 88:88 + SLOTS] = P * np.arange(SLOTS)
    n = np.arange(P)
    later = np.where(n[None, :] > n[:, None], f(MASKED), f(0))
    caus = np.tile(later, (1, 4)).astype(f)
    tri = np.stack([later != 0, np.ones((P, P))], 1).astype(f)
    return {"decay": decay, "sel": sel.reshape(P, 11 * P), "tri": tri, "small": small, "caus": caus,
            "ident": np.eye(P, dtype=f), "identb": np.eye(P, dtype=f)}


def kernel(**inputs):
    import numpy as _np
    import concourse.bacc as _bacc
    from concourse import mybir as _mybir
    from concourse.bass_utils import run_bass_kernel_spmd as _run

    i = {k: _np.asarray(v) for k, v in inputs.items()}

    def by_rows(w):
        return w.reshape(w.shape[0] // P, P, w.shape[1]).transpose(1, 0, 2)

    def everywhere(v):
        return _np.broadcast_to(v[None, :], (P, v.shape[0]))

    wk = i["L1_xattn_w_k"].T
    ffn_cols = (lambda w: by_rows(w.reshape(DIM, FFN_I // 4, 4).transpose(0, 2, 1).reshape(DIM, FFN_I)))
    arrays = {
        "x": i["x"].reshape(TILES, P, DIM),
        "ctxT": by_rows(i["ctx_2048"].reshape(TOKENS, DIM).T),
        "mask_row": i["mask_BxS2_if1"].reshape(1, TOKENS),
        "mask_col": i["mask_BxS2_if1"].reshape(TILES, P).T,
        "g_x": everywhere(i["g_xattn"]),
        "g_f": everywhere(i["g_ffn"]),
        "wh": i["L0_xattn_Wh"].transpose(1, 0, 2),
        "wg": by_rows(i["L0_xattn_wg_w"]),
        "wo0": by_rows(i["L0_xattn_wo_w"]),
        "gamma": everywhere(i["L0_xattn_gn_gamma"]),
        "beta": everywhere(i["L0_xattn_gn_beta"]),
        "router": by_rows(i["L0_ffn_router_w"].T),
        "e_gu": by_rows(_np.concatenate([i["L0_ffn_gate_w"], i["L0_ffn_up_w"]], axis=1).reshape(-1, DIM).T)
        .reshape(P, KT, EXPERTS, 2 * EXPERT_I),
        "e_down": i["L0_ffn_down_w"].transpose(2, 0, 1)[:P],
        "e_down2": i["L0_ffn_down_w"].transpose(2, 0, 1)[P:],
        "wq": by_rows(i["L1_xattn_w_q"].T),
        "wk": by_rows(_np.concatenate([wk, wk], axis=1)),
        "wv": by_rows(i["L1_xattn_w_v"].T),
        "wo1": by_rows(i["L1_xattn_w_o"].T),
        "bo": everywhere(i["L1_xattn_b_o"]),
        "f_gate": ffn_cols(i["L1_ffn_w_gate"]),
        "f_up": ffn_cols(i["L1_ffn_w_up"]),
        "f_down": by_rows(i["L1_ffn_w_down"].reshape(FFN_BLOCKS, P, 4, DIM).transpose(0, 2, 1, 3).reshape(FFN_I, DIM)),
    }
    arrays.update(shape_constants())
    for n in ("caus", "identb", "tri"):
        arrays[n] = arrays[n].astype(_mybir.dt.np(_mybir.dt.bfloat16))
    arrays = {f"in_{n}_dram": _np.ascontiguousarray(v) for n, v in arrays.items()}

    nc = _bacc.Bacc("TRN2", target_bir_lowering=False, num_devices=1)
    args = {n[3:-5]: nc.dram_tensor(n, v.shape, _mybir.dt.from_np(v.dtype), kind="ExternalInput").ap()
            for n, v in arrays.items()}
    out = nc.dram_tensor("out_0_dram", (TILES, P, DIM), _mybir.dt.float32, kind="ExternalOutput").ap()
    build_program(nc, args, out)
    r = _run(nc, [arrays], core_ids=[0])
    return r.results[0]["out_0_dram"].reshape(BATCH, SEQ, DIM)
```
